# Optimizing a Trainium2 kernel written in Bass

```python
import numpy as np
import jax
import jax.numpy as jnp

def _softmax(x, axis=-1):
    return jax.nn.softmax(x, axis=axis)

def _gelu(x):
    return jax.nn.gelu(x, approximate=True)

def _silu(x):
    return jax.nn.silu(x)

def _sigmoid(x):
    return jax.nn.sigmoid(x)

def _layernorm(x, axis=-1, eps=1e-05):
    m = jnp.mean(x, axis=axis, keepdims=True)
    v = jnp.var(x, axis=axis, keepdims=True)
    return (x - m) / jnp.sqrt(v + eps)

def _scatter_add(tgt, idx, src, axis=0):
    return tgt.at[idx].add(src)

def _segment_sum(src, seg, n):
    return jax.ops.segment_sum(src, seg, n)
kernel_name = 'mk_xattn_ffn_d2_seqx_r4_c3095e'

def setup_inputs(seed: int=0):
    np.random.seed(seed)
    _w = jnp.asarray

    def _rec_inputs():
        import jax
        import jax.numpy as jnp
        _rk = jax.random.key(seed)
        x = -0.0002928 + 1 * jax.random.normal(jax.random.fold_in(_rk, 1), (2, 1024, 256), jnp.float32)
        _lenS = 1024 - jax.random.randint(jax.random.fold_in(_rk, 7), (2,), 0, max(1, 1024 // 4) + 1, jnp.int32)
        _lenS2 = 77 - jax.random.randint(jax.random.fold_in(_rk, 8), (2,), 0, max(1, 77 // 4) + 1, jnp.int32)
        _ctx_1024P = jax.random.normal(jax.random.fold_in(_rk, 11), (2, 16, 256), jnp.float32)
        _ctx_1024c = jax.random.dirichlet(jax.random.fold_in(_rk, 511), 0.3 * jnp.ones((16,), jnp.float32), (2, 77))
        _ctx_1024t = jnp.einsum('bsk,bkd->bsd', _ctx_1024c, _ctx_1024P)
        _ctx_1024t = _ctx_1024t * jax.lax.rsqrt(jnp.mean(jnp.square(_ctx_1024t)) + 1e-12) * 0.953939
        ctx_1024 = -1.39393e-06 + 0.999914 * (_ctx_1024t + 0.3 * jax.random.normal(jax.random.fold_in(_rk, 611), (2, 77, 256), jnp.float32))
        _validS = jnp.arange(1024)[None, :] < _lenS[:, None]
        _validS2 = jnp.arange(77)[None, :] < _lenS2[:, None]
        _causal = jnp.tril(jnp.ones((1024, 1024), dtype=bool))
        mask_Bx1x1xS2_ik0 = jnp.where(jnp.broadcast_to(_validS2[:, None, None, :], (2, 1, 1, 77)), 0, 1).astype(jnp.int32)
        mask_1x1xSxS2_ik0 = jnp.where(jnp.broadcast_to(_validS2[0:1, None, None, :], (1, 1, 1024, 77)), 0, 1).astype(jnp.int32)
        return (x, ctx_1024, mask_Bx1x1xS2_ik0, mask_1x1xSxS2_ik0)
    x, ctx_1024, mask_Bx1x1xS2_ik0, mask_1x1xSxS2_ik0 = _rec_inputs()

    def _L0_xattn_setup():
        import jax, jax.numpy as jnp
        import numpy as np
        D_MODEL = 256
        N_HEADS = 16
        HEAD = D_MODEL // N_HEADS
        D_FF = 1024
        LN_EPS = 1e-05

        def _layernorm(x, g, b):
            mu = jnp.mean(x, axis=-1, keepdims=True)
            var = jnp.mean(jnp.square(x - mu), axis=-1, keepdims=True)
            return (x - mu) * jax.lax.rsqrt(var + LN_EPS) * g + b

        def _mha(q_in, k_in, v_in, Wq, Wk, Wv, bv, causal):
            q = jnp.einsum('bsd,hde->bhse', q_in, Wq)
            k = jnp.einsum('btd,hde->bhte', k_in, Wk)
            v = jnp.einsum('btd,hde->bhte', v_in, Wv) + bv[None, :, None, :]
            scale = HEAD ** (-0.5)
            scores = jnp.einsum('bhse,bhte->bhst', q, k) * scale
            if causal:
                S, T = (scores.shape[-2], scores.shape[-1])
                mask = jnp.tril(jnp.ones((S, T), dtype=bool))
                scores = jnp.where(mask, scores, -jnp.inf)
            p = jax.nn.softmax(scores, axis=-1)
            o = jnp.einsum('bhst,bhte->bhse', p, v)
            B, H, S, E = o.shape
            return o.transpose(0, 2, 1, 3).reshape(B, S, H * E)
        key = jax.random.key(seed)
        ks = jax.random.split(key, 20)
        B, S, T = (2, 512, 512)
        sd = D_MODEL ** (-0.5)
        inp = {'input_tensor': jax.random.normal(ks[0], (B, S, D_MODEL), jnp.float32), 'encoder_output': jax.random.normal(ks[1], (B, T, D_MODEL), jnp.float32), 'Wq1': jax.random.normal(ks[2], (N_HEADS, D_MODEL, HEAD), jnp.float32) * sd, 'Wk1': jax.random.normal(ks[3], (N_HEADS, D_MODEL, HEAD), jnp.float32) * sd, 'Wv1': jax.random.normal(ks[4], (N_HEADS, D_MODEL, HEAD), jnp.float32) * sd, 'bv1': jnp.zeros((N_HEADS, HEAD), jnp.float32), 'Wq2': jax.random.normal(ks[5], (N_HEADS, D_MODEL, HEAD), jnp.float32) * sd, 'Wk2': jax.random.normal(ks[6], (N_HEADS, D_MODEL, HEAD), jnp.float32) * sd, 'Wv2': jax.random.normal(ks[7], (N_HEADS, D_MODEL, HEAD), jnp.float32) * sd, 'bv2': jnp.zeros((N_HEADS, HEAD), jnp.float32), 'g1': jnp.ones((D_MODEL,), jnp.float32), 'be1': jnp.zeros((D_MODEL,), jnp.float32), 'g2': jnp.ones((D_MODEL,), jnp.float32), 'be2': jnp.zeros((D_MODEL,), jnp.float32), 'g3': jnp.ones((D_MODEL,), jnp.float32), 'be3': jnp.zeros((D_MODEL,), jnp.float32), 'Wf1': jax.random.normal(ks[8], (D_MODEL, D_FF), jnp.float32) * sd, 'bf1': jnp.zeros((D_FF,), jnp.float32), 'Wf2': jax.random.normal(ks[9], (D_FF, D_MODEL), jnp.float32) * D_FF ** (-0.5), 'bf2': jnp.zeros((D_MODEL,), jnp.float32)}
        return inp
    _L0_xattn_all = _L0_xattn_setup()
    _L0_xattn_in = {k: v for k, v in _L0_xattn_all.items() if k in ('Wq1', 'Wk1', 'Wv1', 'bv1', 'Wq2', 'Wk2', 'Wv2', 'bv2', 'g1', 'be1', 'g2', 'be2', 'g3', 'be3', 'Wf1', 'bf1', 'Wf2', 'bf2')}
    del _L0_xattn_all

    def _L0_ffn_setup():
        import jax, jax.numpy as jnp
        import numpy as np
        ALPHA = 1.0
        key = jax.random.key(seed)
        ks = jax.random.split(key, 7)
        B, S, IN, OUT = (8, 2048, 256, 256)
        RANK, DDIM, UDIM = (4, 100, 50)
        return {'hidden_states': jax.random.normal(ks[0], (B, S, IN), dtype=jnp.float32), 'W': jax.random.normal(ks[1], (OUT, IN), dtype=jnp.float32) * 0.02, 'b': jax.random.normal(ks[2], (OUT,), dtype=jnp.float32) * 0.02, 'lora_down': jax.random.normal(ks[3], (RANK, DDIM), dtype=jnp.float32) * 0.1, 'lora_up': jax.random.normal(ks[4], (UDIM, RANK), dtype=jnp.float32) * 0.1, 'down_aux': jax.random.normal(ks[5], (DDIM, IN), dtype=jnp.float32) * 0.03, 'up_aux': jax.random.normal(ks[6], (OUT, UDIM), dtype=jnp.float32) * 0.03}
    _L0_ffn_all = _L0_ffn_setup()
    _L0_ffn_in = {k: v for k, v in _L0_ffn_all.items() if k in ('W', 'b', 'lora_down', 'lora_up', 'down_aux', 'up_aux')}
    del _L0_ffn_all

    def _L1_xattn_setup():
        import jax, jax.numpy as jnp
        import numpy as np
        E, H = (256, 16)
        N, S, T = (2, 512, 512)
        key = jax.random.key(seed)
        ks = jax.random.split(key, 8)
        scale = 1.0 / np.sqrt(E)
        q = jax.random.normal(ks[0], (N, S, E), dtype=jnp.float32)
        k = jax.random.normal(ks[1], (N, T, E), dtype=jnp.float32)
        v = jax.random.normal(ks[2], (N, T, E), dtype=jnp.float32)
        pad_mask = jax.random.randint(ks[3], (N, 1, 1, T), 0, 2, dtype=jnp.int32)
        subsq_mask = jnp.tril(jnp.ones((S, T), dtype=jnp.int32))[None, None]
        Wq = jax.random.normal(ks[4], (E, E), dtype=jnp.float32) * scale
        Wk = jax.random.normal(ks[5], (E, E), dtype=jnp.float32) * scale
        Wv = jax.random.normal(ks[6], (E, E), dtype=jnp.float32) * scale
        bq = jnp.zeros((E,), dtype=jnp.float32)
        bk = jnp.zeros((E,), dtype=jnp.float32)
        bv = jnp.zeros((E,), dtype=jnp.float32)
        return {'query': q, 'key': k, 'value': v, 'pad_mask': pad_mask, 'subsq_mask': subsq_mask, 'Wq': Wq, 'bq': bq, 'Wk': Wk, 'bk': bk, 'Wv': Wv, 'bv': bv}
    _L1_xattn_all = _L1_xattn_setup()
    _L1_xattn_in = {k: v for k, v in _L1_xattn_all.items() if k in ('Wq', 'bq', 'Wk', 'bk', 'Wv', 'bv')}
    del _L1_xattn_all

    def _L1_ffn_setup():
        import jax, jax.numpy as jnp
        import numpy as np
        B, T, C = (4, 512, 256)
        H = 128
        E_ATT = 8
        E_MOE = 8
        I = 256
        MIN_ATT = 2
        MIN_MOE = 2
        EPS_LN = 1e-05

        def _normalize(x, axis):
            n = jnp.linalg.norm(x, axis=axis, keepdims=True)
            return x / jnp.maximum(n, 1e-12)

        def _layernorm(x, w, b):
            m = jnp.mean(x, axis=-1, keepdims=True)
            v = jnp.mean(jnp.square(x - m), axis=-1, keepdims=True)
            return (x - m) / jnp.sqrt(v + EPS_LN) * w + b

        def _gating(flat_hs, sim, gates, min_experts):
            logits = _normalize(flat_hs, -1) @ _normalize(sim, 0) - jax.nn.sigmoid(gates)
            gated = jax.nn.relu(logits)
            mask = (gated > 0).astype(gated.dtype)
            inactive = jnp.sum(mask, axis=1) == 0
            _, idx = jax.lax.top_k(logits, min_experts)
            onehot = jnp.sum(jax.nn.one_hot(idx, logits.shape[-1], dtype=gated.dtype), axis=1)
            put = inactive[:, None] & (onehot > 0)
            mask = jnp.where(put, 1.0, mask)
            masked = jnp.where(mask > 0, gated, -jnp.inf)
            return jax.nn.softmax(masked, axis=-1)
        key = jax.random.key(seed)
        ks = jax.random.split(key, 12)
        d = {}
        d['x'] = jax.random.normal(ks[0], (B, T, C), dtype=jnp.float32)
        d['ln1_w'] = jnp.ones((C,), jnp.float32)
        d['ln1_b'] = jnp.zeros((C,), jnp.float32)
        d['ln2_w'] = jnp.ones((C,), jnp.float32)
        d['ln2_b'] = jnp.zeros((C,), jnp.float32)
        d['smha_sim'] = jax.random.normal(ks[1], (C, E_ATT), dtype=jnp.float32)
        d['smha_gates'] = jnp.zeros((E_ATT,), jnp.float32)
        sq = 1.0 / np.sqrt(C + H)
        d['q_proj'] = jax.random.normal(ks[2], (E_ATT, C, H), dtype=jnp.float32) * sq
        d['k_proj'] = jax.random.normal(ks[3], (E_ATT, C, H), dtype=jnp.float32) * sq
        d['v_proj'] = jax.random.normal(ks[4], (E_ATT, C, H), dtype=jnp.float32) * sq
        d['o_proj'] = jax.random.normal(ks[5], (E_ATT, H, C), dtype=jnp.float32) * sq
        d['moe_sim'] = jax.random.normal(ks[6], (C, E_MOE), dtype=jnp.float32)
        d['moe_gates'] = jnp.zeros((E_MOE,), jnp.float32)
        d['w1'] = jax.random.normal(ks[7], (E_MOE, C, I), dtype=jnp.float32) * (1.0 / np.sqrt(C))
        d['w2'] = jax.random.normal(ks[8], (E_MOE, I, C), dtype=jnp.float32) * (1.0 / np.sqrt(I))
        return d
    _L1_ffn_all = _L1_ffn_setup()
    _L1_ffn_in = {k: v for k, v in _L1_ffn_all.items() if k in ('ln1_w', 'ln1_b', 'ln2_w', 'ln2_b', 'smha_sim', 'smha_gates', 'q_proj', 'k_proj', 'v_proj', 'o_proj', 'moe_sim', 'moe_gates', 'w1', 'w2')}
    del _L1_ffn_all
    return {'x': x, 'ctx_1024': ctx_1024, 'mask_Bx1x1xS2_ik0': mask_Bx1x1xS2_ik0, 'mask_1x1xSxS2_ik0': mask_1x1xSxS2_ik0, 'L0_xattn_Wq1': _L0_xattn_in['Wq1'], 'L0_xattn_Wk1': _L0_xattn_in['Wk1'], 'L0_xattn_Wv1': _L0_xattn_in['Wv1'], 'L0_xattn_bv1': _L0_xattn_in['bv1'], 'L0_xattn_Wq2': _L0_xattn_in['Wq2'], 'L0_xattn_Wk2': _L0_xattn_in['Wk2'], 'L0_xattn_Wv2': _L0_xattn_in['Wv2'], 'L0_xattn_bv2': _L0_xattn_in['bv2'], 'L0_xattn_g1': _L0_xattn_in['g1'], 'L0_xattn_be1': _L0_xattn_in['be1'], 'L0_xattn_g2': _L0_xattn_in['g2'], 'L0_xattn_be2': _L0_xattn_in['be2'], 'L0_xattn_g3': _L0_xattn_in['g3'], 'L0_xattn_be3': _L0_xattn_in['be3'], 'L0_xattn_Wf1': _L0_xattn_in['Wf1'], 'L0_xattn_bf1': _L0_xattn_in['bf1'], 'L0_xattn_Wf2': _L0_xattn_in['Wf2'], 'L0_xattn_bf2': _L0_xattn_in['bf2'], 'L0_ffn_W': _L0_ffn_in['W'], 'L0_ffn_b': _L0_ffn_in['b'], 'L0_ffn_lora_down': _L0_ffn_in['lora_down'], 'L0_ffn_lora_up': _L0_ffn_in['lora_up'], 'L0_ffn_down_aux': _L0_ffn_in['down_aux'], 'L0_ffn_up_aux': _L0_ffn_in['up_aux'], 'L1_xattn_Wq': _L1_xattn_in['Wq'], 'L1_xattn_bq': _L1_xattn_in['bq'], 'L1_xattn_Wk': _L1_xattn_in['Wk'], 'L1_xattn_bk': _L1_xattn_in['bk'], 'L1_xattn_Wv': _L1_xattn_in['Wv'], 'L1_xattn_bv': _L1_xattn_in['bv'], 'L1_ffn_ln1_w': _L1_ffn_in['ln1_w'], 'L1_ffn_ln1_b': _L1_ffn_in['ln1_b'], 'L1_ffn_ln2_w': _L1_ffn_in['ln2_w'], 'L1_ffn_ln2_b': _L1_ffn_in['ln2_b'], 'L1_ffn_smha_sim': _L1_ffn_in['smha_sim'], 'L1_ffn_smha_gates': _L1_ffn_in['smha_gates'], 'L1_ffn_q_proj': _L1_ffn_in['q_proj'], 'L1_ffn_k_proj': _L1_ffn_in['k_proj'], 'L1_ffn_v_proj': _L1_ffn_in['v_proj'], 'L1_ffn_o_proj': _L1_ffn_in['o_proj'], 'L1_ffn_moe_sim': _L1_ffn_in['moe_sim'], 'L1_ffn_moe_gates': _L1_ffn_in['moe_gates'], 'L1_ffn_w1': _L1_ffn_in['w1'], 'L1_ffn_w2': _L1_ffn_in['w2']}

def reference(x, ctx_1024, mask_Bx1x1xS2_ik0, mask_1x1xSxS2_ik0, L0_xattn_Wq1, L0_xattn_Wk1, L0_xattn_Wv1, L0_xattn_bv1, L0_xattn_Wq2, L0_xattn_Wk2, L0_xattn_Wv2, L0_xattn_bv2, L0_xattn_g1, L0_xattn_be1, L0_xattn_g2, L0_xattn_be2, L0_xattn_g3, L0_xattn_be3, L0_xattn_Wf1, L0_xattn_bf1, L0_xattn_Wf2, L0_xattn_bf2, L0_ffn_W, L0_ffn_b, L0_ffn_lora_down, L0_ffn_lora_up, L0_ffn_down_aux, L0_ffn_up_aux, L1_xattn_Wq, L1_xattn_bq, L1_xattn_Wk, L1_xattn_bk, L1_xattn_Wv, L1_xattn_bv, L1_ffn_ln1_w, L1_ffn_ln1_b, L1_ffn_ln2_w, L1_ffn_ln2_b, L1_ffn_smha_sim, L1_ffn_smha_gates, L1_ffn_q_proj, L1_ffn_k_proj, L1_ffn_v_proj, L1_ffn_o_proj, L1_ffn_moe_sim, L1_ffn_moe_gates, L1_ffn_w1, L1_ffn_w2):
    import jax
    import jax.numpy as jnp

    def _L0_xattn_ref(input_tensor, encoder_output, Wq1, Wk1, Wv1, bv1, Wq2, Wk2, Wv2, bv2, g1, be1, g2, be2, g3, be3, Wf1, bf1, Wf2, bf2):
        import jax, jax.numpy as jnp
        import numpy as np
        D_MODEL = 256
        N_HEADS = 16
        HEAD = D_MODEL // N_HEADS
        D_FF = 1024
        LN_EPS = 1e-05

        def _layernorm(x, g, b):
            mu = jnp.mean(x, axis=-1, keepdims=True)
            var = jnp.mean(jnp.square(x - mu), axis=-1, keepdims=True)
            return (x - mu) * jax.lax.rsqrt(var + LN_EPS) * g + b

        def _mha(q_in, k_in, v_in, Wq, Wk, Wv, bv, causal):
            q = jnp.einsum('bsd,hde->bhse', q_in, Wq)
            k = jnp.einsum('btd,hde->bhte', k_in, Wk)
            v = jnp.einsum('btd,hde->bhte', v_in, Wv) + bv[None, :, None, :]
            scale = HEAD ** (-0.5)
            scores = jnp.einsum('bhse,bhte->bhst', q, k) * scale
            if causal:
                S, T = (scores.shape[-2], scores.shape[-1])
                mask = jnp.tril(jnp.ones((S, T), dtype=bool))
                scores = jnp.where(mask, scores, -jnp.inf)
            p = jax.nn.softmax(scores, axis=-1)
            o = jnp.einsum('bhst,bhte->bhse', p, v)
            B, H, S, E = o.shape
            return o.transpose(0, 2, 1, 3).reshape(B, S, H * E)
        x = input_tensor
        sa = _mha(x, x, x, Wq1, Wk1, Wv1, bv1, causal=True)
        x = _layernorm(sa + input_tensor, g1, be1)
        ca = _mha(x, encoder_output, encoder_output, Wq2, Wk2, Wv2, bv2, causal=False)
        x = _layernorm(x + ca, g2, be2)
        ffn = jax.nn.relu(x @ Wf1 + bf1) @ Wf2 + bf2
        x = _layernorm(x + ffn, g3, be3)
        return x

    def _L0_ffn_ref(hidden_states, W, b, lora_down, lora_up, down_aux, up_aux):
        import jax, jax.numpy as jnp
        import numpy as np
        ALPHA = 1.0
        lilora_weight = up_aux @ (lora_up @ (lora_down @ down_aux))
        base = jnp.einsum('bsi,oi->bso', hidden_states, W) + b
        delta = jnp.einsum('bsi,oi->bso', hidden_states, lilora_weight)
        return base + ALPHA * delta

    def _L1_xattn_ref(query, key, value, pad_mask, subsq_mask, Wq, bq, Wk, bk, Wv, bv):
        import jax, jax.numpy as jnp
        import numpy as np
        E, H = (256, 16)
        N, S, T = (2, 512, 512)
        n, s, e = query.shape
        t = value.shape[1]
        d = e // H
        q = (query @ Wq.T + bq).reshape(n, s, H, d).transpose(0, 2, 1, 3)
        k = (key @ Wk.T + bk).reshape(n, t, H, d).transpose(0, 2, 1, 3)
        v = (value @ Wv.T + bv).reshape(n, t, H, d).transpose(0, 2, 1, 3)
        att = jnp.einsum('bhsd,bhtd->bhst', q, k) / jnp.sqrt(jnp.float32(d))
        att = jnp.where(pad_mask == 0, jnp.float32(-1000000000.0), att)
        att = jnp.where(subsq_mask == 0, jnp.float32(-1000000000.0), att)
        prob = jax.nn.softmax(att, axis=-1)
        out = jnp.einsum('bhst,bhtd->bhsd', prob, v)
        return out.transpose(0, 2, 1, 3).reshape(n, s, e)

    def _L1_ffn_ref(x, ln1_w, ln1_b, ln2_w, ln2_b, smha_sim, smha_gates, q_proj, k_proj, v_proj, o_proj, moe_sim, moe_gates, w1, w2):
        import jax, jax.numpy as jnp
        import numpy as np
        B, T, C = (4, 512, 256)
        H = 128
        E_ATT = 8
        E_MOE = 8
        I = 256
        MIN_ATT = 2
        MIN_MOE = 2
        EPS_LN = 1e-05

        def _normalize(x, axis):
            n = jnp.linalg.norm(x, axis=axis, keepdims=True)
            return x / jnp.maximum(n, 1e-12)

        def _layernorm(x, w, b):
            m = jnp.mean(x, axis=-1, keepdims=True)
            v = jnp.mean(jnp.square(x - m), axis=-1, keepdims=True)
            return (x - m) / jnp.sqrt(v + EPS_LN) * w + b

        def _gating(flat_hs, sim, gates, min_experts):
            logits = _normalize(flat_hs, -1) @ _normalize(sim, 0) - jax.nn.sigmoid(gates)
            gated = jax.nn.relu(logits)
            mask = (gated > 0).astype(gated.dtype)
            inactive = jnp.sum(mask, axis=1) == 0
            _, idx = jax.lax.top_k(logits, min_experts)
            onehot = jnp.sum(jax.nn.one_hot(idx, logits.shape[-1], dtype=gated.dtype), axis=1)
            put = inactive[:, None] & (onehot > 0)
            mask = jnp.where(put, 1.0, mask)
            masked = jnp.where(mask > 0, gated, -jnp.inf)
            return jax.nn.softmax(masked, axis=-1)
        b, t, c = x.shape
        n1 = _layernorm(x, ln1_w, ln1_b)
        rw = _gating(n1.reshape(b * t, c), smha_sim, smha_gates, MIN_ATT).reshape(b, t, -1)
        q = jnp.einsum('btc,ech,bte->bth', n1, q_proj, rw)
        k = jnp.einsum('btc,ech,bte->bth', n1, k_proj, rw)
        v = jnp.einsum('btc,ech,bte->bth', n1, v_proj, rw)
        scale = 1.0 / jnp.sqrt(jnp.asarray(q.shape[-1], q.dtype))
        scores = jnp.einsum('bth,bsh->bts', q, k) * scale
        causal = jnp.tril(jnp.ones((t, t), dtype=bool))
        scores = jnp.where(causal, scores, -jnp.inf)
        attn = jnp.einsum('bts,bsh->bth', jax.nn.softmax(scores, axis=-1), v)
        attn_out = jnp.einsum('bth,ehc,bte->btc', attn, o_proj, rw)
        hs = x + attn_out
        n2 = _layernorm(hs, ln2_w, ln2_b)
        rw2 = _gating(n2.reshape(b * t, c), moe_sim, moe_gates, MIN_MOE).reshape(b, t, -1)
        inter = jax.nn.gelu(jnp.einsum('btc,eci->btei', n2, w1), approximate=False)
        moe_out = jnp.einsum('btei,eic,bte->btc', inter, w2, rw2)
        return hs + moe_out
    x = x + _L0_xattn_ref(_layernorm(x, axis=-1), ctx_1024, L0_xattn_Wq1, L0_xattn_Wk1, L0_xattn_Wv1, L0_xattn_bv1, L0_xattn_Wq2, L0_xattn_Wk2, L0_xattn_Wv2, L0_xattn_bv2, L0_xattn_g1, L0_xattn_be1, L0_xattn_g2, L0_xattn_be2, L0_xattn_g3, L0_xattn_be3, L0_xattn_Wf1, L0_xattn_bf1, L0_xattn_Wf2, L0_xattn_bf2)
    x = x + _L0_ffn_ref(_layernorm(x, axis=-1), L0_ffn_W, L0_ffn_b, L0_ffn_lora_down, L0_ffn_lora_up, L0_ffn_down_aux, L0_ffn_up_aux)
    x = x + _L1_xattn_ref(_layernorm(x, axis=-1), ctx_1024, ctx_1024, mask_Bx1x1xS2_ik0, mask_1x1xSxS2_ik0, L1_xattn_Wq, L1_xattn_bq, L1_xattn_Wk, L1_xattn_bk, L1_xattn_Wv, L1_xattn_bv)
    x = x + _L1_ffn_ref(_layernorm(x, axis=-1), L1_ffn_ln1_w, L1_ffn_ln1_b, L1_ffn_ln2_w, L1_ffn_ln2_b, L1_ffn_smha_sim, L1_ffn_smha_gates, L1_ffn_q_proj, L1_ffn_k_proj, L1_ffn_v_proj, L1_ffn_o_proj, L1_ffn_moe_sim, L1_ffn_moe_gates, L1_ffn_w1, L1_ffn_w2)
    return x

_drawn_inputs = setup_inputs


def setup_inputs(seed=0):
    import zlib

    import numpy as np

    out = dict(_drawn_inputs(seed))
    spreads = {'L0_xattn_bv1': (0.0, 0.1),
     'L0_xattn_bv2': (0.0, 0.1),
     'L0_xattn_g1': (1.0, 0.2),
     'L0_xattn_be1': (0.0, 0.1),
     'L0_xattn_g2': (1.0, 0.2),
     'L0_xattn_be2': (0.0, 0.1),
     'L0_xattn_g3': (1.0, 0.2),
     'L0_xattn_be3': (0.0, 0.1),
     'L0_xattn_bf1': (0.0, 0.1),
     'L0_xattn_bf2': (0.0, 0.1),
     'L1_xattn_bq': (0.0, 0.364),
     'L1_xattn_bk': (0.0, 0.8),
     'L1_xattn_bv': (0.0, 0.1),
     'L1_ffn_ln1_w': (1.0, 0.2),
     'L1_ffn_ln1_b': (0.0, 0.299),
     'L1_ffn_ln2_w': (1.0, 0.2),
     'L1_ffn_ln2_b': (0.0, 0.1),
     'L1_ffn_smha_gates': (0.0, 0.1),
     'L1_ffn_moe_gates': (0.0, 0.1)}
    factors = {'L0_ffn_b': 2.796,
     'L0_ffn_lora_down': 3.317,
     'L0_ffn_lora_up': 3.351,
     'L0_ffn_down_aux': 3.264,
     'L0_ffn_up_aux': 3.265,
     'L1_ffn_q_proj': 4.852,
     'L1_ffn_k_proj': 4.321}
    for name, (base, spread) in spreads.items():
        noise = np.random.default_rng([zlib.crc32(name.encode()), seed]).standard_normal(out[name].shape)
        drawn = base * np.exp(spread * noise) if base else spread * noise
        out[name] = jnp.asarray(drawn.astype(out[name].dtype))
    for name, factor in factors.items():
        out[name] = (out[name] * factor).astype(out[name].dtype)
    return out
```

```python
from contextlib import ExitStack

import concourse.bass as bass
from concourse import mybir

F32 = mybir.dt.float32
BF16 = mybir.dt.bfloat16
I32 = mybir.dt.int32
ALU = mybir.AluOpType
ACT = mybir.ActivationFunctionType
AX = mybir.AxisListType

P = 128
B, S, D, T = 2, 1024, 256, 77
N = B * S
TILES = N // P
TPB = S // P
HEADS, HD = 16, 16
KC = D // P
FF = 1024
FCH = FF // P
EXPERTS = 8
HA = 128
EPS = 1e-5
BIG = -3.0e38
MASKED = -1.0e9
GRP = 4
GROUPS = B * HEADS // GRP
SLOTS = 3
VW = HD + 1
ROWS = 6 * HD
QPART = [0, 1, 2, 0, 1, 0]
KPART = [0, 0, 0, 1, 1, 2]
LNS = ["in", "g1", "g2", "g3", "lin", "xat", "ffn", "n1", "n2"]
TRANSPOSED = ["t_in", "t_g1", "t_g2", "t_lin", "t_xat", "t_n1", "t_n2"]
AFFINE = ["g1", "g2", "g3", "n1", "n2"]
BCAST = ["bv1", "bv2", "g1", "be1", "g2", "be2", "g3", "be3", "bf2", "lb", "bv3",
         "n1w", "n1b", "n2w", "n2b"]


STEPS = [(tt, c) for tt in range(TPB) for c in range(2) if tt < 4 * (c + 1)]


def attention_plan():
    for n in range(GROUPS + 1):
        maxima = [(j, st) for j in range(GRP) for st in range(TPB)] if n < GROUPS else []
        units = len(STEPS) * GRP
        done = 0
        for u in range(units):
            if n > 0:
                tt, c = STEPS[u // GRP]
                yield "score", n - 1, tt, c, u % GRP
            if u == 1 and n > 1:
                yield "evac", n - 2
            if u == 7 and n > 1:
                yield "out", n - 2
            while done < len(maxima) and done * (units - 10) <= u * len(maxima):
                yield ("max", n) + maxima[done]
                done += 1
            if u == units - 6 and n < GROUPS:
                yield "neg", n
            if n > 0 and u % GRP == 1 and u > GRP:
                yield ("pv", n - 1) + STEPS[u // GRP - 1]
        if n > 0:
            yield ("pv", n - 1) + STEPS[-1]
    yield "evac", GROUPS - 1
    yield "out", GROUPS - 1


def build(nc, a, out, stop=None):
    ctx = ExitStack()
    with ctx:
        def sb(name, shape, dt):
            return ctx.enter_context(nc.sbuf_tensor(name, shape, dt))

        def sem(name):
            return ctx.enter_context(nc.semaphore(name))

        X = sb("X", [P, TILES, D], F32)
        H = sb("H", [P, TILES, D], F32)
        TR = sb("TR", [P, KC, N], F32)
        W6 = sb("W6", [P, 6 * KC * D], F32)
        BC = sb("BC", [P, len(BCAST), D], F32)
        ARENA = sb("ARENA", [P, 31696], F32)
        PS = ctx.enter_context(nc.psum_tensor("PS", [P, 8, 512], F32))

        def bc(name):
            return BC[:, BCAST.index(name), :]

        def region(lo, n, pattern=None, parts=P, **kw):
            v = ARENA[0:parts, lo:lo + n]
            return v.rearrange(pattern, **kw) if pattern else v

        def w6(n):
            return W6[:, n * KC * D:(n + 1) * KC * D].rearrange("p (k f) -> p k f", k=KC)

        ident = sb("ident", [P, P], F32)
        identb = sb("identb", [P, P], BF16)
        maskq = sb("maskq", [P, P], BF16)
        maskk = sb("maskk", [P, P], BF16)
        blockm = sb("blockm", [P, 8], F32)
        lower = sb("lower", [P, EXPERTS, EXPERTS], F32)
        halves = sb("halves", [P, TILES], F32)
        halfp = sb("halfp", [P, TILES], F32)
        stats = sb("stats", [P, TILES, 6], F32)
        mv = sb("mv", [P, TILES, 2], F32)
        var = sb("var", [P, TILES], F32)
        rstd = sb("rstd", [P, TILES], F32)
        tmp = sb("tmp", [P, 2, D], F32)
        ctxT = sb("ctxT", [P, KC, B * T], F32)
        bf1c = sb("bf1c", [P, FCH], F32)
        bq3c = sb("bq3c", [P, KC], F32)
        bk3c = sb("bk3c", [P, KC], F32)
        mx = sb("mx", [P, 2, HEADS], F32)
        sims = sb("sims", [P, 2, KC, EXPERTS], F32)
        simsq = sb("simsq", [P, 2, KC, EXPERTS], F32)
        siminv = sb("siminv", [P, 2, EXPERTS], F32)
        gates = sb("gates", [P, 2, EXPERTS], F32)
        ss = sb("ss", [P, TILES], F32)
        ssr = sb("ssr", [P, TILES], F32)
        NL = TPB * EXPERTS
        gsm = sb("gsm", [P, 4, TPB], F32)
        rw = sb("rw", [P, 2, TILES, EXPERTS], F32)
        l1s = sb("l1s", [P, 2, 4], F32)

        PACKQ = [region(2048 * s, 2048).bitcast(BF16).rearrange("p (j s) -> p j s", j=GRP)
                 for s in range(SLOTS)]
        PACKK = [region(6144 + 2048 * s, 2048).bitcast(BF16).rearrange("p (j s) -> p j s", j=GRP)
                 for s in range(SLOTS)]
        PARTS = [region(12288 + 1536 * s, 1536).bitcast(BF16).rearrange("p (c s) -> p c s", c=3)
                 for s in range(4)]
        SA = region(12288, 4096, "p (i f) -> p i f", i=TILES)
        PROB = [region(18432 + 512 * s, 512) for s in range(8)]
        VEXT = region(22528, TILES * HEADS * VW, "p (i h e) -> p i h e", i=TILES, h=HEADS)
        OTS = region(26880, 1024)
        REST = [region(27904 + 512 * s, 512) for s in range(3)]
        ones = region(30000, P)
        mrest = region(30128, P, parts=GRP * TPB)
        mparts = region(30256, 3 * P, parts=GRP * TPB).bitcast(BF16).rearrange("p (u c s) -> p u c s", u=2, c=3)
        negm = region(30640, 2 * GRP * TPB, "p (u m) -> p u m", u=2)
        rsum = region(30704, GRP * TPB)
        QT = region(0, 4096, "p (g s) -> p g s", g=2)
        KBD = region(4096, B * 2 * 8 * T, "p (b g h t) -> p b g h t", b=B, g=2, h=8)
        VX = region(6560, B * HEADS * VW, "p (b h e) -> p b h e", parts=T, b=B, h=HEADS)
        EX = [region(7104 + 1232 * s, HEADS * T, "p (h t) -> p h t", h=HEADS) for s in range(2)]
        PTS = [region(9568 + 2048 * s, 2048, "p (h s) -> p h s", parts=T, h=HEADS) for s in range(2)]
        KTX = region(13664, 2 * B * T, "p (g t) -> p g t", g=2)
        W3 = region(13972, 1024, "p (w k f) -> p w k f", w=2, k=KC)
        MASKS = region(9568, 616).bitcast(I32).rearrange("p (i t) -> p i t", i=TPB)
        MASKB = region(10184, 154).bitcast(I32).rearrange("p (b t) -> p b t", b=B)
        KEEP = W6[:, 0:TILES * T].rearrange("p (i t) -> p i t", i=TILES)
        NEG = W6[:, TILES * T:2 * TILES * T].rearrange("p (i t) -> p i t", i=TILES)
        HT = [region(4096 * s, 4096, "p (f s) -> p f s", f=FCH) for s in range(2)]
        WF1 = region(16384, 2048, "p (k f) -> p k f", k=KC)
        WF2 = region(18432, 2048, "p (f d) -> p f d", f=FCH)
        WEFF = region(20480, 512, "p (k f) -> p k f", k=KC)
        DAUX = region(20992, 256, parts=100)
        LD1 = region(21248, 256, parts=4)
        LD2 = region(21504, 256, parts=50)
        UPT = region(21760, 256, parts=50)
        LDT = region(22016, 4, parts=100)
        LUT = region(22020, 50, parts=4)
        WO = region(21456, 2048, "p (e f) -> p e f", e=EXPERTS)
        WQKV = region(15312, 6144, "p (k e f) -> p k e f", k=KC, e=EXPERTS)
        W1 = region(23504, 4096, "p (k e f) -> p k e f", k=KC, e=EXPERTS)
        W2 = region(27600, 4096, "p (e k f) -> p e k f", e=EXPERTS, k=KC)
        QKV = region(0, 6144, "p (i f) -> p i f", i=TILES)
        QK1 = region(6144, 4096, "p (w s) -> p w s", w=2)
        NB = region(10240, 4096, "p (i f) -> p i f", i=TILES)
        P1 = [W6[:, 1024 * s:1024 * (s + 1)] for s in range(2)]
        PT1 = W6[:, 2048:3072].rearrange("p (t s) -> p t s", t=TPB)
        ATT = region(14336, 2 * HA, "p (u f) -> p u f", u=2)
        ATTT = region(14592, 2 * HA, "p (u f) -> p u f", u=2)
        SQ = region(6144, 2 * D, "p (u f) -> p u f", u=2)
        RANK = W6[:, 0:2 * NL * EXPERTS].rearrange("p (u i e j) -> p u i e j", u=2, i=TPB, e=EXPERTS)
        LG = W6[:, 1024:1536].rearrange("p (u n) -> p u n", u=8)
        INT = [region(8192 * s if s else 0, 8192, "p (c s) -> p c s", c=16) for s in range(2)]

        scratch = nc.dram_tensor("qk_parts", [B, 2, D, 3, S], BF16, kind="Internal").ap()

        bank_full = [sem(f"bank_full{k}") for k in range(8)]
        bank_free = [sem(f"bank_free{k}") for k in range(8)]
        consts = sem("consts")
        pool_chain = sem("pool_chain")
        dve_chain = sem("dve_chain")
        x_in = [sem(f"x_in{k}") for k in range(4)]
        ln_ready = sem("ln_ready")
        var_ready = sem("var_ready")
        rstd_ready = sem("rstd_ready")
        affine_ready = sem("affine_ready")
        hi_ready = sem("hi_ready")
        mid_ready = sem("mid_ready")
        parts_ready = sem("parts_ready")
        parts_out = [sem(f"parts_out{k}") for k in range(8)]
        pack_in = [sem(f"pack_in{k}") for k in range(SLOTS)]
        mparts_ready = sem("mparts_ready")
        mrows_in = [sem(f"mrows_in{k}") for k in range(SLOTS)]
        pv_done = sem("pv_done")
        sa_used = sem("sa_used")
        kv_ready = sem("kv_ready")
        shift_ready = sem("shift_ready")
        ex_ready = sem("ex_ready")
        sim_ready = sem("sim_ready")
        sim_sum = sem("sim_sum")
        sig_ready = sem("sig_ready")
        ss_ready = sem("ss_ready")
        ssr_ready = sem("ssr_ready")
        gate_in = sem("gate_in")
        gate_exp = sem("gate_exp")
        rw_ready = sem("rw_ready")
        bias_ready = sem("bias_ready")
        stored = sem("stored")

        loads = {"wq1": 1, "wk1": 1, "wv1": 1, "ctx": 1, "bc": 1, "wq2": 1, "wk2": 1, "wv2": 1, "bf1": 1, "bq3": 1,
                 "bk3": 1, "sims": 2, "gates": 2, "wf1": 1, "wf2": 1, "wt": 1, "lora": 4, "w1": 1, "w2": 1,
                 "wq3": 1, "wk3": 1, "wv3": 1, "wqkv": 1, "wo": 1, "masks": 2}
        load_sem = {name: sem("ld_" + name) for name in loads}

        def load(eng, name, dst, src):
            eng.dma_start(dst, src).then_inc(load_sem[name], 16)

        def loaded(eng, name):
            eng.wait_ge(load_sem[name], 16 * loads[name])

        last_use = {}
        uses = {}
        full_count = [0] * 8
        free_count = [0] * 8

        def claim(key, banks, readers=1, signals=1):
            waits = {}
            for k in banks:
                if k in last_use:
                    first, count = last_use[k]
                    waits[first] = max(waits.get(first, 0), count)
            for first, count in waits.items():
                nc.tensor.wait_ge(bank_free[first], count)
            full_count[banks[0]] += signals
            free_count[banks[0]] += readers
            for k in banks:
                last_use[k] = (banks[0], free_count[banks[0]])
            uses[key] = (banks[0], full_count[banks[0]], free_count[banks[0]])

        def filled(ins, key):
            ins.then_inc(bank_full[uses[key][0]], 1)

        def arrived(eng, key):
            eng.wait_ge(bank_full[uses[key][0]], uses[key][1])

        def released(ins, key):
            ins.then_inc(bank_free[uses[key][0]], 1)

        def drained(eng, key):
            eng.wait_ge(bank_free[uses[key][0]], uses[key][2])

        def ln_count(name, i):
            return TILES * LNS.index(name) + i + 1

        def affine_count(name, i):
            return TILES * AFFINE.index(name) + i + 1

        block = ctx.enter_context(nc.Block())

        @block.tensor
        def _(pe):
            def mm(o, lhsT, rhs, start=True, stop=True, **kw):
                return nc.tensor.matmul(o, lhsT, rhs, start=start, stop=stop, **kw)

            def transposes(name, src, ready, base):
                for i in range(TILES):
                    bank = base + i % 2
                    claim((name, i), [bank])
                    ready(i)
                    for k in range(KC):
                        ins = nc.tensor.transpose(PS[:, bank, P * k:P * k + P], src[:, i, P * k:P * k + P], ident[:, :])
                    filled(ins, (name, i))

            def ln_done(name):
                return lambda i: pe.wait_ge(ln_ready, ln_count(name, i))

            def affine_done(name):
                return lambda i: pe.wait_ge(affine_ready, affine_count(name, i))

            def tr_done(inst, i):
                drained(pe, (TRANSPOSED[inst], i))

            def qk_transposes(i):
                claim(("qk1", i), [2 + i % 2])
                drained(pe, ("qkv", i, EXPERTS - 1))
                for w in range(2):
                    ins = nc.tensor.transpose(PS[:, 2 + i % 2, P * w:P * w + P], QKV[:, i, P * w:P * w + P], ident[:, :])
                filled(ins, ("qk1", i))

            pe.wait_ge(consts, 1)
            pe.wait_ge(sim_ready, 1)
            claim("simsum", [7])
            for n in range(2):
                for k in range(KC):
                    ins = mm(PS[:, 7, EXPERTS * n:EXPERTS * n + EXPERTS], ones, simsq[:, n, k, :],
                             start=k == 0, stop=k == KC - 1)
            filled(ins, "simsum")

            transposes("t_in", H, ln_done("in"), 0)
            bank = 2
            for b in range(B):
                tr_done(0, TPB * b + TPB - 1)
                for g in range(2):
                    for w in range(2):
                        loaded(pe, ("wq1", "wk1")[w])
                        for c in range(2):
                            key = ("qk", b, g, w, c)
                            claim(key, [bank])
                            for k in range(KC):
                                ins = mm(PS[:, bank, :], w6(w)[:, k, P * g:P * g + P],
                                         TR[:, k, S * b + 512 * c:S * b + 512 * c + 512], start=k == 0, stop=k == KC - 1)
                            filled(ins, key)
                            bank = 2 + (bank - 1) % 6
                loaded(pe, "wv1")
                for i in range(TPB * b, TPB * b + TPB):
                    claim(("v1", i), [bank])
                    for k in range(KC):
                        ins = mm(PS[:, bank, 0:D], TR[:, k, P * i:P * i + P], w6(2)[:, k, :], start=k == 0, stop=k == KC - 1)
                    filled(ins, ("v1", i))
                    bank = 2 + (bank - 1) % 6

            wide = 0
            narrow = 0
            drained(pe, ("v1", TILES - 1))
            pe.wait_ge(consts, 2)
            for op, n, *at in attention_plan():
                slot, b = n % SLOTS, n // 4
                if op == "max":
                    j, st = at
                    if (j, st) == (0, 0):
                        pe.wait_ge(pack_in[slot], 12 * 16 * (n // SLOTS + 1))
                    claim(("max", n, j, st), [2 * wide, 2 * wide + 1])
                    for c in range(st // 4 + 1):
                        cols = min(512, P * (st + 1) - 512 * c)
                        diag = c == st // 4
                        ins = mm(PS[:, 2 * wide + c, 0:cols], PACKQ[slot][0:ROWS, j, P * st:P * st + P],
                                 PACKK[slot][0:ROWS, j, 512 * c:512 * c + cols], stop=not diag)
                        if diag:
                            ins = mm(PS[:, 2 * wide + c, cols - P:cols], identb[:, :], maskq[:, :], start=False)
                    filled(ins, ("max", n, j, st))
                    wide = 1 - wide
                elif op == "neg":
                    claim(("neg", n), [2 * wide, 2 * wide + 1])
                    drained(pe, ("max", n, GRP - 1, TPB - 1))
                    filled(nc.tensor.transpose(PS[0:GRP * TPB, 2 * wide, 0:P], negm[:, n % 2, :], ident[:, :]), ("neg", n))
                    wide = 1 - wide
                elif op == "score":
                    tt, c, j = at
                    if (tt, c, j) == (0, 0, 0):
                        pe.wait_ge(mrows_in[slot], 3 * 16 * (n // SLOTS + 1))
                    lo = max(P * tt, 512 * c)
                    w = 512 * c + 512 - lo
                    diag = lo == P * tt
                    bank = 4 + narrow
                    claim(("score", n, tt, c, j), [bank])
                    ins = mm(PS[:, bank, 0:w], PACKK[slot][0:ROWS + 3, j, P * tt:P * tt + P],
                             PACKQ[slot][0:ROWS + 3, j, lo:lo + w], stop=not diag)
                    if diag:
                        ins = mm(PS[:, bank, 0:P], identb[:, :], maskk[:, :], start=False)
                    filled(ins, ("score", n, tt, c, j))
                    narrow = 1 - narrow
                elif op == "pv":
                    tt, c = at
                    if (tt, c) == (0, 0):
                        claim(("values", n), [6, 7], signals=0)
                    lo = max(P * tt, 512 * c)
                    w = 512 * c + 512 - lo
                    drained(pe, ("score", n, tt, c, GRP - 1))
                    for j in range(GRP):
                        ins = mm(PS[32 * j:32 * j + VW, 6 + c, lo - 512 * c:512],
                                 VEXT[:, TPB * b + tt, GRP * (n % 4) + j, :],
                                 PROB[GRP * (STEPS.index((tt, c)) % 2) + j][:, 0:w], start=tt == 0, stop=tt == 4 * c + 3)
                    ins.then_inc(pv_done, 1)
                elif op == "out":
                    drained(pe, ("values", n))
                    claim(("out", n), [2 * wide, 2 * wide + 1])
                    for st in range(TPB):
                        ins = nc.tensor.transpose(PS[:, 2 * wide + st // 4, P * (st % 4):P * (st % 4) + P],
                                                  OTS[:, P * st:P * st + P], ident[:, :])
                    filled(ins, ("out", n))
                    wide = 1 - wide

            def cross(layer, wq, wk, wv, inst):
                pe.wait_ge(sa_used, 4)
                loaded(pe, wk[1])
                loaded(pe, "ctx")
                for g in range(2):
                    claim(("kx", layer, g), [6 + g])
                    for k in range(KC):
                        ins = mm(PS[:, 6 + g, 0:B * T], wk[0][:, k, P * g:P * g + P], ctxT[:, k, :], start=k == 0, stop=k == KC - 1)
                    filled(ins, ("kx", layer, g))
                loaded(pe, wv[1])
                for b in range(B):
                    claim(("vx", layer, b), [6 + b])
                    for k in range(KC):
                        ins = mm(PS[0:T, 6 + b, 0:D], ctxT[:, k, T * b:T * b + T], wv[0][:, k, :], start=k == 0, stop=k == KC - 1)
                    filled(ins, ("vx", layer, b))
                loaded(pe, wq[1])
                for c in range(4):
                    tr_done(inst, 4 * c + 3)
                    for g in range(2):
                        key = ("q", layer, c, g)
                        claim(key, [2 + (2 * c + g) % 4])
                        for k in range(KC):
                            ins = mm(PS[:, 2 + (2 * c + g) % 4, :], wq[0][:, k, P * g:P * g + P],
                                     TR[:, k, 512 * c:512 * c + 512], start=k == 0, stop=k == KC - 1)
                        filled(ins, key)
                pe.wait_ge(kv_ready, 2 * B * (layer + 1))
                for b in range(B):
                    drained(pe, ("vx", layer, b))
                for i in range(TILES + 1):
                    if i < TILES:
                        drained(pe, ("q", layer, i // 4, 0))
                        drained(pe, ("q", layer, i // 4, 1))
                        claim(("sx", layer, i), [0, 1, 2, 3])
                        for m in range(4):
                            ins = mm(PS[:, m, 0:4 * T], QT[:, m // 2, P * i:P * i + P],
                                     KBD[:, i // TPB, m // 2, 4 * (m % 2):4 * (m % 2) + 4, :])
                        filled(ins, ("sx", layer, i))
                    if i > 0:
                        t = i - 1
                        pe.wait_ge(ex_ready, TILES * layer + t + 1)
                        for m in range(4):
                            claim(("px", layer, t, m), [4 + m % 2])
                            for h in range(4):
                                ins = nc.tensor.transpose(PS[0:T, 4 + m % 2, P * h:P * h + P],
                                                          EX[t % 2][:, 4 * m + h, :], ident[:, :])
                            filled(ins, ("px", layer, t, m))
                        claim(("ox", layer, t), [6 + t % 2])
                        drained(pe, ("px", layer, t, 2))
                        drained(pe, ("px", layer, t, 3))
                        for h in range(HEADS):
                            ins = mm(PS[:, 6 + t % 2, VW * h:VW * h + VW], PTS[t % 2][:, h, :], VX[:, t // TPB, h, :])
                        filled(ins, ("ox", layer, t))

            transposes("t_g1", H, affine_done("g1"), 0)
            cross(0, (w6(3), "wq2"), (w6(4), "wk2"), (w6(5), "wv2"), 1)

            transposes("t_g2", H, affine_done("g2"), 0)
            loaded(pe, "wf1")
            loaded(pe, "wf2")
            for c in range(5):
                if c < 4:
                    tr_done(2, 4 * c + 3)
                    for f in range(FCH):
                        key = ("f1", c, f)
                        claim(key, [2 + f % 4])
                        for k in range(KC):
                            ins = mm(PS[:, 2 + f % 4, :], WF1[:, k, P * f:P * f + P], TR[:, k, 512 * c:512 * c + 512],
                                     start=k == 0, stop=k == KC - 1)
                        filled(ins, key)
                if c > 0:
                    for f in range(FCH - 4, FCH):
                        drained(pe, ("f1", c - 1, f))
                    for i in range(4 * c - 4, 4 * c):
                        claim(("f2", i), [6 + i % 2])
                        for f in range(FCH):
                            ins = mm(PS[:, 6 + i % 2, 0:D], HT[(c - 1) % 2][:, f, P * (i % 4):P * (i % 4) + P], WF2[:, f, :],
                                     start=f == 0, stop=f == FCH - 1)
                        filled(ins, ("f2", i))

            loaded(pe, "lora")
            claim("l1", [2])
            filled(mm(PS[0:4, 2, 0:D], LDT, DAUX), "l1")
            drained(pe, "l1")
            claim("l2", [3])
            filled(mm(PS[0:50, 3, 0:D], LUT, LD1), "l2")
            drained(pe, "l2")
            claim("l3", [4])
            for k in range(KC):
                ins = mm(PS[:, 4, D * k:D * k + D], LD2[:, P * k:P * k + P], UPT)
            filled(ins, "l3")
            transposes("t_lin", H, ln_done("lin"), 0)
            drained(pe, "l3")
            for i in range(TILES):
                tr_done(3, i)
                claim(("lin", i), [2 + i % 4])
                for k in range(KC):
                    ins = mm(PS[:, 2 + i % 4, 0:D], TR[:, k, P * i:P * i + P], WEFF[:, k, :], start=k == 0, stop=k == KC - 1)
                filled(ins, ("lin", i))

            transposes("t_xat", H, ln_done("xat"), 0)
            cross(1, (w6(5), "wq3"), (W3[:, 0, :, :], "wk3"), (W3[:, 1, :, :], "wv3"), 4)

            def logits(n, i):
                claim(("lg", n, i), [2 + i % 2])
                for k in range(KC):
                    ins = mm(PS[:, 2 + i % 2, 0:EXPERTS], TR[:, k, P * i:P * i + P], sims[:, n, k, :], start=k == 0, stop=k == KC - 1)
                filled(ins, ("lg", n, i))

            transposes("t_n1", NB, affine_done("n1"), 0)
            for i in range(TILES):
                tr_done(5, i)
                logits(0, i)
            loaded(pe, "wqkv")
            for i in range(TILES):
                for e in range(EXPERTS):
                    bank = 4 + (EXPERTS * i + e) % 4
                    key = ("qkv", i, e)
                    claim(key, [bank])
                    for k in range(KC):
                        ins = mm(PS[:, bank, 0:3 * HA], TR[:, k, P * i:P * i + P], WQKV[:, k, e, :], start=k == 0, stop=k == KC - 1)
                    filled(ins, key)
                if i > 0:
                    qk_transposes(i - 1)
            qk_transposes(TILES - 1)
            loaded(pe, "wo")
            for i in range(TILES + 2):
                if i < TILES:
                    b, st = i // TPB, i % TPB
                    drained(pe, ("qk1", i))
                    claim(("s1", i), [0, 1])
                    for c in range(st // 4 + 1):
                        cols = min(512, P * (st + 1) - 512 * c)
                        diag = c == st // 4
                        ins = mm(PS[:, c, 0:cols], QK1[:, 0, P * i:P * i + P],
                                 QK1[:, 1, S * b + 512 * c:S * b + 512 * c + cols], stop=not diag)
                        if diag:
                            ins = mm(PS[:, c, cols - P:cols], identb[:, :], maskq[:, :], start=False)
                    filled(ins, ("s1", i))
                if 1 <= i <= TILES:
                    t = i - 1
                    st = t % TPB
                    drained(pe, ("s1", t))
                    claim(("p1", t), [2, 3])
                    for tt in range(st + 1):
                        ins = nc.tensor.transpose(PS[:, 2 + tt // 4, P * (tt % 4):P * (tt % 4) + P],
                                                  P1[t % 2][:, P * tt:P * tt + P], ident[:, :])
                    filled(ins, ("p1", t))
                    claim(("a1", t), [4])
                    drained(pe, ("p1", t))
                    for tt in range(st + 1):
                        ins = mm(PS[:, 4, 0:HA], PT1[:, tt, :], QKV[:, TPB * (t // TPB) + tt, 2 * HA:3 * HA], start=tt == 0, stop=tt == st)
                    filled(ins, ("a1", t))
                if i >= 2:
                    t = i - 2
                    drained(pe, ("a1", t))
                    claim(("at", t), [5])
                    filled(nc.tensor.transpose(PS[:, 5, 0:HA], ATT[:, t % 2, :], ident[:, :]), ("at", t))
                    drained(pe, ("at", t))
                    for m in range(4):
                        claim(("o1", t, m), [6 + m % 2])
                        ins = mm(PS[:, 6 + m % 2, :], ATTT[:, t % 2, :], WO[:, 2 * m:2 * m + 2, :])
                        filled(ins, ("o1", t, m))

            transposes("t_n2", NB, affine_done("n2"), 0)
            for i in range(TILES):
                tr_done(6, i)
                logits(1, i)
            loaded(pe, "w1")
            loaded(pe, "w2")
            for c in range(5):
                if c < 4:
                    for m in range(2 * EXPERTS):
                        e, ic = m // 2, m % 2
                        claim(("m1", c, m), [2 + m % 4])
                        for k in range(KC):
                            ins = mm(PS[:, 2 + m % 4, :], W1[:, k, e, P * ic:P * ic + P], TR[:, k, 512 * c:512 * c + 512],
                                     start=k == 0, stop=k == KC - 1)
                        filled(ins, ("m1", c, m))
                if c > 0:
                    for m in range(2 * EXPERTS - 4, 2 * EXPERTS):
                        drained(pe, ("m1", c - 1, m))
                    for i in range(4 * c - 4, 4 * c):
                        for e in range(EXPERTS):
                            bank = (0, 1, 6, 7)[e % 4]
                            claim(("m2", i, e), [bank])
                            for k in range(KC):
                                ins = mm(PS[:, bank, 0:D], INT[(c - 1) % 2][:, 2 * e + k, P * (i % 4):P * (i % 4) + P], W2[:, e, k, :],
                                         start=k == 0, stop=k == KC - 1)
                            filled(ins, ("m2", i, e))

        @block.sync
        def _(sp):
            def wload(name, dst, key, pattern="(k p) f -> p k f", **kw):
                load(sp, name, dst, a[key].rearrange(pattern, **kw))

            xd = a["x"].rearrange("(i p) d -> p i d", p=P)
            for k in range(4):
                sp.dma_start(X[:, 4 * k:4 * k + 4, :], xd[:, 4 * k:4 * k + 4, :]).then_inc(x_in[k], 16)
                if k == 0:
                    wload("wq1", w6(0), "wq1", p=P)
                    wload("wk1", w6(1), "wk1", p=P)
            load(sp, "ctx", ctxT[:, :, :], a["ctxT"].rearrange("(k p) t -> p k t", p=P))
            wload("wv1", w6(2), "wv1", p=P)
            load(sp, "bc", BC[:, :, :], a["bcast"].rearrange("(o n) d -> o n d", o=1).broadcast_to([P, len(BCAST), D]))
            for n, name in enumerate(("wq2", "wk2", "wv2")):
                wload(name, w6(3 + n), name, p=P)
            load(sp, "bf1", bf1c[:, :], a["bf1"])
            load(sp, "bq3", bq3c[:, :], a["bq3"])
            load(sp, "bk3", bk3c[:, :], a["bk3"])
            for n, name in enumerate(("sim1", "sim2")):
                load(sp, "sims", sims[:, n, :, :], a[name].rearrange("(k p) e -> p k e", p=P))
            for n, name in enumerate(("gates1", "gates2")):
                load(sp, "gates", gates[:, n, :],
                     a[name].rearrange("(o e) -> o e", o=1).broadcast_to([P, EXPERTS]))

            def load_pack(n):
                b, h0 = n // 4, GRP * (n % 4)
                for w, packs, order in ((0, PACKQ, QPART), (1, PACKK, KPART)):
                    src = scratch[b, w].rearrange("(h e) c s -> c e h s", h=HEADS)
                    for r, part in enumerate(order):
                        sp.dma_start(packs[n % SLOTS][HD * r:HD * r + HD, :, :],
                                     src[part, :, h0:h0 + GRP, :]).then_inc(pack_in[n % SLOTS], 16)

            for u in range(8):
                b, g, w = u // 4, u // 2 % 2, u % 2
                sp.wait_ge(parts_ready, 2 * (u + 1))
                sp.dma_start(scratch[b, w, P * g:P * g + P, :, :], PARTS[u % 4]).then_inc(parts_out[u], 16)
                if u == 1:
                    for v in (0, 1):
                        sp.wait_ge(parts_out[v], 16)
                    load_pack(0)
                    load_pack(1)
            for v in range(2, 8):
                sp.wait_ge(parts_out[v], 16)
            load_pack(2)

            for n in range(GROUPS):
                sp.wait_ge(mparts_ready, n + 1)
                for r in range(3):
                    sp.dma_start(PACKQ[n % SLOTS][ROWS + r:ROWS + r + 1, :, :].rearrange("o j (t s) -> o (j t) s", s=P),
                                 mparts[:, n % 2, r, :]).then_inc(mrows_in[n % SLOTS], 16)
                if 1 <= n < GROUPS - 2:
                    arrived(sp, ("score", n - 1, TPB - 1, 1, GRP - 1))
                    load_pack(n + 2)

            sp.wait_ge(sa_used, 4)
            wload("wf1", WF1, "wf1", p=P)
            wload("wf2", WF2, "wf2", "(f p) d -> p f d", p=P)
            wload("wt", WEFF, "wt", p=P)
            load(sp, "lora", DAUX, a["daux"])
            load(sp, "lora", UPT, a["upT"])
            load(sp, "lora", LDT, a["ldT"])
            load(sp, "lora", LUT, a["luT"])
            load(sp, "w1", W1, a["w1"].rearrange("(k p) e f -> p k e f", p=P))
            load(sp, "w2", W2, a["w2"].rearrange("(m p) f -> p m f", p=P).rearrange("p (e k) f -> p e k f", k=KC))
            drained(sp, ("lin", TILES - 1))
            wload("wq3", w6(5), "wq3", p=P)
            for n, name in enumerate(("wk3", "wv3")):
                wload(name, W3[:, n, :, :], name, p=P)
            load(sp, "wqkv", WQKV, a["wqkv"].rearrange("(k p) e f -> p k e f", p=P))
            wload("wo", WO, "wo", "e p f -> p e f")
            load(sp, "masks", MASKS, a["mask_st"].rearrange("(i p) t -> p i t", p=P))
            load(sp, "masks", MASKB,
                 a["mask_bt"].rearrange("(o b) t -> o b t", o=1).broadcast_to([P, B, T]))

            od = out.rearrange("(i p) d -> p i d", p=P)
            for c in range(8):
                drained(sp, ("m2", 2 * c + 1, EXPERTS - 1))
                sp.dma_start(od[:, 2 * c:2 * c + 2, :], X[:, 2 * c:2 * c + 2, :]).then_inc(stored, 16)
            sp.wait_ge(stored, 16 * 8)

        @block.scalar
        def _(act):
            def evacuate(name, inst):
                for i in range(TILES):
                    arrived(act, (name, i))
                    bank = uses[(name, i)][0]
                    ins = nc.scalar.copy(TR[:, :, P * i:P * i + P], PS[:, bank, 0:D].rearrange("p (k s) -> p k s", k=KC))
                    released(ins, (name, i))

            loaded(act, "gates")
            nc.scalar.activation(gates[:, :, :], gates[:, :, :], ACT.Exp, scale=-1.0).then_inc(sig_ready, 1)

            evacuate("t_in", 0)
            keys = [(b, g, w, c) for b in range(B) for g in range(2) for w in range(2) for c in range(2)]
            for u, mid in [(8 * b + w, w > 0) for b in range(B) for w in range(9)]:
                if not mid or u % 8:
                    b, g, w, c = keys[u]
                    arrived(act, ("qk",) + keys[u])
                    if u >= 8:
                        act.wait_ge(parts_out[u // 2 - 4], 16)
                    nc.scalar.copy(PARTS[u // 2 % 4][:, 0, 512 * c:512 * c + 512],
                                   PS[:, uses[("qk",) + keys[u]][0], :]).then_inc(hi_ready, 1)
                if mid:
                    v = u - 1
                    drained(act, ("qk",) + keys[v])
                    nc.scalar.copy(PARTS[v // 2 % 4][:, 1, 512 * (v % 2):512 * (v % 2) + 512],
                                   REST[v % 3]).then_inc(mid_ready, 1)

            step_exp = 0
            for op, n, *at in attention_plan():
                if op == "score":
                    tt, c, j = at
                    key = ("score", n, tt, c, j)
                    w = 512 * c + 512 - max(P * tt, 512 * c)
                    step = step_exp // GRP
                    arrived(act, key)
                    if step >= 2:
                        act.wait_ge(pv_done, step - 1)
                    ins = nc.scalar.activation(PROB[GRP * (step % 2) + j][:, 0:w], PS[:, uses[key][0], 0:w], ACT.Exp,
                                               scale=HD ** -0.5)
                    released(ins, key)
                    step_exp += 1
                elif op == "evac":
                    act.wait_ge(pv_done, len(STEPS) * (n + 1))
                    if n > 0:
                        arrived(act, ("out", n - 1))
                    ins = nc.scalar.copy(OTS, PS[:, 6:8, :].rearrange("p b s -> p (b s)"))
                    released(ins, ("values", n))

            def cross(layer):
                act.wait_ge(sa_used, 4)
                for g in range(2):
                    arrived(act, ("kx", layer, g))
                    if layer == 0:
                        ins = nc.scalar.copy(KTX[:, g, :], PS[:, 6 + g, 0:B * T])
                    else:
                        ins = nc.scalar.activation(KTX[:, g, :], PS[:, 6 + g, 0:B * T], ACT.Identity, bias=bk3c[:, g:g + 1])
                    released(ins, ("kx", layer, g))
                for c in range(4):
                    for g in range(2):
                        key = ("q", layer, c, g)
                        arrived(act, key)
                        src = PS[:, uses[key][0], :]
                        if layer == 0:
                            ins = nc.scalar.copy(QT[:, g, 512 * c:512 * c + 512], src)
                        else:
                            ins = nc.scalar.activation(QT[:, g, 512 * c:512 * c + 512], src, ACT.Identity, bias=bq3c[:, g:g + 1])
                        released(ins, key)
                for i in range(TILES + 1):
                    if i < TILES:
                        if layer == 0:
                            drained(act, ("sx", 0, i))
                        else:
                            act.wait_ge(shift_ready, i + 1)
                        nc.scalar.activation(EX[i % 2], EX[i % 2], ACT.Exp, scale=HD ** -0.5).then_inc(ex_ready, 1)
                    if i > 0:
                        t = i - 1
                        if t >= 2:
                            arrived(act, ("ox", layer, t - 2))
                        for m in (0, 2):
                            key = ("px", layer, t, m)
                            arrived(act, key)
                            ins = nc.scalar.copy(PTS[t % 2][:, 4 * m:4 * m + 4, :],
                                                 PS[0:T, 4, :].rearrange("p (h s) -> p h s", h=4))
                            released(ins, key)

            evacuate("t_g1", 1)
            cross(0)
            evacuate("t_g2", 2)
            loaded(act, "bf1")
            for c in range(4):
                if c >= 2:
                    arrived(act, ("f2", 4 * (c - 2) + 3))
                for f in range(FCH):
                    key = ("f1", c, f)
                    arrived(act, key)
                    ins = nc.scalar.activation(HT[c % 2][:, f, :], PS[:, uses[key][0], :], ACT.Relu, bias=bf1c[:, f:f + 1])
                    released(ins, key)
            evacuate("t_lin", 3)
            evacuate("t_xat", 4)
            loaded(act, "bq3")
            loaded(act, "bk3")
            cross(1)

            def gate(n):
                for i in range(TILES):
                    act.wait_ge(affine_ready, affine_count(("n1", "n2")[n], i))
                    if i >= 2:
                        act.wait_ge(ss_ready, TILES * n + i - 1)
                    nc.scalar.activation(SQ[:, i % 2, :], NB[:, i, :], ACT.Square, accum_out=ss[:, i:i + 1]).then_inc(ss_ready, 1)
                for b in range(B):
                    act.wait_ge(gate_in, 2 * n + b + 1)
                    nc.scalar.activation(LG[:, 5, :], LG[:, 4, :], ACT.Exp).then_inc(gate_exp, 1)

            evacuate("t_n1", 5)
            gate(0)
            for i in range(TILES):
                arrived(act, ("qk1", i))
                ins = nc.scalar.copy(QK1[:, :, P * i:P * i + P], PS[:, 2 + i % 2, 0:2 * P].rearrange("p (w s) -> p w s", w=2))
                released(ins, ("qk1", i))
            for i in range(TILES + 2):
                if i < TILES:
                    cols = P * (i % TPB + 1)
                    act.wait_ge(bias_ready, i + 1)
                    if i >= 2:
                        arrived(act, ("p1", i - 2))
                    ins = nc.scalar.activation(P1[i % 2][:, 0:cols], PS[:, 0:2, :].rearrange("p b s -> p (b s)")[:, 0:cols], ACT.Exp,
                                               bias=l1s[:, i % 2, 0:1], scale=HA ** -0.5, accum_out=l1s[:, i % 2, 1:2])
                    released(ins, ("s1", i))
                if 1 <= i <= TILES:
                    t = i - 1
                    arrived(act, ("p1", t))
                    if t > 0:
                        arrived(act, ("a1", t - 1))
                    cols = P * (t % TPB + 1)
                    ins = nc.scalar.copy(PT1.rearrange("p t s -> p (t s)")[:, 0:cols],
                                         PS[:, 2:4, :].rearrange("p b s -> p (b s)")[:, 0:cols])
                    released(ins, ("p1", t))
                if i >= 2:
                    t = i - 2
                    arrived(act, ("at", t))
                    if t >= 2:
                        arrived(act, ("o1", t - 2, 3))
                    ins = nc.scalar.copy(ATTT[:, t % 2, :], PS[:, 5, 0:HA])
                    released(ins, ("at", t))

            evacuate("t_n2", 6)
            gate(1)
            act.wait_ge(rw_ready, 4)
            for c in range(4):
                if c >= 2:
                    arrived(act, ("m2", 4 * (c - 2) + 3, EXPERTS - 1))
                for m in range(2 * EXPERTS):
                    key = ("m1", c, m)
                    arrived(act, key)
                    ins = nc.scalar.activation(INT[c % 2][:, m, :], PS[:, uses[key][0], :], ACT.Gelu)
                    released(ins, key)

        @block.vector
        def _(dve):
            links = [0]

            def link(ins):
                links[0] += 1
                ins.then_inc(dve_chain, 1)
                dve.wait_ge(dve_chain, links[0])

            v = nc.vector
            norms = [0]

            def layernorm(src, dst, tiles):
                lo, hi = tiles[0], tiles[-1] + 1
                for i in tiles:
                    ins = v.bn_stats(stats[:, i, :], src[:, i, :])
                link(ins)
                for i in tiles:
                    ins = v.bn_aggr(mv[:, i, :], stats[:, i, :])
                link(ins)
                v.tensor_scalar(var[:, lo:hi], mv[:, lo:hi, 1:2].rearrange("p i o -> p (i o)"), EPS, None,
                                ALU.add).then_inc(var_ready, 1)
                norms[0] += 1
                dve.wait_ge(rstd_ready, norms[0])
                for i in tiles:
                    v.tensor_scalar(dst[:, i, :], src[:, i, :], mv[:, i, 0:1], rstd[:, i:i + 1],
                                    ALU.subtract, ALU.mult).then_inc(ln_ready, 1)

            loaded(dve, "sims")
            v.tensor_tensor(simsq[:, :, :, :], sims[:, :, :, :], sims[:, :, :, :], ALU.mult).then_inc(sim_ready, 1)
            arrived(dve, "simsum")
            ins = v.tensor_copy(siminv[:, :, :], PS[:, 7, 0:2 * EXPERTS].rearrange("p (n e) -> p n e", n=2))
            released(ins, "simsum")
            dve.wait_ge(sim_sum, 1)
            link(v.tensor_scalar(siminv[:, :, :], siminv[:, :, :], 1e-12, None, ALU.max))
            link(v.reciprocal(siminv[:, :, :], siminv[:, :, :]))
            link(v.tensor_tensor(sims[:, :, :, :], sims[:, :, :, :],
                                 siminv[:, :, :].unsqueeze(2).broadcast_to([P, 2, KC, EXPERTS]), ALU.mult))
            dve.wait_ge(sig_ready, 1)
            link(v.tensor_scalar(gates[:, :, :], gates[:, :, :], 1.0, None, ALU.add))
            link(v.reciprocal(gates[:, :, :], gates[:, :, :]))

            batches = [list(range(4 * k, 4 * k + 4)) for k in range(4)]
            for k in range(4):
                dve.wait_ge(x_in[k], 16)
                layernorm(X, H, batches[k])

            loaded(dve, "bc")
            u = 0
            for b in range(B):
                for w in range(9):
                    if w < 8:
                        key = ("qk", b, w // 4, w // 2 % 2, w % 2)
                        part = PARTS[u // 2 % 4]
                        dve.wait_ge(hi_ready, u + 1)
                        if u >= 3:
                            dve.wait_ge(parts_ready, u - 2)
                        ins = v.tensor_tensor(REST[u % 3], PS[:, uses[key][0], :], part[:, 0, 512 * (u % 2):512 * (u % 2) + 512],
                                              ALU.subtract)
                        released(ins, key)
                        u += 1
                    if w > 0:
                        t = u - 2 if w < 8 else u - 1
                        part = PARTS[t // 2 % 4]
                        dve.wait_ge(mid_ready, t + 1)
                        drained(dve, ("qk", b, t // 4 % 2, t // 2 % 2, t % 2))
                        v.tensor_tensor(part[:, 2, 512 * (t % 2):512 * (t % 2) + 512], REST[t % 3],
                                        part[:, 1, 512 * (t % 2):512 * (t % 2) + 512], ALU.subtract).then_inc(parts_ready, 1)
                for i in range(TPB * b, TPB * b + TPB):
                    arrived(dve, ("v1", i))
                    ins = v.tensor_tensor(VEXT[:, i, :, 0:HD],
                                          PS[:, uses[("v1", i)][0], 0:D].rearrange("p (h e) -> p h e", h=HEADS),
                                          bc("bv1").rearrange("p (h e) -> p h e", h=HEADS), ALU.add)
                    released(ins, ("v1", i))

            for op, n, *at in attention_plan():
                if op == "max":
                    j, st = at
                    key = ("max", n, j, st)
                    bank = uses[key][0]
                    arrived(dve, key)
                    ins = v.tensor_reduce(negm[:, n % 2, TPB * j + st:TPB * j + st + 1],
                                          PS[:, bank:bank + 2, :].rearrange("p b s -> p (b s)")[:, 0:P * (st + 1)],
                                          AX.X, ALU.max, negate=True)
                    released(ins, key)
                elif op == "neg":
                    key = ("neg", n)
                    arrived(dve, key)
                    src = PS[0:GRP * TPB, uses[key][0], 0:P]
                    if n >= 2:
                        dve.wait_ge(mrows_in[(n - 2) % SLOTS], 3 * 16 * ((n - 2) // SLOTS + 1))
                    link(v.tensor_copy(mparts[:, n % 2, 0, :], src))
                    ins = v.tensor_tensor(mrest, src, mparts[:, n % 2, 0, :], ALU.subtract)
                    released(ins, key)
                    drained(dve, key)
                    link(v.tensor_copy(mparts[:, n % 2, 1, :], mrest))
                    v.tensor_tensor(mparts[:, n % 2, 2, :], mrest, mparts[:, n % 2, 1, :],
                                    ALU.subtract).then_inc(mparts_ready, 1)
                elif op == "out":
                    key = ("out", n)
                    arrived(dve, key)
                    if n == 0:
                        for k in range(8):
                            dve.wait_ge(parts_out[k], 16)
                    else:
                        drained(dve, ("out", n - 1))
                    src = PS[:, uses[key][0]:uses[key][0] + 2, :].rearrange("p b (m e) -> p (b m) e", e=32)
                    link(v.reciprocal(rsum, src[:, :, HD:HD + 1].rearrange("p m o -> p (m o)")))
                    c0 = GRP * HD * (n % 4)
                    ins = v.tensor_tensor(SA[:, TPB * (n // 4):TPB * (n // 4) + TPB, c0:c0 + GRP * HD].rearrange("p i (j e) -> p i j e", j=GRP),
                                          src[:, :, 0:HD].rearrange("p (i j) e -> p i j e", i=TPB),
                                          rsum.rearrange("p (i j) -> p i j", i=TPB).unsqueeze(3).broadcast_to([P, TPB, GRP, HD]),
                                          ALU.mult)
                    released(ins, key)
            drained(dve, ("out", GROUPS - 1))
            for k in range(4):
                for i in batches[k]:
                    ins = v.tensor_tensor(H[:, i, :], H[:, i, :], SA[:, i, :], ALU.add)
                ins.then_inc(sa_used, 1)
                dve.wait_ge(sa_used, k + 1)
                layernorm(H, H, batches[k])

            def cross(layer):
                x = X if layer else H
                if layer == 0:
                    dve.wait_ge(sa_used, 4)
                else:
                    loaded(dve, "masks")
                    link(v.tensor_scalar(EX[0].rearrange("p h t -> p (h t)")[:, 0:B * T], MASKB.rearrange("p b t -> p (b t)"), 0.0, None, ALU.not_equal))
                    maskb = EX[0].rearrange("p h t -> p (h t)")[:, 0:B * T].rearrange("p (b t) -> p b t", b=B)
                    for b in range(B):
                        ins = v.tensor_scalar(KEEP[:, TPB * b:TPB * b + TPB, :], MASKS, 0.0, None, ALU.not_equal)
                    link(ins)
                    for b in range(B):
                        ins = v.tensor_tensor(KEEP[:, TPB * b:TPB * b + TPB, :], KEEP[:, TPB * b:TPB * b + TPB, :],
                                              maskb[:, b:b + 1, :].broadcast_to([P, TPB, T]), ALU.mult)
                    link(ins)
                    link(v.tensor_scalar(NEG, KEEP, -1.0, -MASKED / HD ** -0.5, ALU.add, ALU.mult))
                link(v.memset(VX[:, :, :, HD:HD + 1], 1.0))
                for g in range(2):
                    drained(dve, ("kx", layer, g))
                for b in range(B):
                    for g in range(2):
                        v.tensor_tensor(KBD[:, b, g, :, :],
                                        KTX[:, g, T * b:T * b + T].unsqueeze(1).broadcast_to([P, 8, T]),
                                        blockm[:, :].unsqueeze(2).broadcast_to([P, 8, T]), ALU.mult).then_inc(kv_ready, 1)
                for b in range(B):
                    key = ("vx", layer, b)
                    arrived(dve, key)
                    ins = v.tensor_tensor(VX[:, b, :, 0:HD], PS[0:T, 6 + b, 0:D].rearrange("p (h e) -> p h e", h=HEADS),
                                          bc(("bv2", "bv3")[layer])[0:T, :].rearrange("p (h e) -> p h e", h=HEADS), ALU.add)
                    released(ins, key)
                for i in range(TILES + 1):
                    if i < TILES:
                        key = ("sx", layer, i)
                        ex = EX[i % 2].rearrange("p (m h) t -> p m h t", m=4)
                        src = PS[:, 0:4, 0:4 * T].rearrange("p m (h t) -> p m h t", h=4)
                        m4 = mx[:, i % 2, :].rearrange("p (m h) -> p m h", m=4)
                        arrived(dve, key)
                        if i >= 2:
                            arrived(dve, ("px", layer, i - 2, 3))
                        if layer:
                            ins = v.tensor_tensor(ex, src, KEEP[:, i, :].unsqueeze(1).unsqueeze(1).broadcast_to([P, 4, 4, T]), ALU.mult)
                            released(ins, key)
                            drained(dve, key)
                            link(v.tensor_tensor(ex, ex, NEG[:, i, :].unsqueeze(1).unsqueeze(1).broadcast_to([P, 4, 4, T]), ALU.add))
                            src = ex
                        link(v.tensor_reduce(m4, src, AX.X, ALU.max))
                        ins = v.tensor_tensor(ex, src, m4.unsqueeze(3).broadcast_to([P, 4, 4, T]), ALU.subtract)
                        if layer:
                            ins.then_inc(shift_ready, 1)
                        else:
                            released(ins, key)
                    if i > 0:
                        t = i - 1
                        if t >= 2:
                            arrived(dve, ("ox", layer, t - 2))
                        for m in (1, 3):
                            key = ("px", layer, t, m)
                            arrived(dve, key)
                            ins = v.tensor_copy(PTS[t % 2][:, 4 * m:4 * m + 4, :],
                                                PS[0:T, 5, :].rearrange("p (h s) -> p h s", h=4))
                            released(ins, key)
                        key = ("ox", layer, t)
                        arrived(dve, key)
                        src = PS[:, 6 + t % 2, 0:HEADS * VW].rearrange("p (h e) -> p h e", h=HEADS)
                        link(v.reciprocal(mx[:, t % 2, :], src[:, :, HD:HD + 1].rearrange("p h o -> p (h o)")))
                        ins = v.tensor_tensor(tmp[:, t % 2, :].rearrange("p (h e) -> p h e", h=HEADS), src[:, :, 0:HD],
                                              mx[:, t % 2, :].unsqueeze(2).broadcast_to([P, HEADS, HD]), ALU.mult)
                        released(ins, key)
                        drained(dve, key)
                        link(v.tensor_tensor(x[:, t, :], x[:, t, :], tmp[:, t % 2, :], ALU.add))
                        if t % 4 == 3:
                            layernorm(x, H, batches[t // 4])

            dve.wait_ge(affine_ready, affine_count("g1", TILES - 1))
            cross(0)

            dve.wait_ge(affine_ready, affine_count("g2", TILES - 1))
            for i in range(TILES):
                arrived(dve, ("f2", i))
                ins = v.tensor_tensor(tmp[:, i % 2, :], PS[:, 6 + i % 2, 0:D], bc("bf2"), ALU.add)
                released(ins, ("f2", i))
                drained(dve, ("f2", i))
                link(v.tensor_tensor(H[:, i, :], H[:, i, :], tmp[:, i % 2, :], ALU.add))
                if i % 4 == 3:
                    layernorm(H, H, batches[i // 4])
            for n, (key, dst) in enumerate((("l1", LD1), ("l2", LD2))):
                arrived(dve, key)
                parts = (4, 50)[n]
                ins = v.tensor_copy(dst, PS[0:parts, 2 + n, 0:D])
                released(ins, key)
            arrived(dve, "l3")
            loaded(dve, "wt")
            ins = v.tensor_tensor(WEFF, WEFF, PS[:, 4, :].rearrange("p (k f) -> p k f", k=KC), ALU.add)
            released(ins, "l3")
            for k in range(4):
                dve.wait_ge(affine_ready, affine_count("g3", 4 * k + 3))
                for i in batches[k]:
                    ins = v.tensor_tensor(X[:, i, :], X[:, i, :], H[:, i, :], ALU.add)
                link(ins)
                layernorm(X, H, batches[k])
            for i in range(TILES):
                arrived(dve, ("lin", i))
                ins = v.tensor_tensor(tmp[:, i % 2, :], PS[:, 2 + i % 4, 0:D], bc("lb"), ALU.add)
                released(ins, ("lin", i))
                drained(dve, ("lin", i))
                link(v.tensor_tensor(X[:, i, :], X[:, i, :], tmp[:, i % 2, :], ALU.add))
                if i % 4 == 3:
                    layernorm(X, H, batches[i // 4])
            cross(1)

            for k in range(4):
                dve.wait_ge(ln_ready, ln_count("ffn", 4 * k + 3))
                layernorm(H, NB, batches[k])

            def gate(n):
                dve.wait_ge(ssr_ready, n + 1)
                link(v.tensor_scalar(ssr[:, :], ssr[:, :], 1e-12, None, ALU.max))
                link(v.reciprocal(ssr[:, :], ssr[:, :]))
                for b in range(B):
                    l = [LG[:, k, :].rearrange("p (i e) -> p i e", i=TPB) for k in range(8)]
                    for i in range(TPB * b, TPB * b + TPB):
                        key = ("lg", n, i)
                        arrived(dve, key)
                        ins = v.scalar_tensor_tensor(out=l[0][:, i % TPB, :], in0=PS[:, 2 + i % 2, 0:EXPERTS], scalar=ssr[:, i:i + 1],
                                                     in1=gates[:, n, :], op0=ALU.mult, op1=ALU.subtract)
                        released(ins, key)
                    drained(dve, ("lg", n, TPB * b + TPB - 2))
                    drained(dve, key)
                    full = [P, TPB, EXPERTS, EXPERTS]
                    other = l[0].unsqueeze(2).broadcast_to(full)
                    own = l[0].unsqueeze(3).broadcast_to(full)
                    v.tensor_tensor(RANK[:, 0], other, own, ALU.is_gt)
                    link(v.tensor_tensor(RANK[:, 1], other, own, ALU.is_equal))
                    link(v.tensor_tensor(RANK[:, 1], RANK[:, 1], lower[:, :, :].unsqueeze(1).broadcast_to(full), ALU.mult))
                    link(v.tensor_tensor(RANK[:, 0], RANK[:, 0], RANK[:, 1], ALU.add))
                    v.tensor_reduce(l[3], RANK[:, 0], AX.X, ALU.add)
                    v.tensor_scalar(l[2], l[0], 0.0, None, ALU.is_gt)
                    link(v.tensor_scalar(l[1], l[0], 0.0, None, ALU.max))
                    link(v.tensor_reduce(gsm[:, 0, :], l[1], AX.X, ALU.max))
                    per = [P, TPB, EXPERTS]
                    v.tensor_tensor(l[4], l[1], gsm[:, 0, :].unsqueeze(2).broadcast_to(per), ALU.subtract).then_inc(gate_in, 1)
                    link(v.tensor_scalar(gsm[:, 1, :], gsm[:, 0, :], 0.0, None, ALU.is_equal))
                    link(v.scalar_tensor_tensor(out=l[6], in0=l[3], scalar=2.0, in1=gsm[:, 1, :].unsqueeze(2).broadcast_to(per),
                                                op0=ALU.is_lt, op1=ALU.mult))
                    link(v.tensor_tensor(l[2], l[2], l[6], ALU.max))
                    dve.wait_ge(gate_exp, 2 * n + b + 1)
                    link(v.tensor_tensor(l[7], l[5], l[2], ALU.mult))
                    link(v.tensor_reduce(gsm[:, 2, :], l[7], AX.X, ALU.add))
                    link(v.reciprocal(gsm[:, 3, :], gsm[:, 2, :]))
                    ins = v.tensor_tensor(rw[:, n, TPB * b:TPB * b + TPB, :], l[7], gsm[:, 3, :].unsqueeze(2).broadcast_to(per), ALU.mult)
                    ins.then_inc(rw_ready, 1)
                    dve.wait_ge(rw_ready, 2 * n + b + 1)

            gate(0)
            for i in range(TILES):
                for e in range(EXPERTS):
                    key = ("qkv", i, e)
                    arrived(dve, key)
                    src, w = PS[:, uses[key][0], 0:3 * HA], rw[:, 0, i, e:e + 1]
                    if e == 0:
                        ins = v.tensor_scalar(QKV[:, i, :], src, w, None, ALU.mult)
                    else:
                        ins = v.scalar_tensor_tensor(out=QKV[:, i, :], in0=src, scalar=w, in1=QKV[:, i, :], op0=ALU.mult, op1=ALU.add)
                    released(ins, key)
                    drained(dve, key)
            for i in range(TILES + 2):
                if i < TILES:
                    arrived(dve, ("s1", i))
                    s = l1s[:, i % 2, :]
                    link(v.tensor_reduce(s[:, 3:4], PS[:, 0:2, :].rearrange("p b s -> p (b s)")[:, 0:P * (i % TPB + 1)],
                                         AX.X, ALU.max, negate=True))
                    v.tensor_scalar(s[:, 0:1], s[:, 3:4], HA ** -0.5, None, ALU.mult).then_inc(bias_ready, 1)
                if 1 <= i <= TILES:
                    t = i - 1
                    s = l1s[:, t % 2, :]
                    arrived(dve, ("a1", t))
                    if t >= 2:
                        drained(dve, ("at", t - 2))
                    drained(dve, ("s1", t))
                    link(v.reciprocal(s[:, 2:3], s[:, 1:2]))
                    ins = v.tensor_scalar(ATT[:, t % 2, :], PS[:, 4, 0:HA], s[:, 2:3], None, ALU.mult)
                    released(ins, ("a1", t))
                if i >= 2:
                    t = i - 2
                    for m in range(4):
                        key = ("o1", t, m)
                        arrived(dve, key)
                        for e in range(2):
                            ins = v.scalar_tensor_tensor(out=H[:, t, :], in0=PS[:, 6 + m % 2, D * e:D * e + D],
                                                         scalar=rw[:, 0, t, 2 * m + e:2 * m + e + 1], in1=H[:, t, :],
                                                         op0=ALU.mult, op1=ALU.add)
                            if e == 0:
                                link(ins)
                        released(ins, key)
                        drained(dve, key)
                    if t % 4 == 3:
                        layernorm(H, NB, batches[t // 4])
            for i in range(TILES):
                ins = v.tensor_tensor(X[:, i, :], X[:, i, :], H[:, i, :], ALU.add)
            link(ins)
            gate(1)
            for i in range(TILES):
                for e in range(EXPERTS):
                    key = ("m2", i, e)
                    arrived(dve, key)
                    ins = v.scalar_tensor_tensor(out=X[:, i, :], in0=PS[:, uses[key][0], 0:D], scalar=rw[:, 1, i, e:e + 1],
                                                 in1=X[:, i, :], op0=ALU.mult, op1=ALU.add)
                    released(ins, key)
                    drained(dve, key)

        @block.gpsimd
        def _(pool):
            g = nc.gpsimd
            links = [0]

            def link(ins):
                links[0] += 1
                ins.then_inc(pool_chain, 1)
                pool.wait_ge(pool_chain, links[0])

            g.memset(ident[:, :], 0.0)
            g.memset(halves[:, :], -0.5)
            g.memset(halfp[:, :], 0.5)
            g.memset(maskq[:, :], 0.0)
            g.memset(maskk[:, :], 0.0)
            g.memset(blockm[:, :], 1.0)
            link(g.memset(lower[:, :, :], 1.0))
            ins = g.memset(ones, 1.0)
            link(g.affine_select(out=ident[:, :], in_=ident[:, :], compare_op=ALU.not_equal, fill=1.0, base=0,
                                 pattern=[[-1, P]], channel_multiplier=1))
            g.affine_select(out=maskq[:, :], in_=maskq[:, :], compare_op=ALU.is_ge, fill=BIG, base=0,
                            pattern=[[-1, P]], channel_multiplier=1)
            g.affine_select(out=maskk[:, :], in_=maskk[:, :], compare_op=ALU.is_ge, fill=BIG, base=0,
                            pattern=[[1, P]], channel_multiplier=-1)
            link(g.affine_select(out=blockm[:, :], in_=blockm[:, :], compare_op=ALU.is_ge, fill=0.0, base=0,
                                 pattern=[[-HD, 8]], channel_multiplier=1))
            g.affine_select(out=blockm[:, :], in_=blockm[:, :], compare_op=ALU.is_ge, fill=0.0, base=HD - 1,
                            pattern=[[HD, 8]], channel_multiplier=-1)
            g.affine_select(out=lower[:, :, :], in_=lower[:, :, :], compare_op=ALU.is_gt, fill=0.0, base=0,
                            pattern=[[1, EXPERTS], [-1, EXPERTS]], channel_multiplier=0)
            g.tensor_copy(identb[:, :], ident[:, :]).then_inc(consts, 1)
            link(g.memset(VEXT[:, :, :, HD:HD + 1], 1.0))
            for s in range(SLOTS):
                link(g.memset(PACKK[s][ROWS:ROWS + 3, :, :], 1.0))
            g.memset(mparts[:, :, :, :], 0.0).then_inc(consts, 1)
            drained(pool, "simsum")
            g.tensor_tensor(siminv[:, :, :].rearrange("p n e -> p (n e)"), siminv[:, :, :].rearrange("p n e -> p (n e)"),
                            halfp[:, :], ALU.pow).then_inc(sim_sum, 1)

            for n, name in enumerate(LNS):
                for k in range(4):
                    pool.wait_ge(var_ready, 4 * n + k + 1)
                    g.tensor_tensor(rstd[:, 4 * k:4 * k + 4], var[:, 4 * k:4 * k + 4], halves[:, 0:4], ALU.pow).then_inc(rstd_ready, 1)
                    if name in AFFINE:
                        w, bias = {"g1": ("g1", "be1"), "g2": ("g2", "be2"), "g3": ("g3", "be3"),
                                   "n1": ("n1w", "n1b"), "n2": ("n2w", "n2b")}[name]
                        dst = NB if name in ("n1", "n2") else H
                        for i in range(4 * k, 4 * k + 4):
                            pool.wait_ge(ln_ready, ln_count(name, i))
                            link(g.tensor_tensor(dst[:, i, :], dst[:, i, :], bc(w), ALU.mult))
                            g.tensor_tensor(dst[:, i, :], dst[:, i, :], bc(bias), ALU.add).then_inc(affine_ready, 1)
                if name in ("n1", "n2"):
                    m = ("n1", "n2").index(name)
                    pool.wait_ge(ss_ready, TILES * (m + 1))
                    g.tensor_tensor(ssr[:, :], ss[:, :], halfp[:, :], ALU.pow).then_inc(ssr_ready, 1)


def _layout(inputs):
    import numpy as np

    f = {k: np.asarray(v) for k, v in inputs.items()}
    r = {"x": f["x"].reshape(N, D), "ctxT": f["ctx_1024"].reshape(B * T, D).T}
    for n in (1, 2):
        for w in "qkv":
            r[f"w{w}{n}"] = f[f"L0_xattn_W{w}{n}"].transpose(1, 0, 2).reshape(D, D)
    for w in "qkv":
        r[f"w{w}3"] = f[f"L1_xattn_W{w}"].T
    r |= {"bq3": f["L1_xattn_bq"], "bk3": f["L1_xattn_bk"], "bf1": f["L0_xattn_bf1"], "wf1": f["L0_xattn_Wf1"],
          "wf2": f["L0_xattn_Wf2"], "wt": f["L0_ffn_W"].T, "daux": f["L0_ffn_down_aux"], "upT": f["L0_ffn_up_aux"].T,
          "ldT": f["L0_ffn_lora_down"].T, "luT": f["L0_ffn_lora_up"].T}
    r["wqkv"] = np.concatenate([f[f"L1_ffn_{w}_proj"].transpose(1, 0, 2) for w in "qkv"], axis=2)
    r |= {"wo": f["L1_ffn_o_proj"], "w1": f["L1_ffn_w1"].transpose(1, 0, 2), "w2": f["L1_ffn_w2"].reshape(EXPERTS * D, D), "sim1": f["L1_ffn_smha_sim"],
          "sim2": f["L1_ffn_moe_sim"], "gates1": f["L1_ffn_smha_gates"], "gates2": f["L1_ffn_moe_gates"],
          "mask_st": f["mask_1x1xSxS2_ik0"].reshape(S, T), "mask_bt": f["mask_Bx1x1xS2_ik0"].reshape(B, T)}
    for name in ("bq3", "bk3", "bf1"):
        r[name] = r[name].reshape(-1, P).T
    rows = {"bv1": f["L0_xattn_bv1"], "bv2": f["L0_xattn_bv2"], "g1": f["L0_xattn_g1"], "be1": f["L0_xattn_be1"],
            "g2": f["L0_xattn_g2"], "be2": f["L0_xattn_be2"], "g3": f["L0_xattn_g3"], "be3": f["L0_xattn_be3"],
            "bf2": f["L0_xattn_bf2"], "lb": f["L0_ffn_b"], "bv3": f["L1_xattn_bv"], "n1w": f["L1_ffn_ln1_w"],
            "n1b": f["L1_ffn_ln1_b"], "n2w": f["L1_ffn_ln2_w"], "n2b": f["L1_ffn_ln2_b"]}
    r["bcast"] = np.stack([rows[name].reshape(D) for name in BCAST])
    return {k: np.ascontiguousarray(v) for k, v in r.items()}


def kernel(**inputs):
    import concourse.bacc as bacc
    from concourse.bass_utils import run_bass_kernel_spmd

    arrays = _layout(inputs)
    nc = bacc.Bacc("TRN2", target_bir_lowering=False, num_devices=1)
    args = {k: nc.dram_tensor(f"in_{k}", v.shape, mybir.dt.from_np(v.dtype), kind="ExternalInput").ap()
            for k, v in arrays.items()}
    out = nc.dram_tensor("out_x", (N, D), F32, kind="ExternalOutput").ap()
    build(nc, args, out)
    r = run_bass_kernel_spmd(nc, [{f"in_{k}": v for k, v in arrays.items()}], core_ids=[0])
    return r.results[0]["out_x"].reshape(B, S, D)
```

```python
from contextlib import ExitStack

import concourse.bass as bass
from concourse import mybir

F32 = mybir.dt.float32
BF16 = mybir.dt.bfloat16
I32 = mybir.dt.int32
ALU = mybir.AluOpType
ACT = mybir.ActivationFunctionType
AX = mybir.AxisListType

P = 128
B, S, D, T = 2, 1024, 256, 77
N = B * S
TILES = N // P
TPB = S // P
HEADS, HD = 16, 16
KC = D // P
FF = 1024
FCH = FF // P
EXPERTS = 8
HA = 128
EPS = 1e-5
BIG = -3.0e38
MASKED = -1.0e9
GRP = 4
GROUPS = B * HEADS // GRP
SLOTS = 3
VW = HD + 1
ROWS = 6 * HD
QPART = [0, 1, 2, 0, 1, 0]
KPART = [0, 0, 0, 1, 1, 2]
UNITS = 2 * TILES
HH = HEADS // 2
BCAST = ["bv1", "bv2", "g1", "be1", "g2", "be2", "g3", "be3", "bf2", "lb", "bv3",
         "n1w", "n1b", "n2w", "n2b"]


STEPS = [(tt, c) for tt in range(TPB) for c in range(2) if tt < 4 * (c + 1)]


def norm_order():
    for name in ("in", "g1", "g2"):
        for k in range(4):
            yield name, k
    for s in range(1, 6):
        if s >= 2:
            yield "xat", s - 2
        if s <= 4:
            yield "g3", s - 1
            yield "lin", s - 1
    for name in ("ffn", "n1", "n2"):
        for k in range(4):
            yield name, k


NORMS = list(norm_order())


def attention_plan():
    for n in range(GROUPS + 1):
        maxima = [(j, st) for j in range(GRP) for st in range(TPB)] if n < GROUPS else []
        units = len(STEPS) * GRP
        done = 0
        for u in range(units):
            if n > 0:
                tt, c = STEPS[u // GRP]
                yield "score", n - 1, tt, c, u % GRP
            if u == 1 and n > 1:
                yield "evac", n - 2
            if u == 7 and n > 1:
                yield "out", n - 2
            if u == 20 and n in (5, 6):
                yield "norm", n - 5
            if u == 20 and n in (6, 7):
                yield "turn", n - 6
            while done < len(maxima) and done * (units - 10) <= u * len(maxima):
                yield ("max", n) + maxima[done]
                done += 1
            if u == units - 6 and n < GROUPS:
                yield "neg", n
            if n > 0 and u % GRP == 1 and u > GRP:
                yield ("pv", n - 1) + STEPS[u // GRP - 1]
        if n > 0:
            yield ("pv", n - 1) + STEPS[-1]
    yield "evac", GROUPS - 1
    yield "out", GROUPS - 1


def build(nc, a, out, stop=None):
    ctx = ExitStack()
    with ctx:
        def sb(name, shape, dt):
            return ctx.enter_context(nc.sbuf_tensor(name, shape, dt))

        def sem(name):
            return ctx.enter_context(nc.semaphore(name))

        X = sb("X", [P, TILES, D], F32)
        H = sb("H", [P, TILES, D], F32)
        TR = sb("TR", [P, KC, N], F32)
        W6 = sb("W6", [P, 6 * KC * D], F32)
        BC = sb("BC", [P, len(BCAST), D], F32)
        ARENA = sb("ARENA", [P, 31696], F32)
        PS = ctx.enter_context(nc.psum_tensor("PS", [P, 8, 512], F32))

        def bc(name):
            return BC[:, BCAST.index(name), :]

        def region(lo, n, pattern=None, parts=P, **kw):
            v = ARENA[0:parts, lo:lo + n]
            return v.rearrange(pattern, **kw) if pattern else v

        def w6(n):
            return W6[:, n * KC * D:(n + 1) * KC * D].rearrange("p (k f) -> p k f", k=KC)

        ident = sb("ident", [P, P], F32)
        identb = sb("identb", [P, P], BF16)
        maskq = sb("maskq", [P, P], BF16)
        maskk = sb("maskk", [P, P], BF16)
        blockm = sb("blockm", [P, 8], F32)
        lower = sb("lower", [P, EXPERTS, EXPERTS], F32)
        halves = sb("halves", [P, TILES], F32)
        halfp = sb("halfp", [P, TILES], F32)
        stats = sb("stats", [P, TILES, 6], F32)
        mv = sb("mv", [P, TILES, 2], F32)
        var = sb("var", [P, TILES], F32)
        rstd = sb("rstd", [P, TILES], F32)
        tmp = sb("tmp", [P, 2, D], F32)
        ctxT = sb("ctxT", [P, KC, B * T], F32)
        bf1c = sb("bf1c", [P, FCH], F32)
        bq3c = sb("bq3c", [P, KC], F32)
        bk3c = sb("bk3c", [P, KC], F32)
        mx = sb("mx", [P, 2, HEADS], F32)
        sims = sb("sims", [P, 2, KC, EXPERTS], F32)
        simsq = sb("simsq", [P, 2, KC, EXPERTS], F32)
        siminv = sb("siminv", [P, 2, EXPERTS], F32)
        gates = sb("gates", [P, 2, EXPERTS], F32)
        ss = sb("ss", [P, TILES], F32)
        ssr = sb("ssr", [P, TILES], F32)
        NL = TILES * EXPERTS
        gsm = sb("gsm", [P, 4, TILES], F32)
        rw = sb("rw", [P, 2, TILES, EXPERTS], F32)
        l1s = sb("l1s", [P, 2, 4], F32)

        PACKQ = [region(2048 * s, 2048).bitcast(BF16).rearrange("p (j s) -> p j s", j=GRP)
                 for s in range(SLOTS)]
        PACKK = [region(6144 + 2048 * s, 2048).bitcast(BF16).rearrange("p (j s) -> p j s", j=GRP)
                 for s in range(SLOTS)]
        PARTS = [region(12288 + 1536 * s, 1536).bitcast(BF16).rearrange("p (c s) -> p c s", c=3)
                 for s in range(4)]
        SA = region(12288, 4096, "p (i f) -> p i f", i=TILES)
        PROB = [region(18432 + 512 * s, 512) for s in range(8)]
        VEXT = region(22528, TILES * HEADS * VW, "p (i h e) -> p i h e", i=TILES, h=HEADS)
        OTS = region(26880, 1024)
        REST = [region(27904 + 512 * s, 512) for s in range(3)]
        ones = region(30000, P)
        mrest = region(30128, P, parts=GRP * TPB)
        mparts = region(30256, 3 * P, parts=GRP * TPB).bitcast(BF16).rearrange("p (u c s) -> p u c s", u=2, c=3)
        negm = region(30640, 2 * GRP * TPB, "p (u m) -> p u m", u=2)
        rsum = region(30704, GRP * TPB)
        QT = region(0, 4096, "p (g s) -> p g s", g=2)
        KBD = region(4096, B * 2 * 8 * T, "p (b g h t) -> p b g h t", b=B, g=2, h=8)
        VX = region(6560, B * HEADS * VW, "p (b h e) -> p b h e", parts=T, b=B, h=HEADS)
        EX = [region(7104 + HH * T * s, HH * T, "p (h t) -> p h t", h=HH) for s in range(4)]
        PTS = [region(9568 + 1024 * s, 1024, "p (h s) -> p h s", parts=T, h=HH) for s in range(4)]
        KTX = region(13664, 2 * B * T, "p (g t) -> p g t", g=2)
        W3 = region(13972, 1024, "p (w k f) -> p w k f", w=2, k=KC)
        MASKS = region(9568, 616).bitcast(I32).rearrange("p (i t) -> p i t", i=TPB)
        MASKB = region(10184, 154).bitcast(I32).rearrange("p (b t) -> p b t", b=B)
        KEEP = W6[:, 0:TILES * T].bitcast(I32).rearrange("p (i t) -> p i t", i=TILES)
        KEEPF = W6[:, TILES * T:2 * TILES * T].rearrange("p (i t) -> p i t", i=TILES)
        HT = [region(23504 + 4096 * s, 4096, "p (f s) -> p f s", f=FCH) for s in range(2)]
        WF1 = region(16384, 2048, "p (k f) -> p k f", k=KC)
        WF2 = region(18432, 2048, "p (f d) -> p f d", f=FCH)
        WEFF = region(20480, 512, "p (k f) -> p k f", k=KC)
        DAUX = region(20992, 256, parts=100)
        LD1 = region(21248, 256, parts=4)
        LD2 = region(21504, 256, parts=50)
        UPT = region(21760, 256, parts=50)
        LDT = region(22016, 4, parts=100)
        LUT = region(22020, 50, parts=4)
        WO = region(21456, 2048, "p (e f) -> p e f", e=EXPERTS)
        WQKV = region(15312, 6144, "p (k e f) -> p k e f", k=KC, e=EXPERTS)
        W1 = region(23504, 4096, "p (k e f) -> p k e f", k=KC, e=EXPERTS)
        W2 = region(27600, 4096, "p (e k f) -> p e k f", e=EXPERTS, k=KC)
        QKV = region(0, 6144, "p (i f) -> p i f", i=TILES)
        QK1 = region(6144, 4096, "p (w s) -> p w s", w=2)
        NB = region(10240, 4096, "p (i f) -> p i f", i=TILES)
        P1 = [W6[:, 1024 * s:1024 * (s + 1)] for s in range(2)]
        PT1 = W6[:, 2048:3072].rearrange("p (t s) -> p t s", t=TPB)
        ATT = region(14336, 2 * HA, "p (u f) -> p u f", u=2)
        ATTT = region(14592, 2 * HA, "p (u f) -> p u f", u=2)
        SQ = region(6144, 2 * D, "p (u f) -> p u f", u=2)
        RANK = W6[:, 0:2 * NL * EXPERTS].rearrange("p (u i e j) -> p u i e j", u=2, i=TILES, e=EXPERTS)
        LG = W6[:, 2 * NL * EXPERTS:(2 * EXPERTS + 8) * NL].rearrange("p (u n) -> p u n", u=8)
        INT = [region(8192 * s if s else 0, 8192, "p (c s) -> p c s", c=16) for s in range(2)]

        scratch = nc.dram_tensor("qk_parts", [B, 2, D, 3, S], BF16, kind="Internal").ap()

        bank_full = [sem(f"bank_full{k}") for k in range(8)]
        bank_free = [sem(f"bank_free{k}") for k in range(8)]
        consts = sem("consts")
        pool_chain = sem("pool_chain")
        dve_chain = sem("dve_chain")
        x_in = [sem(f"x_in{k}") for k in range(4)]
        ln_ready = sem("ln_ready")
        var_ready = sem("var_ready")
        rstd_ready = sem("rstd_ready")
        fill_ready = sem("fill_ready")
        hi_ready = sem("hi_ready")
        mid_ready = sem("mid_ready")
        parts_ready = sem("parts_ready")
        parts_out = [sem(f"parts_out{k}") for k in range(8)]
        pack_in = [sem(f"pack_in{k}") for k in range(SLOTS)]
        mparts_ready = sem("mparts_ready")
        mrows_in = [sem(f"mrows_in{k}") for k in range(SLOTS)]
        pv_done = sem("pv_done")
        sa_used = sem("sa_used")
        kv_ready = sem("kv_ready")
        shift_ready = sem("shift_ready")
        ex_ready = sem("ex_ready")
        sim_ready = sem("sim_ready")
        sim_sum = sem("sim_sum")
        sig_ready = sem("sig_ready")
        ss_ready = sem("ss_ready")
        ssr_ready = sem("ssr_ready")
        gate_in = sem("gate_in")
        gate_exp = sem("gate_exp")
        rw_ready = sem("rw_ready")
        bias_ready = sem("bias_ready")
        stored = sem("stored")

        loads = {"wq1": 1, "wk1": 1, "wv1": 1, "ctx": 1, "bc": 1, "wq2": 1, "wk2": 1, "wv2": 1, "bf1": 1, "bq3": 1,
                 "bk3": 1, "sims": 2, "gates": 2, "wf1": 1, "wf2": 1, "wt": 1, "lora": 4, "w1": 1, "w2": 1,
                 "wq3": 1, "wk3": 1, "wv3": 1, "wqkv": 1, "wo": 1, "masks": 2}
        load_sem = {name: sem("ld_" + name) for name in loads}

        def load(eng, name, dst, src):
            eng.dma_start(dst, src).then_inc(load_sem[name], 16)

        def loaded(eng, name):
            eng.wait_ge(load_sem[name], 16 * loads[name])

        last_use = {}
        uses = {}
        full_count = [0] * 8
        free_count = [0] * 8

        def claim(key, banks, readers=1, signals=1):
            waits = {}
            for k in banks:
                if k in last_use:
                    first, count = last_use[k]
                    waits[first] = max(waits.get(first, 0), count)
            for first, count in waits.items():
                nc.tensor.wait_ge(bank_free[first], count)
            full_count[banks[0]] += signals
            free_count[banks[0]] += readers
            for k in banks:
                last_use[k] = (banks[0], free_count[banks[0]])
            uses[key] = (banks[0], full_count[banks[0]], free_count[banks[0]])

        def filled(ins, key):
            ins.then_inc(bank_full[uses[key][0]], 1)

        def arrived(eng, key):
            eng.wait_ge(bank_full[uses[key][0]], uses[key][1])

        def released(ins, key):
            ins.then_inc(bank_free[uses[key][0]], 1)

        def drained(eng, key):
            eng.wait_ge(bank_free[uses[key][0]], uses[key][2])

        def ln_count(name, i):
            return 4 * NORMS.index((name, i // 4)) + i % 4 + 1

        block = ctx.enter_context(nc.Block())

        @block.tensor
        def _(pe):
            def mm(o, lhsT, rhs, start=True, stop=True, **kw):
                return nc.tensor.matmul(o, lhsT, rhs, start=start, stop=stop, **kw)

            def turn(name, norm, src, c):
                for i in range(4 * c, 4 * c + 4):
                    claim((name, i), [i % 2])
                    pe.wait_ge(ln_ready, ln_count(norm, i))
                    for k in range(KC):
                        ins = nc.tensor.transpose(PS[:, i % 2, P * k:P * k + P], src[:, i, P * k:P * k + P], ident[:, :])
                    filled(ins, (name, i))

            def turned(name, c):
                for i in (4 * c + 2, 4 * c + 3):
                    drained(pe, (name, i))

            def qk_transposes(i):
                claim(("qk1", i), [2 + i % 2])
                drained(pe, ("qkv", i, EXPERTS - 1))
                for w in range(2):
                    ins = nc.tensor.transpose(PS[:, 2 + i % 2, P * w:P * w + P], QKV[:, i, P * w:P * w + P], ident[:, :])
                filled(ins, ("qk1", i))

            pe.wait_ge(consts, 1)
            pe.wait_ge(sim_ready, 1)
            claim("simsum", [7])
            for n in range(2):
                for k in range(KC):
                    ins = mm(PS[:, 7, EXPERTS * n:EXPERTS * n + EXPERTS], ones, simsq[:, n, k, :],
                             start=k == 0, stop=k == KC - 1)
            filled(ins, "simsum")

            bank = 2
            for b in range(B):
                for c in (2 * b, 2 * b + 1):
                    turn("t_in", "in", H, c)
                for c in (2 * b, 2 * b + 1):
                    turned("t_in", c)
                for g in range(2):
                    for w in range(2):
                        loaded(pe, ("wq1", "wk1")[w])
                        for c in range(2):
                            key = ("qk", b, g, w, c)
                            claim(key, [bank])
                            for k in range(KC):
                                ins = mm(PS[:, bank, :], w6(w)[:, k, P * g:P * g + P],
                                         TR[:, k, S * b + 512 * c:S * b + 512 * c + 512], start=k == 0, stop=k == KC - 1)
                            filled(ins, key)
                            bank = 2 + (bank - 1) % 6
                loaded(pe, "wv1")
                for i in range(TPB * b, TPB * b + TPB):
                    claim(("v1", i), [bank])
                    for k in range(KC):
                        ins = mm(PS[:, bank, 0:D], TR[:, k, P * i:P * i + P], w6(2)[:, k, :], start=k == 0, stop=k == KC - 1)
                    filled(ins, ("v1", i))
                    bank = 2 + (bank - 1) % 6

            wide = 0
            narrow = 0
            drained(pe, ("v1", TILES - 1))
            pe.wait_ge(consts, 2)
            for op, n, *at in attention_plan():
                slot, b = n % SLOTS, n // 4
                if op == "max":
                    j, st = at
                    if (j, st) == (0, 0):
                        pe.wait_ge(pack_in[slot], 12 * 16 * (n // SLOTS + 1))
                    claim(("max", n, j, st), [2 * wide, 2 * wide + 1])
                    for c in range(st // 4 + 1):
                        cols = min(512, P * (st + 1) - 512 * c)
                        diag = c == st // 4
                        ins = mm(PS[:, 2 * wide + c, 0:cols], PACKQ[slot][0:ROWS, j, P * st:P * st + P],
                                 PACKK[slot][0:ROWS, j, 512 * c:512 * c + cols], stop=not diag)
                        if diag:
                            ins = mm(PS[:, 2 * wide + c, cols - P:cols], identb[:, :], maskq[:, :], start=False)
                    filled(ins, ("max", n, j, st))
                    wide = 1 - wide
                elif op == "neg":
                    claim(("neg", n), [2 * wide, 2 * wide + 1])
                    drained(pe, ("max", n, GRP - 1, TPB - 1))
                    filled(nc.tensor.transpose(PS[0:GRP * TPB, 2 * wide, 0:P], negm[:, n % 2, :], ident[:, :]), ("neg", n))
                    wide = 1 - wide
                elif op == "score":
                    tt, c, j = at
                    if (tt, c, j) == (0, 0, 0):
                        pe.wait_ge(mrows_in[slot], 3 * 16 * (n // SLOTS + 1))
                    lo = max(P * tt, 512 * c)
                    w = 512 * c + 512 - lo
                    diag = lo == P * tt
                    bank = 4 + narrow
                    claim(("score", n, tt, c, j), [bank])
                    ins = mm(PS[:, bank, 0:w], PACKK[slot][0:ROWS + 3, j, P * tt:P * tt + P],
                             PACKQ[slot][0:ROWS + 3, j, lo:lo + w], stop=not diag)
                    if diag:
                        ins = mm(PS[:, bank, 0:P], identb[:, :], maskk[:, :], start=False)
                    filled(ins, ("score", n, tt, c, j))
                    narrow = 1 - narrow
                elif op == "pv":
                    tt, c = at
                    if (tt, c) == (0, 0):
                        claim(("values", n), [6, 7], signals=0)
                    lo = max(P * tt, 512 * c)
                    w = 512 * c + 512 - lo
                    drained(pe, ("score", n, tt, c, GRP - 1))
                    for j in range(GRP):
                        ins = mm(PS[32 * j:32 * j + VW, 6 + c, lo - 512 * c:512],
                                 VEXT[:, TPB * b + tt, GRP * (n % 4) + j, :],
                                 PROB[GRP * (STEPS.index((tt, c)) % 2) + j][:, 0:w], start=tt == 0, stop=tt == 4 * c + 3)
                    ins.then_inc(pv_done, 1)
                elif op == "turn":
                    pe.wait_ge(ln_ready, ln_count("g1", 4 * n + 3))
                    claim(("turn", n), [2 * wide, 2 * wide + 1])
                    for i in range(4):
                        for k in range(KC):
                            col = P * (2 * (i % 2) + k)
                            ins = nc.tensor.transpose(PS[:, 2 * wide + i // 2, col:col + P],
                                                      H[:, 4 * n + i, P * k:P * k + P], ident[:, :])
                    filled(ins, ("turn", n))
                    wide = 1 - wide
                elif op == "out":
                    drained(pe, ("values", n))
                    claim(("out", n), [2 * wide, 2 * wide + 1])
                    for st in range(TPB):
                        ins = nc.tensor.transpose(PS[:, 2 * wide + st // 4, P * (st % 4):P * (st % 4) + P],
                                                  OTS[:, P * st:P * st + P], ident[:, :])
                    filled(ins, ("out", n))
                    wide = 1 - wide

            def context(layer, wk, wv):
                pe.wait_ge(sa_used, 4)
                loaded(pe, wk[1])
                loaded(pe, "ctx")
                for g in range(2):
                    claim(("kx", layer, g), [6 + g])
                    for k in range(KC):
                        ins = mm(PS[:, 6 + g, 0:B * T], wk[0][:, k, P * g:P * g + P], ctxT[:, k, :], start=k == 0, stop=k == KC - 1)
                    filled(ins, ("kx", layer, g))
                loaded(pe, wv[1])
                for b in range(B):
                    claim(("vx", layer, b), [6 + b])
                    for k in range(KC):
                        ins = mm(PS[0:T, 6 + b, 0:D], ctxT[:, k, T * b:T * b + T], wv[0][:, k, :], start=k == 0, stop=k == KC - 1)
                    filled(ins, ("vx", layer, b))

            def queries(layer, wq, c):
                loaded(pe, wq[1])
                for g in range(2):
                    key = ("q", layer, c, g)
                    claim(key, [4 + g])
                    for k in range(KC):
                        ins = mm(PS[:, 4 + g, :], wq[0][:, k, P * g:P * g + P],
                                 TR[:, k, 512 * c:512 * c + 512], start=k == 0, stop=k == KC - 1)
                    filled(ins, key)

            def cross(layer):
                pe.wait_ge(kv_ready, 2 * B * (layer + 1))
                for b in range(B):
                    drained(pe, ("vx", layer, b))

                def scores(u):
                    i, g = u // 2, u % 2
                    for m in range(2):
                        drained(pe, ("q", layer, i // 4, m))
                    claim(("sx", layer, u), [2 * g, 2 * g + 1])
                    for m in range(2):
                        ins = mm(PS[:, 2 * g + m, 0:4 * T], QT[:, g, P * i:P * i + P], KBD[:, i // TPB, g, 4 * m:4 * m + 4, :])
                    filled(ins, ("sx", layer, u))

                def turn_probs(u):
                    pe.wait_ge(ex_ready, UNITS * layer + u + 1)
                    for m in range(2):
                        claim(("px", layer, u, m), [4 + m])
                        for h in range(4):
                            ins = nc.tensor.transpose(PS[0:T, 4 + m, P * h:P * h + P], EX[u % 4][:, 4 * m + h, :], ident[:, :])
                        filled(ins, ("px", layer, u, m))

                def values(u):
                    t, g = u // 2, u % 2
                    if g == 0:
                        claim(("ox", layer, t), [6 + t % 2])
                    drained(pe, ("px", layer, u, 0))
                    drained(pe, ("px", layer, u, 1))
                    for h in range(HH):
                        col = VW * (HH * g + h)
                        ins = mm(PS[:, 6 + t % 2, col:col + VW], PTS[u % 4][:, h, :], VX[:, t // TPB, HH * g + h, :])
                    if g == 1:
                        filled(ins, ("ox", layer, t))

                for u in range(-2, UNITS + 1):
                    if layer == 0 and (u + 2) % 8 == 0 and u + 2 < UNITS:
                        c = (u + 2) // 8
                        if c < 2:
                            drained(pe, ("turn", c))
                        else:
                            turn("t_g1", "g1", H, c)
                            turned("t_g1", c)
                        queries(0, (w6(3), "wq2"), c)
                    if u + 2 < UNITS:
                        scores(u + 2)
                    if 0 <= u < UNITS:
                        turn_probs(u)
                    if u >= 1:
                        values(u - 1)

            context(0, (w6(4), "wk2"), (w6(5), "wv2"))
            cross(0)

            loaded(pe, "lora")
            claim("l1", [2])
            filled(mm(PS[0:4, 2, 0:D], LDT, DAUX), "l1")
            drained(pe, "l1")
            claim("l2", [3])
            filled(mm(PS[0:50, 3, 0:D], LUT, LD1), "l2")
            drained(pe, "l2")
            claim("l3", [4])
            for k in range(KC):
                ins = mm(PS[:, 4, D * k:D * k + D], LD2[:, P * k:P * k + P], UPT)
            filled(ins, "l3")

            loaded(pe, "wf1")
            loaded(pe, "wf2")
            for s in range(7):
                if s < 4:
                    turn("t_g2", "g2", H, s)
                    turned("t_g2", s)
                    for f in range(FCH):
                        key = ("f1", s, f)
                        claim(key, [2 + f % 4])
                        for k in range(KC):
                            ins = mm(PS[:, 2 + f % 4, :], WF1[:, k, P * f:P * f + P], TR[:, k, 512 * s:512 * s + 512],
                                     start=k == 0, stop=k == KC - 1)
                        filled(ins, key)
                if 2 <= s < 6:
                    turn("t_lin", "lin", H, s - 2)
                    turned("t_lin", s - 2)
                    drained(pe, "l3")
                    for i in range(4 * s - 8, 4 * s - 4):
                        claim(("lin", i), [2 + i % 4])
                        for k in range(KC):
                            ins = mm(PS[:, 2 + i % 4, 0:D], TR[:, k, P * i:P * i + P], WEFF[:, k, :], start=k == 0, stop=k == KC - 1)
                        filled(ins, ("lin", i))
                if 1 <= s < 5:
                    for f in range(FCH - 4, FCH):
                        drained(pe, ("f1", s - 1, f))
                    for i in range(4 * s - 4, 4 * s):
                        claim(("f2", i), [6 + i % 2])
                        for f in range(FCH):
                            ins = mm(PS[:, 6 + i % 2, 0:D], HT[(s - 1) % 2][:, f, P * (i % 4):P * (i % 4) + P], WF2[:, f, :],
                                     start=f == 0, stop=f == FCH - 1)
                        filled(ins, ("f2", i))
                if s >= 3:
                    turn("t_xat", "xat", H, s - 3)
                    turned("t_xat", s - 3)
                    queries(1, (w6(5), "wq3"), s - 3)
                if s == 5:
                    context(1, (W3[:, 0, :, :], "wk3"), (W3[:, 1, :, :], "wv3"))
            cross(1)

            def logits(n):
                claim(("lg", n), [2])
                for i in range(TILES):
                    for k in range(KC):
                        ins = mm(PS[:, 2, EXPERTS * i:EXPERTS * i + EXPERTS], TR[:, k, P * i:P * i + P], sims[:, n, k, :],
                                 start=k == 0, stop=k == KC - 1)
                filled(ins, ("lg", n))

            for c in range(4):
                turn("t_n1", "n1", NB, c)
            turned("t_n1", 3)
            logits(0)
            loaded(pe, "wqkv")
            for i in range(TILES):
                for e in range(EXPERTS):
                    bank = 4 + (EXPERTS * i + e) % 4
                    key = ("qkv", i, e)
                    claim(key, [bank])
                    for k in range(KC):
                        ins = mm(PS[:, bank, 0:3 * HA], TR[:, k, P * i:P * i + P], WQKV[:, k, e, :], start=k == 0, stop=k == KC - 1)
                    filled(ins, key)
                if i > 0:
                    qk_transposes(i - 1)
            qk_transposes(TILES - 1)
            loaded(pe, "wo")
            def row_scores(i):
                b, st = i // TPB, i % TPB
                drained(pe, ("qk1", i))
                claim(("s1", i), [0, 1])
                for c in range(st // 4 + 1):
                    cols = min(512, P * (st + 1) - 512 * c)
                    diag = c == st // 4
                    ins = mm(PS[:, c, 0:cols], QK1[:, 0, P * i:P * i + P],
                             QK1[:, 1, S * b + 512 * c:S * b + 512 * c + cols], stop=not diag)
                    if diag:
                        ins = mm(PS[:, c, cols - P:cols], identb[:, :], maskq[:, :], start=False)
                filled(ins, ("s1", i))

            row_scores(0)
            for i in range(TILES + 1):
                if i + 1 < TILES:
                    row_scores(i + 1)
                if i > 0:
                    t = i - 1
                    drained(pe, ("a1", t))
                    claim(("at", t), [5])
                    filled(nc.tensor.transpose(PS[:, 5, 0:HA], ATT[:, t % 2, :], ident[:, :]), ("at", t))
                if i < TILES:
                    drained(pe, ("s1", i))
                    claim(("p1", i), [2, 3])
                    for tt in range(i % TPB + 1):
                        ins = nc.tensor.transpose(PS[:, 2 + tt // 4, P * (tt % 4):P * (tt % 4) + P],
                                                  P1[i % 2][:, P * tt:P * tt + P], ident[:, :])
                    filled(ins, ("p1", i))
                if i > 0:
                    drained(pe, ("at", t))
                    for m in range(4):
                        claim(("o1", t, m), [6 + m % 2])
                        ins = mm(PS[:, 6 + m % 2, :], ATTT[:, t % 2, :], WO[:, 2 * m:2 * m + 2, :])
                        filled(ins, ("o1", t, m))
                if i < TILES:
                    claim(("a1", i), [4])
                    drained(pe, ("p1", i))
                    for tt in range(i % TPB + 1):
                        ins = mm(PS[:, 4, 0:HA], PT1[:, tt, :], QKV[:, TPB * (i // TPB) + tt, 2 * HA:3 * HA],
                                 start=tt == 0, stop=tt == i % TPB)
                    filled(ins, ("a1", i))

            for c in range(4):
                turn("t_n2", "n2", NB, c)
            turned("t_n2", 3)
            logits(1)
            loaded(pe, "w1")
            loaded(pe, "w2")
            for c in range(5):
                if c < 4:
                    for m in range(2 * EXPERTS):
                        e, ic = m // 2, m % 2
                        claim(("m1", c, m), [2 + m % 4])
                        for k in range(KC):
                            ins = mm(PS[:, 2 + m % 4, :], W1[:, k, e, P * ic:P * ic + P], TR[:, k, 512 * c:512 * c + 512],
                                     start=k == 0, stop=k == KC - 1)
                        filled(ins, ("m1", c, m))
                if c > 0:
                    for m in range(2 * EXPERTS - 4, 2 * EXPERTS):
                        drained(pe, ("m1", c - 1, m))
                    for i in range(4 * c - 4, 4 * c):
                        for e in range(EXPERTS):
                            bank = (0, 1, 6, 7)[e % 4]
                            claim(("m2", i, e), [bank])
                            for k in range(KC):
                                ins = mm(PS[:, bank, 0:D], INT[(c - 1) % 2][:, 2 * e + k, P * (i % 4):P * (i % 4) + P], W2[:, e, k, :],
                                         start=k == 0, stop=k == KC - 1)
                            filled(ins, ("m2", i, e))

        @block.sync
        def _(sp):
            def wload(name, dst, key, pattern="(k p) f -> p k f", **kw):
                load(sp, name, dst, a[key].rearrange(pattern, **kw))

            xd = a["x"].rearrange("(i p) d -> p i d", p=P)
            for k in range(4):
                sp.dma_start(X[:, 4 * k:4 * k + 4, :], xd[:, 4 * k:4 * k + 4, :]).then_inc(x_in[k], 16)
                if k == 0:
                    wload("wq1", w6(0), "wq1", p=P)
                    wload("wk1", w6(1), "wk1", p=P)
            load(sp, "ctx", ctxT[:, :, :], a["ctxT"].rearrange("(k p) t -> p k t", p=P))
            wload("wv1", w6(2), "wv1", p=P)
            load(sp, "bc", BC[:, :, :], a["bcast"].rearrange("(o n) d -> o n d", o=1).broadcast_to([P, len(BCAST), D]))
            for n, name in enumerate(("wq2", "wk2", "wv2")):
                wload(name, w6(3 + n), name, p=P)
            load(sp, "bf1", bf1c[:, :], a["bf1"])
            load(sp, "bq3", bq3c[:, :], a["bq3"])
            load(sp, "bk3", bk3c[:, :], a["bk3"])
            for n, name in enumerate(("sim1", "sim2")):
                load(sp, "sims", sims[:, n, :, :], a[name].rearrange("(k p) e -> p k e", p=P))
            for n, name in enumerate(("gates1", "gates2")):
                load(sp, "gates", gates[:, n, :],
                     a[name].rearrange("(o e) -> o e", o=1).broadcast_to([P, EXPERTS]))

            def load_pack(n):
                b, h0 = n // 4, GRP * (n % 4)
                for w, packs, order in ((0, PACKQ, QPART), (1, PACKK, KPART)):
                    src = scratch[b, w].rearrange("(h e) c s -> c e h s", h=HEADS)
                    for r, part in enumerate(order):
                        sp.dma_start(packs[n % SLOTS][HD * r:HD * r + HD, :, :],
                                     src[part, :, h0:h0 + GRP, :]).then_inc(pack_in[n % SLOTS], 16)

            for u in range(8):
                b, g, w = u // 4, u // 2 % 2, u % 2
                sp.wait_ge(parts_ready, 2 * (u + 1))
                sp.dma_start(scratch[b, w, P * g:P * g + P, :, :], PARTS[u % 4]).then_inc(parts_out[u], 16)
                if u == 1:
                    for v in (0, 1):
                        sp.wait_ge(parts_out[v], 16)
                    load_pack(0)
                    load_pack(1)
            for v in range(2, 8):
                sp.wait_ge(parts_out[v], 16)
            load_pack(2)

            for n in range(GROUPS):
                sp.wait_ge(mparts_ready, n + 1)
                for r in range(3):
                    sp.dma_start(PACKQ[n % SLOTS][ROWS + r:ROWS + r + 1, :, :].rearrange("o j (t s) -> o (j t) s", s=P),
                                 mparts[:, n % 2, r, :]).then_inc(mrows_in[n % SLOTS], 16)
                if 1 <= n < GROUPS - 2:
                    arrived(sp, ("score", n - 1, TPB - 1, 1, GRP - 1))
                    load_pack(n + 2)

            sp.wait_ge(sa_used, 4)
            load(sp, "lora", DAUX, a["daux"])
            load(sp, "lora", UPT, a["upT"])
            load(sp, "lora", LDT, a["ldT"])
            load(sp, "lora", LUT, a["luT"])
            wload("wt", WEFF, "wt", p=P)
            wload("wf1", WF1, "wf1", p=P)
            wload("wf2", WF2, "wf2", "(f p) d -> p f d", p=P)
            for n, name in enumerate(("wk3", "wv3")):
                wload(name, W3[:, n, :, :], name, p=P)
            arrived(sp, ("vx", 0, B - 1))
            wload("wq3", w6(5), "wq3", p=P)
            arrived(sp, ("ox", 0, TILES - 1))
            load(sp, "masks", MASKS, a["mask_st"].rearrange("(i p) t -> p i t", p=P))
            load(sp, "masks", MASKB,
                 a["mask_bt"].rearrange("(o b) t -> o b t", o=1).broadcast_to([P, B, T]))
            drained(sp, ("lin", TILES - 1))
            load(sp, "wqkv", WQKV, a["wqkv"].rearrange("(k p) e f -> p k e f", p=P))
            wload("wo", WO, "wo", "e p f -> p e f")
            load(sp, "w1", W1, a["w1"].rearrange("(k p) e f -> p k e f", p=P))
            load(sp, "w2", W2, a["w2"].rearrange("(m p) f -> p m f", p=P).rearrange("p (e k) f -> p e k f", k=KC))

            od = out.rearrange("(i p) d -> p i d", p=P)
            for c in range(8):
                drained(sp, ("m2", 2 * c + 1, EXPERTS - 1))
                sp.dma_start(od[:, 2 * c:2 * c + 2, :], X[:, 2 * c:2 * c + 2, :]).then_inc(stored, 16)
            sp.wait_ge(stored, 16 * 8)

        @block.scalar
        def _(act):
            def evacuate(name, c):
                for i in range(4 * c, 4 * c + 4):
                    arrived(act, (name, i))
                    released(nc.scalar.copy(TR[:, :, P * i:P * i + P], PS[:, i % 2, 0:D].rearrange("p (k s) -> p k s", k=KC)), (name, i))

            loaded(act, "gates")
            nc.scalar.activation(gates[:, :, :], gates[:, :, :], ACT.Exp, scale=-1.0).then_inc(sig_ready, 1)

            keys = [(b, g, w, c) for b in range(B) for g in range(2) for w in range(2) for c in range(2)]
            for u, mid in [(8 * b + w, w > 0) for b in range(B) for w in range(9)]:
                if not mid:
                    for c in (u // 4, u // 4 + 1):
                        evacuate("t_in", c)
                if not mid or u % 8:
                    b, g, w, c = keys[u]
                    arrived(act, ("qk",) + keys[u])
                    if u >= 8:
                        act.wait_ge(parts_out[u // 2 - 4], 16)
                    nc.scalar.copy(PARTS[u // 2 % 4][:, 0, 512 * c:512 * c + 512],
                                   PS[:, uses[("qk",) + keys[u]][0], :]).then_inc(hi_ready, 1)
                if mid:
                    v = u - 1
                    drained(act, ("qk",) + keys[v])
                    nc.scalar.copy(PARTS[v // 2 % 4][:, 1, 512 * (v % 2):512 * (v % 2) + 512],
                                   REST[v % 3]).then_inc(mid_ready, 1)

            step_exp = 0
            for op, n, *at in attention_plan():
                if op == "score":
                    tt, c, j = at
                    key = ("score", n, tt, c, j)
                    w = 512 * c + 512 - max(P * tt, 512 * c)
                    step = step_exp // GRP
                    arrived(act, key)
                    if step >= 2:
                        act.wait_ge(pv_done, step - 1)
                    ins = nc.scalar.activation(PROB[GRP * (step % 2) + j][:, 0:w], PS[:, uses[key][0], 0:w], ACT.Exp,
                                               scale=HD ** -0.5)
                    released(ins, key)
                    step_exp += 1
                elif op == "turn":
                    arrived(act, ("turn", n))
                    bank = uses[("turn", n)][0]
                    ins = nc.scalar.copy(TR[:, :, 512 * n:512 * n + 512].rearrange("p k (i s) -> p i k s", i=4),
                                         PS[:, bank:bank + 2, :].rearrange("p b (i k s) -> p (b i) k s", i=2, k=KC))
                    released(ins, ("turn", n))
                elif op == "evac":
                    act.wait_ge(pv_done, len(STEPS) * (n + 1))
                    if n > 0:
                        arrived(act, ("out", n - 1))
                    ins = nc.scalar.copy(OTS, PS[:, 6:8, :].rearrange("p b s -> p (b s)"))
                    released(ins, ("values", n))

            def context(layer):
                act.wait_ge(sa_used, 4)
                for g in range(2):
                    arrived(act, ("kx", layer, g))
                    if layer == 0:
                        ins = nc.scalar.copy(KTX[:, g, :], PS[:, 6 + g, 0:B * T])
                    else:
                        ins = nc.scalar.activation(KTX[:, g, :], PS[:, 6 + g, 0:B * T], ACT.Identity, bias=bk3c[:, g:g + 1])
                    released(ins, ("kx", layer, g))

            def queries(layer, c):
                for g in range(2):
                    key = ("q", layer, c, g)
                    arrived(act, key)
                    src, dst = PS[:, 4 + g, :], QT[:, g, 512 * c:512 * c + 512]
                    if layer == 0:
                        ins = nc.scalar.copy(dst, src)
                    else:
                        ins = nc.scalar.activation(dst, src, ACT.Identity, bias=bq3c[:, g:g + 1])
                    released(ins, key)

            def cross(layer):
                for u in range(-2, UNITS + 1):
                    if 0 <= u < UNITS:
                        if layer:
                            act.wait_ge(shift_ready, u + 1)
                        else:
                            drained(act, ("sx", 0, u))
                        nc.scalar.activation(EX[u % 4], EX[u % 4], ACT.Exp, scale=HD ** -0.5).then_inc(ex_ready, 1)
                    if u >= 1:
                        if u >= 5:
                            arrived(act, ("ox", layer, (u - 5) // 2))
                        for m in range(2):
                            key = ("px", layer, u - 1, m)
                            arrived(act, key)
                            released(nc.scalar.copy(PTS[(u - 1) % 4][:, 4 * m:4 * m + 4, :],
                                                    PS[0:T, 4 + m, :].rearrange("p (h s) -> p h s", h=4)), key)
                    if layer == 0 and (u + 2) % 8 == 0 and u + 2 < UNITS:
                        if u + 2 >= 16:
                            evacuate("t_g1", (u + 2) // 8)
                        queries(0, (u + 2) // 8)

            context(0)
            cross(0)
            loaded(act, "bf1")
            loaded(act, "bq3")
            loaded(act, "bk3")
            for s in range(7):
                if s < 4:
                    evacuate("t_g2", s)
                    if s >= 2:
                        arrived(act, ("f2", 4 * (s - 2) + 3))
                    for f in range(FCH):
                        key = ("f1", s, f)
                        arrived(act, key)
                        released(nc.scalar.activation(HT[s % 2][:, f, :], PS[:, 2 + f % 4, :], ACT.Relu, bias=bf1c[:, f:f + 1]), key)
                if 2 <= s < 6:
                    evacuate("t_lin", s - 2)
                if s >= 3:
                    evacuate("t_xat", s - 3)
                    queries(1, s - 3)
                if s == 5:
                    context(1)
            cross(1)

            def gate(n):
                for i in range(TILES):
                    act.wait_ge(ln_ready, ln_count(("n1", "n2")[n], i))
                    if i >= 2:
                        act.wait_ge(ss_ready, TILES * n + i - 1)
                    nc.scalar.activation(SQ[:, i % 2, :], NB[:, i, :], ACT.Square, accum_out=ss[:, i:i + 1]).then_inc(ss_ready, 1)
                act.wait_ge(gate_in, n + 1)
                nc.scalar.activation(LG[:, 5, :], LG[:, 4, :], ACT.Exp).then_inc(gate_exp, 1)

            for c in range(4):
                evacuate("t_n1", c)
            gate(0)
            for i in range(TILES):
                arrived(act, ("qk1", i))
                ins = nc.scalar.copy(QK1[:, :, P * i:P * i + P], PS[:, 2 + i % 2, 0:2 * P].rearrange("p (w s) -> p w s", w=2))
                released(ins, ("qk1", i))
            def row_probs(i):
                cols = P * (i % TPB + 1)
                act.wait_ge(bias_ready, i + 1)
                if i >= 2:
                    arrived(act, ("p1", i - 2))
                ins = nc.scalar.activation(P1[i % 2][:, 0:cols], PS[:, 0:2, :].rearrange("p b s -> p (b s)")[:, 0:cols], ACT.Exp,
                                           bias=l1s[:, i % 2, 0:1], scale=HA ** -0.5, accum_out=l1s[:, i % 2, 1:2])
                released(ins, ("s1", i))

            row_probs(0)
            for i in range(TILES + 1):
                if i > 0:
                    t = i - 1
                    arrived(act, ("at", t))
                    if t >= 2:
                        arrived(act, ("o1", t - 2, 3))
                    released(nc.scalar.copy(ATTT[:, t % 2, :], PS[:, 5, 0:HA]), ("at", t))
                if i + 1 < TILES:
                    row_probs(i + 1)
                if i < TILES:
                    arrived(act, ("p1", i))
                    if i > 0:
                        arrived(act, ("a1", i - 1))
                    cols = P * (i % TPB + 1)
                    released(nc.scalar.copy(PT1.rearrange("p t s -> p (t s)")[:, 0:cols],
                                            PS[:, 2:4, :].rearrange("p b s -> p (b s)")[:, 0:cols]), ("p1", i))

            for c in range(4):
                evacuate("t_n2", c)
            gate(1)
            for c in range(4):
                if c >= 2:
                    arrived(act, ("m2", 4 * (c - 2) + 3, EXPERTS - 1))
                for m in range(2 * EXPERTS):
                    key = ("m1", c, m)
                    arrived(act, key)
                    ins = nc.scalar.activation(INT[c % 2][:, m, :], PS[:, uses[key][0], :], ACT.Gelu)
                    released(ins, key)

        @block.vector
        def _(dve):
            links = [0]

            def link(ins):
                links[0] += 1
                ins.then_inc(dve_chain, 1)
                dve.wait_ge(dve_chain, links[0])

            v = nc.vector
            norms = [0]

            def layernorm(src, dst, tiles, scale=None, shift=None):
                lo, hi = tiles[0], tiles[-1] + 1
                for i in tiles:
                    ins = v.bn_stats(stats[:, i, :], src[:, i, :])
                link(ins)
                for i in tiles:
                    ins = v.bn_aggr(mv[:, i, :], stats[:, i, :])
                link(ins)
                v.tensor_scalar(var[:, lo:hi], mv[:, lo:hi, 1:2].rearrange("p i o -> p (i o)"), EPS, None,
                                ALU.add).then_inc(var_ready, 1)
                norms[0] += 1
                if scale:
                    for i in tiles:
                        ins = v.scalar_tensor_tensor(out=dst[:, i, :], in0=src[:, i, :], scalar=mv[:, i, 0:1], in1=bc(scale),
                                                     op0=ALU.subtract, op1=ALU.mult)
                    link(ins)
                    dve.wait_ge(rstd_ready, norms[0])
                    for i in tiles:
                        v.scalar_tensor_tensor(out=dst[:, i, :], in0=dst[:, i, :], scalar=rstd[:, i:i + 1], in1=bc(shift),
                                               op0=ALU.mult, op1=ALU.add).then_inc(ln_ready, 1)
                    return
                dve.wait_ge(rstd_ready, norms[0])
                for i in tiles:
                    v.tensor_scalar(dst[:, i, :], src[:, i, :], mv[:, i, 0:1], rstd[:, i:i + 1],
                                    ALU.subtract, ALU.mult).then_inc(ln_ready, 1)

            loaded(dve, "sims")
            v.tensor_tensor(simsq[:, :, :, :], sims[:, :, :, :], sims[:, :, :, :], ALU.mult).then_inc(sim_ready, 1)
            arrived(dve, "simsum")
            ins = v.tensor_copy(siminv[:, :, :], PS[:, 7, 0:2 * EXPERTS].rearrange("p (n e) -> p n e", n=2))
            released(ins, "simsum")
            dve.wait_ge(sim_sum, 1)
            link(v.tensor_scalar(siminv[:, :, :], siminv[:, :, :], 1e-12, None, ALU.max))
            link(v.reciprocal(siminv[:, :, :], siminv[:, :, :]))
            link(v.tensor_tensor(sims[:, :, :, :], sims[:, :, :, :],
                                 siminv[:, :, :].unsqueeze(2).broadcast_to([P, 2, KC, EXPERTS]), ALU.mult))
            dve.wait_ge(sig_ready, 1)
            link(v.tensor_scalar(gates[:, :, :], gates[:, :, :], 1.0, None, ALU.add))
            link(v.reciprocal(gates[:, :, :], gates[:, :, :]))

            batches = [list(range(4 * k, 4 * k + 4)) for k in range(4)]
            for k in range(4):
                dve.wait_ge(x_in[k], 16)
                layernorm(X, H, batches[k])

            loaded(dve, "bc")
            u = 0
            for b in range(B):
                for w in range(9):
                    if w < 8:
                        key = ("qk", b, w // 4, w // 2 % 2, w % 2)
                        part = PARTS[u // 2 % 4]
                        dve.wait_ge(hi_ready, u + 1)
                        if u >= 3:
                            dve.wait_ge(parts_ready, u - 2)
                        ins = v.tensor_tensor(REST[u % 3], PS[:, uses[key][0], :], part[:, 0, 512 * (u % 2):512 * (u % 2) + 512],
                                              ALU.subtract)
                        released(ins, key)
                        u += 1
                    if w > 0:
                        t = u - 2 if w < 8 else u - 1
                        part = PARTS[t // 2 % 4]
                        dve.wait_ge(mid_ready, t + 1)
                        drained(dve, ("qk", b, t // 4 % 2, t // 2 % 2, t % 2))
                        v.tensor_tensor(part[:, 2, 512 * (t % 2):512 * (t % 2) + 512], REST[t % 3],
                                        part[:, 1, 512 * (t % 2):512 * (t % 2) + 512], ALU.subtract).then_inc(parts_ready, 1)
                for i in range(TPB * b, TPB * b + TPB):
                    arrived(dve, ("v1", i))
                    ins = v.tensor_tensor(VEXT[:, i, :, 0:HD],
                                          PS[:, uses[("v1", i)][0], 0:D].rearrange("p (h e) -> p h e", h=HEADS),
                                          bc("bv1").rearrange("p (h e) -> p h e", h=HEADS), ALU.add)
                    released(ins, ("v1", i))

            def add_norm(k):
                for i in batches[k]:
                    ins = v.tensor_tensor(H[:, i, :], H[:, i, :], SA[:, i, :], ALU.add)
                ins.then_inc(sa_used, 1)
                dve.wait_ge(sa_used, k + 1)
                if k < 2:
                    layernorm(H, H, batches[k], "g1", "be1")

            for op, n, *at in attention_plan():
                if op == "max":
                    j, st = at
                    key = ("max", n, j, st)
                    bank = uses[key][0]
                    arrived(dve, key)
                    ins = v.tensor_reduce(negm[:, n % 2, TPB * j + st:TPB * j + st + 1],
                                          PS[:, bank:bank + 2, :].rearrange("p b s -> p (b s)")[:, 0:P * (st + 1)],
                                          AX.X, ALU.max, negate=True)
                    released(ins, key)
                elif op == "neg":
                    key = ("neg", n)
                    arrived(dve, key)
                    src = PS[0:GRP * TPB, uses[key][0], 0:P]
                    if n >= 2:
                        dve.wait_ge(mrows_in[(n - 2) % SLOTS], 3 * 16 * ((n - 2) // SLOTS + 1))
                    link(v.tensor_copy(mparts[:, n % 2, 0, :], src))
                    ins = v.tensor_tensor(mrest, src, mparts[:, n % 2, 0, :], ALU.subtract)
                    released(ins, key)
                    drained(dve, key)
                    link(v.tensor_copy(mparts[:, n % 2, 1, :], mrest))
                    v.tensor_tensor(mparts[:, n % 2, 2, :], mrest, mparts[:, n % 2, 1, :],
                                    ALU.subtract).then_inc(mparts_ready, 1)
                elif op == "norm":
                    if n == 0:
                        drained(dve, ("out", GROUPS // 2 - 1))
                    add_norm(n)
                elif op == "out":
                    key = ("out", n)
                    arrived(dve, key)
                    if n == 0:
                        for k in range(8):
                            dve.wait_ge(parts_out[k], 16)
                    else:
                        drained(dve, ("out", n - 1))
                    src = PS[:, uses[key][0]:uses[key][0] + 2, :].rearrange("p b (m e) -> p (b m) e", e=32)
                    link(v.reciprocal(rsum, src[:, :, HD:HD + 1].rearrange("p m o -> p (m o)")))
                    c0 = GRP * HD * (n % 4)
                    ins = v.tensor_tensor(SA[:, TPB * (n // 4):TPB * (n // 4) + TPB, c0:c0 + GRP * HD].rearrange("p i (j e) -> p i j e", j=GRP),
                                          src[:, :, 0:HD].rearrange("p (i j) e -> p i j e", i=TPB),
                                          rsum.rearrange("p (i j) -> p i j", i=TPB).unsqueeze(3).broadcast_to([P, TPB, GRP, HD]),
                                          ALU.mult)
                    released(ins, key)
            drained(dve, ("out", GROUPS - 1))
            add_norm(2)
            add_norm(3)

            def context(layer):
                if layer == 1:
                    loaded(dve, "masks")
                    maskb = KEEPF[:, 0, :].unsqueeze(1)
                    for b in range(B):
                        link(v.tensor_scalar(KEEPF[:, 0, :], MASKB[:, b, :], 0.0, None, ALU.not_equal))
                        link(v.tensor_scalar(KEEPF[:, TPB:2 * TPB, :], MASKS, 0.0, None, ALU.not_equal))
                        link(v.tensor_tensor(KEEP[:, TPB * b:TPB * b + TPB, :], KEEPF[:, TPB:2 * TPB, :],
                                             maskb.broadcast_to([P, TPB, T]), ALU.mult))
                v.memset(VX[:, :, :, HD:HD + 1], 1.0).then_inc(kv_ready, 1)
                for g in range(2):
                    drained(dve, ("kx", layer, g))
                for b in range(B):
                    for g in range(2):
                        v.tensor_tensor(KBD[:, b, g, :, :],
                                        KTX[:, g, T * b:T * b + T].unsqueeze(1).broadcast_to([P, 8, T]),
                                        blockm[:, :].unsqueeze(2).broadcast_to([P, 8, T]), ALU.mult).then_inc(kv_ready, 1)
                for b in range(B):
                    key = ("vx", layer, b)
                    arrived(dve, key)
                    released(v.tensor_tensor(VX[:, b, :, 0:HD], PS[0:T, 6 + b, 0:D].rearrange("p (h e) -> p h e", h=HEADS),
                                             bc(("bv2", "bv3")[layer])[0:T, :].rearrange("p (h e) -> p h e", h=HEADS), ALU.add), key)

            def cross(layer):
                x = X if layer else H

                def shift(u):
                    i, g = u // 2, u % 2
                    key = ("sx", layer, u)
                    full = [P, 2, 4, T]
                    ex = EX[u % 4].rearrange("p (m h) t -> p m h t", m=2)
                    src = PS[:, 2 * g:2 * g + 2, 0:4 * T].rearrange("p m (h t) -> p m h t", h=4)
                    most = mx[:, 0, HH * g:HH * g + HH].rearrange("p (m h) -> p m h", m=2)
                    if u >= 4:
                        arrived(dve, ("px", layer, u - 4, 1))
                    if layer:
                        dve.wait_ge(fill_ready, u + 1)
                        arrived(dve, key)
                        ins = v.copy_predicated(ex, KEEP[:, i, :].unsqueeze(1).unsqueeze(1).broadcast_to(full), src)
                        released(ins, key)
                        drained(dve, key)
                        src = ex
                    else:
                        arrived(dve, key)
                    link(v.tensor_reduce(most, src, AX.X, ALU.max))
                    ins = v.tensor_tensor(ex, src, most.unsqueeze(3).broadcast_to(full), ALU.subtract)
                    if layer:
                        ins.then_inc(shift_ready, 1)
                    else:
                        released(ins, key)

                def divide(t):
                    key = ("ox", layer, t)
                    arrived(dve, key)
                    src = PS[:, 6 + t % 2, 0:HEADS * VW].rearrange("p (h e) -> p h e", h=HEADS)
                    link(v.reciprocal(mx[:, 1, :], src[:, :, HD:HD + 1].rearrange("p h o -> p (h o)")))
                    ins = v.tensor_tensor(tmp[:, t % 2, :].rearrange("p (h e) -> p h e", h=HEADS), src[:, :, 0:HD],
                                          mx[:, 1, :].unsqueeze(2).broadcast_to([P, HEADS, HD]), ALU.mult)
                    released(ins, key)
                    drained(dve, key)
                    link(v.tensor_tensor(x[:, t, :], x[:, t, :], tmp[:, t % 2, :], ALU.add))
                    if t % 4 == 3:
                        if layer:
                            layernorm(x, H, batches[t // 4])
                        else:
                            layernorm(x, H, batches[t // 4], "g2", "be2")

                for u in range(UNITS + 3):
                    if u < UNITS:
                        shift(u)
                    if u >= 4 and u % 2 == 0:
                        divide((u - 4) // 2)

            context(0)
            layernorm(H, H, batches[2], "g1", "be1")
            layernorm(H, H, batches[3], "g1", "be1")
            cross(0)

            for n, (key, dst) in enumerate((("l1", LD1), ("l2", LD2))):
                arrived(dve, key)
                released(v.tensor_copy(dst, PS[0:(4, 50)[n], 2 + n, 0:D]), key)
            arrived(dve, "l3")
            loaded(dve, "wt")
            released(v.tensor_tensor(WEFF, WEFF, PS[:, 4, :].rearrange("p (k f) -> p k f", k=KC), ALU.add), "l3")
            for s in range(1, 6):
                if s >= 2:
                    for i in batches[s - 2]:
                        arrived(dve, ("lin", i))
                        released(v.tensor_tensor(tmp[:, i % 2, :], PS[:, 2 + i % 4, 0:D], bc("lb"), ALU.add), ("lin", i))
                        drained(dve, ("lin", i))
                        link(v.tensor_tensor(X[:, i, :], X[:, i, :], tmp[:, i % 2, :], ALU.add))
                    layernorm(X, H, batches[s - 2])
                if s <= 4:
                    for i in batches[s - 1]:
                        arrived(dve, ("f2", i))
                        released(v.tensor_tensor(tmp[:, i % 2, :], PS[:, 6 + i % 2, 0:D], bc("bf2"), ALU.add), ("f2", i))
                        drained(dve, ("f2", i))
                        link(v.tensor_tensor(H[:, i, :], H[:, i, :], tmp[:, i % 2, :], ALU.add))
                    layernorm(H, H, batches[s - 1], "g3", "be3")
                    dve.wait_ge(ln_ready, ln_count("g3", 4 * s - 1))
                    for i in batches[s - 1]:
                        ins = v.tensor_tensor(X[:, i, :], X[:, i, :], H[:, i, :], ALU.add)
                    link(ins)
                    layernorm(X, H, batches[s - 1])
            context(1)
            cross(1)

            for k in range(4):
                dve.wait_ge(ln_ready, ln_count("ffn", 4 * k + 3))
                layernorm(H, NB, batches[k], "n1w", "n1b")

            def gate(n):
                dve.wait_ge(ssr_ready, n + 1)
                link(v.tensor_scalar(ssr[:, :], ssr[:, :], 1e-12, None, ALU.max))
                link(v.reciprocal(ssr[:, :], ssr[:, :]))
                l = [LG[:, k, :].rearrange("p (i e) -> p i e", i=TILES) for k in range(8)]
                per = [P, TILES, EXPERTS]
                full = [P, TILES, EXPERTS, EXPERTS]
                arrived(dve, ("lg", n))
                link(v.tensor_tensor(l[0], PS[:, 2, 0:NL].rearrange("p (i e) -> p i e", i=TILES),
                                     ssr[:, :].unsqueeze(2).broadcast_to(per), ALU.mult))
                ins = v.tensor_tensor(l[0], l[0], gates[:, n, :].unsqueeze(1).broadcast_to(per), ALU.subtract)
                released(ins, ("lg", n))
                drained(dve, ("lg", n))
                other = l[0].unsqueeze(2).broadcast_to(full)
                own = l[0].unsqueeze(3).broadcast_to(full)
                v.tensor_tensor(RANK[:, 0], other, own, ALU.is_gt)
                link(v.tensor_tensor(RANK[:, 1], other, own, ALU.is_equal))
                link(v.tensor_tensor(RANK[:, 1], RANK[:, 1], lower[:, :, :].unsqueeze(1).broadcast_to(full), ALU.mult))
                link(v.tensor_tensor(RANK[:, 0], RANK[:, 0], RANK[:, 1], ALU.add))
                v.tensor_reduce(l[3], RANK[:, 0], AX.X, ALU.add)
                v.tensor_scalar(l[2], l[0], 0.0, None, ALU.is_gt)
                link(v.tensor_scalar(l[1], l[0], 0.0, None, ALU.max))
                link(v.tensor_reduce(gsm[:, 0, :], l[1], AX.X, ALU.max))
                v.tensor_tensor(l[4], l[1], gsm[:, 0, :].unsqueeze(2).broadcast_to(per), ALU.subtract).then_inc(gate_in, 1)
                link(v.tensor_scalar(gsm[:, 1, :], gsm[:, 0, :], 0.0, None, ALU.is_equal))
                link(v.scalar_tensor_tensor(out=l[6], in0=l[3], scalar=2.0, in1=gsm[:, 1, :].unsqueeze(2).broadcast_to(per),
                                            op0=ALU.is_lt, op1=ALU.mult))
                link(v.tensor_tensor(l[2], l[2], l[6], ALU.max))
                dve.wait_ge(gate_exp, n + 1)
                link(v.tensor_tensor(l[7], l[5], l[2], ALU.mult))
                link(v.tensor_reduce(gsm[:, 2, :], l[7], AX.X, ALU.add))
                link(v.reciprocal(gsm[:, 3, :], gsm[:, 2, :]))
                link(v.tensor_tensor(rw[:, n, :, :], l[7], gsm[:, 3, :].unsqueeze(2).broadcast_to(per), ALU.mult))

            gate(0)
            for i in range(TILES):
                for e in range(EXPERTS):
                    key = ("qkv", i, e)
                    arrived(dve, key)
                    src, w = PS[:, uses[key][0], 0:3 * HA], rw[:, 0, i, e:e + 1]
                    if e == 0:
                        ins = v.tensor_scalar(QKV[:, i, :], src, w, None, ALU.mult)
                    else:
                        ins = v.scalar_tensor_tensor(out=QKV[:, i, :], in0=src, scalar=w, in1=QKV[:, i, :], op0=ALU.mult, op1=ALU.add)
                    released(ins, key)
                    drained(dve, key)
            def row_max(i):
                arrived(dve, ("s1", i))
                s = l1s[:, i % 2, :]
                link(v.tensor_reduce(s[:, 3:4], PS[:, 0:2, :].rearrange("p b s -> p (b s)")[:, 0:P * (i % TPB + 1)],
                                     AX.X, ALU.max, negate=True))
                v.tensor_scalar(s[:, 0:1], s[:, 3:4], HA ** -0.5, None, ALU.mult).then_inc(bias_ready, 1)

            row_max(0)
            for i in range(TILES + 1):
                if i > 0:
                    t = i - 1
                    s = l1s[:, t % 2, :]
                    arrived(dve, ("a1", t))
                    if t >= 2:
                        drained(dve, ("at", t - 2))
                    drained(dve, ("s1", t))
                    link(v.reciprocal(s[:, 2:3], s[:, 1:2]))
                    released(v.tensor_scalar(ATT[:, t % 2, :], PS[:, 4, 0:HA], s[:, 2:3], None, ALU.mult), ("a1", t))
                if i + 1 < TILES:
                    row_max(i + 1)
                if i > 0:
                    for m in range(4):
                        key = ("o1", t, m)
                        arrived(dve, key)
                        for e in range(2):
                            ins = v.scalar_tensor_tensor(out=H[:, t, :], in0=PS[:, 6 + m % 2, D * e:D * e + D],
                                                         scalar=rw[:, 0, t, 2 * m + e:2 * m + e + 1], in1=H[:, t, :],
                                                         op0=ALU.mult, op1=ALU.add)
                            if e == 0:
                                link(ins)
                        released(ins, key)
                        drained(dve, key)
                    if t % 4 == 3:
                        layernorm(H, NB, batches[t // 4], "n2w", "n2b")
            for i in range(TILES):
                ins = v.tensor_tensor(X[:, i, :], X[:, i, :], H[:, i, :], ALU.add)
            link(ins)
            gate(1)
            for i in range(TILES):
                for e in range(EXPERTS):
                    key = ("m2", i, e)
                    arrived(dve, key)
                    ins = v.scalar_tensor_tensor(out=X[:, i, :], in0=PS[:, uses[key][0], 0:D], scalar=rw[:, 1, i, e:e + 1],
                                                 in1=X[:, i, :], op0=ALU.mult, op1=ALU.add)
                    released(ins, key)
                    drained(dve, key)

        @block.gpsimd
        def _(pool):
            g = nc.gpsimd
            links = [0]

            def link(ins):
                links[0] += 1
                ins.then_inc(pool_chain, 1)
                pool.wait_ge(pool_chain, links[0])

            g.memset(ident[:, :], 0.0)
            g.memset(halves[:, :], -0.5)
            g.memset(halfp[:, :], 0.5)
            g.memset(maskq[:, :], 0.0)
            g.memset(maskk[:, :], 0.0)
            g.memset(blockm[:, :], 1.0)
            link(g.memset(lower[:, :, :], 1.0))
            ins = g.memset(ones, 1.0)
            link(g.affine_select(out=ident[:, :], in_=ident[:, :], compare_op=ALU.not_equal, fill=1.0, base=0,
                                 pattern=[[-1, P]], channel_multiplier=1))
            g.affine_select(out=maskq[:, :], in_=maskq[:, :], compare_op=ALU.is_ge, fill=BIG, base=0,
                            pattern=[[-1, P]], channel_multiplier=1)
            g.affine_select(out=maskk[:, :], in_=maskk[:, :], compare_op=ALU.is_ge, fill=BIG, base=0,
                            pattern=[[1, P]], channel_multiplier=-1)
            link(g.affine_select(out=blockm[:, :], in_=blockm[:, :], compare_op=ALU.is_ge, fill=0.0, base=0,
                                 pattern=[[-HD, 8]], channel_multiplier=1))
            g.affine_select(out=blockm[:, :], in_=blockm[:, :], compare_op=ALU.is_ge, fill=0.0, base=HD - 1,
                            pattern=[[HD, 8]], channel_multiplier=-1)
            g.affine_select(out=lower[:, :, :], in_=lower[:, :, :], compare_op=ALU.is_gt, fill=0.0, base=0,
                            pattern=[[1, EXPERTS], [-1, EXPERTS]], channel_multiplier=0)
            g.tensor_copy(identb[:, :], ident[:, :]).then_inc(consts, 1)
            link(g.memset(VEXT[:, :, :, HD:HD + 1], 1.0))
            for s in range(SLOTS):
                link(g.memset(PACKK[s][ROWS:ROWS + 3, :, :], 1.0))
            g.memset(mparts[:, :, :, :], 0.0).then_inc(consts, 1)
            drained(pool, "simsum")
            g.tensor_tensor(siminv[:, :, :].rearrange("p n e -> p (n e)"), siminv[:, :, :].rearrange("p n e -> p (n e)"),
                            halfp[:, :], ALU.pow).then_inc(sim_sum, 1)

            for n, (name, k) in enumerate(NORMS):
                pool.wait_ge(var_ready, n + 1)
                g.tensor_tensor(rstd[:, 4 * k:4 * k + 4], var[:, 4 * k:4 * k + 4], halves[:, 0:4], ALU.pow).then_inc(rstd_ready, 1)
                if (name, k) in (("n1", 3), ("n2", 3)):
                    m = ("n1", "n2").index(name)
                    pool.wait_ge(ss_ready, TILES * (m + 1))
                    g.tensor_tensor(ssr[:, :], ss[:, :], halfp[:, :], ALU.pow).then_inc(ssr_ready, 1)
                if (name, k) == ("xat", 3) or name == "ffn" and k < 3:
                    lo = 0 if name == "xat" else 8 * k + 12
                    hi = 12 if name == "xat" else min(8 * k + 20, UNITS)
                    for u in range(lo, hi):
                        if u >= 4:
                            arrived(pool, ("px", 1, u - 4, 1))
                        elif u == 0:
                            arrived(pool, ("ox", 0, TILES - 1))
                        g.memset(EX[u % 4], MASKED / HD ** -0.5).then_inc(fill_ready, 1)


def _layout(inputs):
    import numpy as np

    f = {k: np.asarray(v) for k, v in inputs.items()}
    r = {"x": f["x"].reshape(N, D), "ctxT": f["ctx_1024"].reshape(B * T, D).T}
    for n in (1, 2):
        for w in "qkv":
            r[f"w{w}{n}"] = f[f"L0_xattn_W{w}{n}"].transpose(1, 0, 2).reshape(D, D)
    for w in "qkv":
        r[f"w{w}3"] = f[f"L1_xattn_W{w}"].T
    r |= {"bq3": f["L1_xattn_bq"], "bk3": f["L1_xattn_bk"], "bf1": f["L0_xattn_bf1"], "wf1": f["L0_xattn_Wf1"],
          "wf2": f["L0_xattn_Wf2"], "wt": f["L0_ffn_W"].T, "daux": f["L0_ffn_down_aux"], "upT": f["L0_ffn_up_aux"].T,
          "ldT": f["L0_ffn_lora_down"].T, "luT": f["L0_ffn_lora_up"].T}
    r["wqkv"] = np.concatenate([f[f"L1_ffn_{w}_proj"].transpose(1, 0, 2) for w in "qkv"], axis=2)
    r |= {"wo": f["L1_ffn_o_proj"], "w1": f["L1_ffn_w1"].transpose(1, 0, 2), "w2": f["L1_ffn_w2"].reshape(EXPERTS * D, D), "sim1": f["L1_ffn_smha_sim"],
          "sim2": f["L1_ffn_moe_sim"], "gates1": f["L1_ffn_smha_gates"], "gates2": f["L1_ffn_moe_gates"],
          "mask_st": f["mask_1x1xSxS2_ik0"].reshape(S, T), "mask_bt": f["mask_Bx1x1xS2_ik0"].reshape(B, T)}
    for name in ("bq3", "bk3", "bf1"):
        r[name] = r[name].reshape(-1, P).T
    rows = {"bv1": f["L0_xattn_bv1"], "bv2": f["L0_xattn_bv2"], "g1": f["L0_xattn_g1"], "be1": f["L0_xattn_be1"],
            "g2": f["L0_xattn_g2"], "be2": f["L0_xattn_be2"], "g3": f["L0_xattn_g3"], "be3": f["L0_xattn_be3"],
            "bf2": f["L0_xattn_bf2"], "lb": f["L0_ffn_b"], "bv3": f["L1_xattn_bv"], "n1w": f["L1_ffn_ln1_w"],
            "n1b": f["L1_ffn_ln1_b"], "n2w": f["L1_ffn_ln2_w"], "n2b": f["L1_ffn_ln2_b"]}
    r["bcast"] = np.stack([rows[name].reshape(D) for name in BCAST])
    return {k: np.ascontiguousarray(v) for k, v in r.items()}


def kernel(**inputs):
    import concourse.bacc as bacc
    from concourse.bass_utils import run_bass_kernel_spmd

    arrays = _layout(inputs)
    nc = bacc.Bacc("TRN2", target_bir_lowering=False, num_devices=1)
    args = {k: nc.dram_tensor(f"in_{k}", v.shape, mybir.dt.from_np(v.dtype), kind="ExternalInput").ap()
            for k, v in arrays.items()}
    out = nc.dram_tensor("out_x", (N, D), F32, kind="ExternalOutput").ap()
    build(nc, args, out)
    r = run_bass_kernel_spmd(nc, [{f"in_{k}": v for k, v in arrays.items()}], core_ids=[0])
    return r.results[0]["out_x"].reshape(B, S, D)
```

```python
from contextlib import ExitStack

import concourse.bass as bass
from concourse import mybir

F32 = mybir.dt.float32
F32R = mybir.dt.float32r
BF16 = mybir.dt.bfloat16
I32 = mybir.dt.int32
ALU = mybir.AluOpType
ACT = mybir.ActivationFunctionType
AX = mybir.AxisListType

P = 128
B, S, D, T = 2, 1024, 256, 77
N = B * S
TILES = N // P
TPB = S // P
HEADS, HD = 16, 16
KC = D // P
FF = 1024
FCH = FF // P
EXPERTS = 8
HA = 128
EPS = 1e-5
BIG = -3.0e38
MASKED = -1.0e9
GRP = 4
GROUPS = B * HEADS // GRP
SLOTS = 3
VW = HD + 1
ROWS = 6 * HD
QPART = [0, 1, 2, 0, 1, 0]
KPART = [0, 0, 0, 1, 1, 2]
UNITS = 2 * TILES
HH = HEADS // 2
PIECES = [(lo, min(P, HH * T - lo)) for lo in range(0, HH * T, P)]
PIECE_HEADS = [(lo // T, (lo + rows - 1) // T + 1) for lo, rows in PIECES]
BCAST = ["bv1", "bv2", "g1", "be1", "g2", "be2", "g3", "be3", "bf2", "lb", "bv3",
         "n1w", "n1b", "n2w", "n2b"]


STEPS = [(tt, c) for tt in range(TPB) for c in range(2) if tt < 4 * (c + 1)]
ROW_ORDER = [0, 7, 6, 1, 2, 5, 4, 3]
LEAD, NEG_LEAD, PV_LAG, OUT_AT, STEP_WEIGHT, ROW_WEIGHT = 15, 10, 2, 6, 600, 1000
EARLY_PIECES = 5
PROJ_STEPS = 8 + 1 + TPB // 2


def norm_order():
    for name in ("in", "g1", "g2"):
        for k in range(4):
            yield name, k
    for s in range(5):
        if s > 0:
            yield "xat", s - 1
        if s < 4:
            yield "g3", s
            yield "lin", s
    for k in range(4):
        yield "ffn", k
        yield "n1", k
    for k in range(4):
        yield "n2", k


NORMS = list(norm_order())


def attention_plan():
    for n in range(GROUPS + 1):
        maxima = [(j, st) for j in range(GRP) for st in ROW_ORDER] if n < GROUPS else []
        units = len(STEPS) * GRP
        steps_work = [STEP_WEIGHT + 512 * (c + 1) - max(P * tt, 512 * c) for tt, c in STEPS for _ in range(GRP)]
        maxima_work = [ROW_WEIGHT + P * (st + 1) for _, st in maxima]
        done = 0
        for u in range(units):
            if n > 0:
                tt, c = STEPS[u // GRP]
                yield "score", n - 1, tt, c, u % GRP
            if u == 1 and n > 1:
                yield "evac", n - 2
            if u == OUT_AT and n > 1:
                yield "out", n - 2
            if u == 20 and n in (5, 6):
                yield "norm", n - 5
            if u == 20 and n in (6, 7):
                yield "turn", n - 6
            if n == 0:
                for m in ((2 * u, 2 * u + 1) if u < len(maxima) // 2 else ()):
                    yield ("max", n) + maxima[m]
                    done += 1
                if u < PROJ_STEPS:
                    yield "project", n, u
            while done < len(maxima) and (sum(maxima_work[:done + 1]) * sum(steps_work[:-LEAD])
                                          <= sum(steps_work[:u + 1]) * sum(maxima_work)):
                yield ("max", n) + maxima[done]
                done += 1
            if u == units - NEG_LEAD and n < GROUPS:
                assert done == len(maxima)
                yield "neg", n
            if n > 0 and u % GRP == PV_LAG and u > GRP:
                yield ("pv", n - 1) + STEPS[u // GRP - 1]
        if n > 0:
            yield ("pv", n - 1) + STEPS[-1]
    yield "evac", GROUPS - 1
    yield "out", GROUPS - 1


def build(nc, a, out):
    ctx = ExitStack()
    with ctx:
        def sb(name, shape, dt):
            return ctx.enter_context(nc.sbuf_tensor(name, shape, dt))

        def sem(name):
            return ctx.enter_context(nc.semaphore(name))

        X = sb("X", [P, TILES, D], F32)
        H = sb("H", [P, TILES, D], F32)
        tr_at = nc.sbuf_base
        TR = sb("TR", [P, KC, N], F32)
        w6_at = nc.sbuf_base
        W6 = sb("W6", [P, 6 * KC * D], F32)
        BC = sb("BC", [P, len(BCAST), D], F32)
        arena_at = nc.sbuf_base
        ARENA = sb("ARENA", [P, 31696], F32)
        TRR = nc.alloc_sbuf_tensor_at("TRR", [P, KC, N], F32R, offset=tr_at)
        PS = ctx.enter_context(nc.psum_tensor("PS", [P, 8, 512], F32))

        def bc(name):
            return BC[:, BCAST.index(name), :]

        def region(lo, n, pattern=None, parts=P, **kw):
            v = ARENA[0:parts, lo:lo + n]
            return v.rearrange(pattern, **kw) if pattern else v

        def part(name, lo, n, pattern, **kw):
            return nc.alloc_sbuf_tensor_at(name, [P, n], F32R, offset=arena_at + 4 * lo)[:, :].rearrange(pattern, **kw)

        def w6(n):
            return W6[:, n * KC * D:(n + 1) * KC * D].rearrange("p (k f) -> p k f", k=KC)

        ident = sb("ident", [P, P], F32)
        identb = sb("identb", [P, P], BF16)
        maskq = sb("maskq", [P, P], BF16)
        blockm = sb("blockm", [P, 8], F32)
        lower = sb("lower", [P, EXPERTS, EXPERTS], F32)
        halves = sb("halves", [P, TILES], F32)
        halfp = sb("halfp", [P, TILES], F32)
        stats = sb("stats", [P, TILES, 6], F32)
        mv = sb("mv", [P, TILES, 2], F32)
        var = sb("var", [P, TILES], F32)
        rstd = sb("rstd", [P, TILES], F32)
        tmp = sb("tmp", [P, 2, D], F32)
        ctxT = sb("ctxT", [P, KC, B * T], F32)
        bf1c = sb("bf1c", [P, FCH], F32)
        bq3c = sb("bq3c", [P, KC], F32)
        bk3c = sb("bk3c", [P, KC], F32)
        mx = sb("mx", [P, 2, HEADS], F32)
        sims = sb("sims", [P, 2, KC, EXPERTS], F32)
        simsq = sb("simsq", [P, 2, KC, EXPERTS], F32)
        siminv = sb("siminv", [P, 2, EXPERTS], F32)
        simparts = sb("simparts", [P, 2, 2, KC, EXPERTS], F32R)
        gates = sb("gates", [P, 2, EXPERTS], F32)
        ss = sb("ss", [P, TILES], F32)
        ssr = sb("ssr", [P, TILES], F32)
        gsm = sb("gsm", [P, 4, TILES], F32)
        rw = sb("rw", [P, 2, TILES, EXPERTS], F32)
        l1s = sb("l1s", [P, 2, 4], F32)

        PACKQ = [region(2048 * s, 2048).bitcast(BF16).rearrange("p (j s) -> p j s", j=GRP)
                 for s in range(SLOTS)]
        PACKK = [region(6144 + 2048 * s, 2048).bitcast(BF16).rearrange("p (j s) -> p j s", j=GRP)
                 for s in range(SLOTS)]
        PARTS = [region(12288 + 1536 * s, 1536).bitcast(BF16).rearrange("p (c s) -> p c s", c=3)
                 for s in range(4)]
        SA = region(14336, 4096, "p (i f) -> p i f", i=TILES)
        PROB = [region(18432 + 512 * s, 512) for s in range(8)]
        VEXT = region(22528, TILES * HEADS * VW, "p (i h e) -> p i h e", i=TILES, h=HEADS)
        OTS = region(26880, 1024)
        REST = [region(27904 + 512 * s, 512) for s in range(3)]
        ones = region(30000, P)
        mrest = region(30128, P, parts=GRP * TPB)
        mparts = region(30256, 3 * P, parts=GRP * TPB).bitcast(BF16).rearrange("p (u c s) -> p u c s", u=2, c=3)
        negm = region(30640, 2 * GRP * TPB, "p (u m) -> p u m", u=2)
        rsum = region(30704, GRP * TPB)
        QT = region(0, 4096, "p (g s) -> p g s", g=2)
        KBD = region(4096, B * 2 * 8 * T, "p (b g h t) -> p b g h t", b=B, g=2, h=8)
        VBD = region(6560, 4 * 5 * HH * VW, "p (b g j h e) -> p b g j h e", b=B, g=2, j=len(PIECES), h=HH)
        EX = [region(9280 + HH * T * s, HH * T, "p (h t) -> p h t", h=HH) for s in range(4)]
        PTS = [region(11744 + 640 * s, 640, "p (j s) -> p j s", s=P) for s in range(4)]
        KTX = region(29136, 2 * B * T, "p (g t) -> p g t", g=2)
        CREP = [[v.rearrange("p (k h t) -> p k h t", k=KC, h=HH) for v in pair]
                for pair in ((region(27904, 1232), W6[:, 0:1232]), (region(23504, 1232), region(24736, 1232)))]
        W3 = region(14612, 1024, "p (w k f) -> p w k f", w=2, k=KC)
        MASKS = region(4096, 616).bitcast(I32).rearrange("p (i t) -> p i t", i=TPB)
        MASKB = region(4712, 154).bitcast(I32).rearrange("p (b t) -> p b t", b=B)
        KEEP = W6[:, 0:TILES * T].bitcast(I32).rearrange("p (i t) -> p i t", i=TILES)
        KEEPF = W6[:, TILES * T:2 * TILES * T].rearrange("p (i t) -> p i t", i=TILES)
        WF1 = region(16384, 2048, "p (k f) -> p k f", k=KC)
        WF1P = [part(f"WF1P{w}", lo, 2048, "p (k f) -> p k f", k=KC) for w, lo in enumerate((18432, 16384))]
        WF2 = region(9280, 2048, "p (f d) -> p f d", f=FCH)
        WF2P = [part(f"WF2P{w}", lo, 2048, "p (f d) -> p f d", f=FCH) for w, lo in enumerate((11328, 9280))]
        HT = [part(f"HT{w}", lo, 4096, "p (f s) -> p f s", f=FCH) for w, lo in enumerate((23504, 27600))]
        HTF = [region(20992 + 512 * s, 512) for s in range(4)]
        TRG = [nc.alloc_sbuf_tensor_at(f"TRG{s}", [P, KC, 512], F32R, offset=w6_at + 4096 * s)[:, :, :] for s in range(2)]
        TRGF = region(13376, 1024, "p (i k s) -> p i k s", i=4, k=KC)
        WEFF = region(20480, 512, "p (k f) -> p k f", k=KC)
        DAUX = region(20992, 256, parts=100)
        LD1 = region(21248, 256, parts=4)
        LD2 = region(21504, 256, parts=50)
        UPT = region(21760, 256, parts=50)
        LDT = region(22016, 4, parts=100)
        LUT = region(22020, 50, parts=4)
        WQKV = region(15312, 6144, "p (k e f) -> p k e f", k=KC, e=EXPERTS)
        WQKVP = [part(f"WQKVP{w}", lo, 6144, "p (k e f) -> p k e f", k=KC, e=EXPERTS) for w, lo in enumerate((21456, 15312))]
        WO = region(27600, 2048, "p (e f) -> p e f", e=EXPERTS)
        W1 = region(15312, 4096, "p (k e f) -> p k e f", k=KC, e=EXPERTS)
        W1P = [part(f"W1P{w}", lo, 4096, "p (k e f) -> p k e f", k=KC, e=EXPERTS) for w, lo in enumerate((19408, 15312))]
        W2 = region(23504, 4096, "p (e k f) -> p e k f", e=EXPERTS, k=KC)
        W2P = [part(f"W2P{w}", lo, 4096, "p (e k f) -> p e k f", e=EXPERTS, k=KC) for w, lo in enumerate((0, 23504))]
        TRP = [[TRR[:, :, :], part(f"TRL{n}", lo, 4096, "p (k s) -> p k s", k=KC)] for n, lo in enumerate((0, 10240))]
        NBX = region(29648, 2048, "p (c i f) -> p c i f", c=2, i=4)
        SQ = BC[:, 0:2, :]
        TRF = BC[:, 2:6, :].rearrange("p i (k s) -> p i k s", k=KC)
        QK1 = region(0, 4096, "p (w s) -> p w s", w=2)
        QKV = region(4096, 6144, "p (i f) -> p i f", i=TILES)
        P1 = [W6[:, 1024 * s:1024 * (s + 1)] for s in range(2)]
        PT1 = W6[:, 2048:3072].rearrange("p (t s) -> p t s", t=TPB)
        ATT = BC[:, 6:10, :].rearrange("p n f -> p (n f)").rearrange("p (e f) -> p e f", e=EXPERTS)
        ATTT = TR[:, :, N - 4 * P:N]
        RANK = tmp[:, :, :].rearrange("p u (i e j) -> p u i e j", i=4, e=EXPERTS)
        LG = region(14848, 8 * 4 * EXPERTS, "p (u n) -> p u n", u=8)
        INT = [part(f"INT{s}", (4096, 6144, 8192, 27600)[s], 2048, "p (w c s) -> p w c s", w=2, c=KC) for s in range(4)]
        INTF = [W6[:, 512 * s:512 * (s + 1)] for s in range(4)]

        scratch = nc.dram_tensor("qk_parts", [B, 2, D, 3, S], BF16, kind="Internal").ap()

        bank_full = [sem(f"bank_full{k}") for k in range(8)]
        bank_free = [sem(f"bank_free{k}") for k in range(8)]
        consts = sem("consts")
        pool_chain = sem("pool_chain")
        dve_chain = sem("dve_chain")
        x_in = [sem(f"x_in{k}") for k in range(4)]
        ln_ready = sem("ln_ready")
        var_ready = sem("var_ready")
        rstd_ready = sem("rstd_ready")
        fill_ready = sem("fill_ready")
        hi_ready = sem("hi_ready")
        mid_ready = sem("mid_ready")
        parts_ready = sem("parts_ready")
        parts_out = [sem(f"parts_out{k}") for k in range(8)]
        pack_in = [sem(f"pack_in{k}") for k in range(SLOTS)]
        mparts_ready = sem("mparts_ready")
        mrows_in = [sem(f"mrows_in{k}") for k in range(SLOTS)]
        pv_done = sem("pv_done")
        cleared = sem("cleared")
        sa_used = sem("sa_used")
        kv_ready = sem("kv_ready")
        crep_ready = sem("crep_ready")
        vbd_clear = sem("vbd_clear")
        vx_ready = sem("vx_ready")
        shift_ready = sem("shift_ready")
        ex_ready = sem("ex_ready")
        sim_ready = sem("sim_ready")
        sim_sum = sem("sim_sum")
        sig_ready = sem("sig_ready")
        ss_ready = sem("ss_ready")
        ssr_ready = sem("ssr_ready")
        gate_in = sem("gate_in")
        gate_exp = sem("gate_exp")
        bias_ready = sem("bias_ready")
        lower_ready = sem("lower_ready")
        trg_ready = sem("trg_ready")
        ht_ready = sem("ht_ready")
        wf1_split = sem("wf1_split")
        wf2_upper = sem("wf2_upper")
        wf2_split = sem("wf2_split")
        most_ready = sem("most_ready")
        wqkv_upper = sem("wqkv_upper")
        wqkv_split = sem("wqkv_split")
        w1_split = sem("w1_split")
        w2_split = sem("w2_split")
        sims_split = sem("sims_split")
        int_ready = sem("int_ready")
        stored = sem("stored")

        loads = {"wq1": 1, "wk1": 1, "wv1": 1, "ctx": 1, "bc": 1, "wq2": 1, "wk2": 1, "wv2": 1, "bf1": 1, "bq3": 1,
                 "bk3": 1, "sims": 2, "gates": 2, "wf1": 1, "wf2": 1, "wt": 1, "lora": 4, "w1": 1, "w2": 1,
                 "wq3": 1, "wk3": 1, "wv3": 1, "wqkv": 1, "wo": 1, "masks": 2}
        load_sem = {name: sem("ld_" + name) for name in loads}

        def load(eng, name, dst, src):
            eng.dma_start(dst, src).then_inc(load_sem[name], 16)

        def loaded(eng, name):
            eng.wait_ge(load_sem[name], 16 * loads[name])

        last_use = {}
        uses = {}
        full_count = [0] * 8
        free_count = [0] * 8

        def claim(key, banks, readers=1, signals=1):
            waits = {}
            for k in banks:
                if k in last_use:
                    first, count = last_use[k]
                    waits[first] = max(waits.get(first, 0), count)
            for first, count in waits.items():
                nc.tensor.wait_ge(bank_free[first], count)
            full_count[banks[0]] += signals
            free_count[banks[0]] += readers
            for k in banks:
                last_use[k] = (banks[0], free_count[banks[0]])
            uses[key] = (banks[0], full_count[banks[0]], free_count[banks[0]])

        def filled(ins, key):
            ins.then_inc(bank_full[uses[key][0]], 1)

        def arrived(eng, key):
            eng.wait_ge(bank_full[uses[key][0]], uses[key][1])

        def released(ins, key):
            ins.then_inc(bank_free[uses[key][0]], 1)

        def drained(eng, key):
            eng.wait_ge(bank_free[uses[key][0]], uses[key][2])

        def ln_count(name, i):
            return 4 * NORMS.index((name, i // 4)) + i % 4 + 1

        def chunk_at(u, first, every):
            c, rest = divmod(u - first, every)
            return c if rest == 0 and 0 <= c < 4 else None

        block = ctx.enter_context(nc.Block())

        @block.tensor
        def _(pe):
            def mm(o, lhsT, rhs, start=True, stop=True, **kw):
                return nc.tensor.matmul(o, lhsT, rhs, start=start, stop=stop, **kw)

            def mm3(o, lhs, rhs, pieces=KC):
                terms = [(k, l, r) for k in range(pieces) for l, r in ((0, 0), (0, 1), (1, 0))]
                for n, (k, l, r) in enumerate(terms):
                    ins = mm(o, lhs(l, k), rhs(r, k), start=n == 0, stop=n == len(terms) - 1)
                return ins

            def turn(name, norm, src, c, banks=(0, 1)):
                for i in range(4 * c, 4 * c + 4):
                    bank = banks[i % 2]
                    claim((name, i), [bank])
                    pe.wait_ge(ln_ready, ln_count(norm, i))
                    for k in range(KC):
                        ins = nc.tensor.transpose(PS[:, bank, P * k:P * k + P], src[:, i, P * k:P * k + P], ident[:, :])
                    filled(ins, (name, i))

            def turned(name, c):
                for i in range(4 * c, 4 * c + 4):
                    drained(pe, (name, i))

            def qk_transposes(i):
                claim(("qk1", i), [2 + i % 2])
                drained(pe, ("qkv", i, EXPERTS - 1))
                for w in range(2):
                    ins = nc.tensor.transpose(PS[:, 2 + i % 2, P * w:P * w + P], QKV[:, i, P * w:P * w + P], ident[:, :])
                filled(ins, ("qk1", i))

            pe.wait_ge(consts, 1)
            def project(b, step):
                banks = ((2, 3, 4, 5, 6, 7), (6, 7, 4, 5))[b]
                if step == 0:
                    for c in (2 * b, 2 * b + 1):
                        turn("t_in", "in", H, c, ((0, 1), (4, 5))[b])
                    for c in (2 * b, 2 * b + 1):
                        turned("t_in", c)
                if step < 8:
                    g, w, c = step // 4, step // 2 % 2, step % 2
                    loaded(pe, ("wq1", "wk1")[w])
                    bank = banks[step % len(banks)]
                    key = ("qk", b, g, w, c)
                    claim(key, [bank])
                    for k in range(KC):
                        ins = mm(PS[:, bank, :], w6(w)[:, k, P * g:P * g + P],
                                 TR[:, k, S * b + 512 * c:S * b + 512 * c + 512], start=k == 0, stop=k == KC - 1)
                    filled(ins, key)
                elif step > 8:
                    loaded(pe, "wv1")
                    for m in (2 * step - 18, 2 * step - 17):
                        i = TPB * b + m
                        bank = banks[(8 + m) % len(banks)]
                        claim(("v1", i), [bank])
                        for k in range(KC):
                            ins = mm(PS[:, bank, 0:D], TR[:, k, P * i:P * i + P], w6(2)[:, k, :], start=k == 0, stop=k == KC - 1)
                        filled(ins, ("v1", i))

            for step in range(PROJ_STEPS):
                project(0, step)

            def context(layer, wk):
                loaded(pe, wk[1])
                loaded(pe, "ctx")
                for g in range(2):
                    claim(("kx", layer, g), [4 + g])
                    for k in range(KC):
                        ins = mm(PS[:, 4 + g, 0:B * T], wk[0][:, k, P * g:P * g + P], ctxT[:, k, :], start=k == 0, stop=k == KC - 1)
                    filled(ins, ("kx", layer, g))

            def queries(layer, wq, c):
                loaded(pe, wq[1])
                for g in range(2):
                    key = ("q", layer, c, g)
                    claim(key, [4 + g])
                    for k in range(KC):
                        ins = mm(PS[:, 4 + g, :], wq[0][:, k, P * g:P * g + P],
                                 TR[:, k, 512 * c:512 * c + 512], start=k == 0, stop=k == KC - 1)
                    filled(ins, key)

            def gate_input(n, u, first, every):
                for m in range(4):
                    c = chunk_at(u, first + m, every)
                    if c is not None:
                        i = 4 * c + m
                        key = (("t_n1", "t_n2")[n], i)
                        bank = 4 + i % 2
                        if n:
                            bank = (7 if m else 4) if u < TILES + 2 else 4 - 2 * (u % 2)
                        claim(key, [bank])
                        pe.wait_ge(ln_ready, ln_count(("n1", "n2")[n], i))
                        for k in range(KC):
                            ins = nc.tensor.transpose(PS[:, bank, P * k:P * k + P], NBX[:, c % 2, m, P * k:P * k + P], ident[:, :])
                        filled(ins, key)
                c = chunk_at(u, first + 4, every)
                if c is not None:
                    pe.wait_ge(lower_ready, TILES * n + 4 * c + 4)
                    bank = 5 if c < 2 else 0
                    if n:
                        bank = 7 if u < TILES + 2 else 5 - 2 * (u % 2)
                    claim(("lg", n, c), [bank])
                    for m in range(4):
                        i = 4 * c + m
                        ins = mm3(PS[:, bank, EXPERTS * m:EXPERTS * m + EXPERTS], lambda w, k: TRP[n][w][:, k, P * i:P * i + P],
                                  lambda w, k: simparts[:, w, n, k, :])
                    filled(ins, ("lg", n, c))

            def gate_columns():
                pe.wait_ge(sim_ready, 1)
                claim("simsum", [7])
                for n in range(2):
                    for k in range(KC):
                        ins = mm(PS[:, 7, EXPERTS * n:EXPERTS * n + EXPERTS], ones, simsq[:, n, k, :],
                                 start=k == 0, stop=k == KC - 1)
                filled(ins, "simsum")

            turn_of = [0]

            def wide(n):
                first = turn_of[0] + (n - 1) * (turn_of[0] % 2)
                first %= 4
                turn_of[0] = (first + n) % 4
                return first

            narrow = 0
            pe.wait_ge(consts, 2)
            for op, n, *at in attention_plan():
                slot, b = n % SLOTS, n // 4
                if op == "project":
                    project(1, *at)
                elif op == "max":
                    j, st = at
                    if (j, st) == (0, 0):
                        pe.wait_ge(pack_in[slot], 12 * 16 * (n // SLOTS + 1))
                    need = st // 4 + 1
                    first = wide(need)
                    claim(("max", n, j, st), list(range(first, first + need)))
                    for c in range(st // 4 + 1):
                        cols = min(512, P * (st + 1) - 512 * c)
                        diag = c == st // 4
                        ins = mm(PS[:, first + c, 0:cols], PACKQ[slot][0:ROWS, j, P * st:P * st + P],
                                 PACKK[slot][0:ROWS, j, 512 * c:512 * c + cols], stop=not diag)
                        if diag:
                            ins = mm(PS[:, first + c, cols - P:cols], identb[:, :], maskq[:, :], start=False)
                    filled(ins, ("max", n, j, st))
                elif op == "neg":
                    first = wide(1)
                    claim(("neg", n), [first])
                    drained(pe, ("max", n, GRP - 1, ROW_ORDER[-1]))
                    filled(nc.tensor.transpose(PS[0:GRP * TPB, first, 0:P], negm[:, n % 2, :], ident[:, :]), ("neg", n))
                    if n == 0:
                        gate_columns()
                elif op == "score":
                    tt, c, j = at
                    if (tt, c, j) == (0, 0, 0):
                        pe.wait_ge(mrows_in[slot], 3 * 16 * (n // SLOTS + 1))
                    lo = max(P * tt, 512 * c)
                    w = 512 * c + 512 - lo
                    bank = 4 + narrow
                    claim(("score", n, tt, c, j), [bank])
                    ins = mm(PS[:, bank, 0:w], PACKK[slot][0:ROWS + 3, j, P * tt:P * tt + P],
                             PACKQ[slot][0:ROWS + 3, j, lo:lo + w])
                    filled(ins, ("score", n, tt, c, j))
                    narrow = 1 - narrow
                elif op == "pv":
                    tt, c = at
                    if (tt, c) == (0, 0):
                        claim(("values", n), [6, 7], signals=0)
                        for i in (TPB * b + TPB - 2, TPB * b + TPB - 1):
                            drained(pe, ("v1", i))
                    lo = max(P * tt, 512 * c)
                    w = 512 * c + 512 - lo
                    drained(pe, ("score", n, tt, c, GRP - 1))
                    if c == tt // 4:
                        pe.wait_ge(cleared, GRP * (TPB * n + tt + 1))
                    for j in range(GRP):
                        ins = mm(PS[32 * j:32 * j + VW, 6 + c, lo - 512 * c:512],
                                 VEXT[:, TPB * b + tt, GRP * (n % 4) + j, :],
                                 PROB[GRP * (STEPS.index((tt, c)) % 2) + j][:, 0:w], start=tt == 0, stop=tt == 4 * c + 3)
                    ins.then_inc(pv_done, 1)
                elif op == "turn":
                    pe.wait_ge(ln_ready, ln_count("g1", 4 * n + 3))
                    first = wide(2)
                    claim(("turn", n), [first, first + 1])
                    for i in range(4):
                        for k in range(KC):
                            col = P * (2 * (i % 2) + k)
                            ins = nc.tensor.transpose(PS[:, first + i // 2, col:col + P],
                                                      H[:, 4 * n + i, P * k:P * k + P], ident[:, :])
                    filled(ins, ("turn", n))
                elif op == "out":
                    if n == GROUPS - 1:
                        context(0, (w6(4), "wk2"))
                        queries(0, (w6(3), "wq2"), 0)
                    drained(pe, ("values", n))
                    first = wide(2)
                    claim(("out", n), [first, first + 1])
                    for st in range(TPB):
                        ins = nc.tensor.transpose(PS[:, first + st // 4, P * (st % 4):P * (st % 4) + P],
                                                  OTS[:, P * st:P * st + P], ident[:, :])
                    filled(ins, ("out", n))

            def low_rank(u):
                bank = 6 + (u // 2) % 2
                if u == 12:
                    loaded(pe, "lora")
                    claim("l1", [bank])
                    filled(mm(PS[0:4, bank, 0:D], LDT, DAUX), "l1")
                elif u == 16:
                    drained(pe, "l1")
                    claim("l2", [bank])
                    filled(mm(PS[0:50, bank, 0:D], LUT, LD1), "l2")
                elif u == 20:
                    drained(pe, "l2")
                    claim("l3", [bank])
                    for k in range(KC):
                        ins = mm(PS[:, bank, D * k:D * k + D], LD2[:, P * k:P * k + P], UPT)
                    filled(ins, "l3")

            def cross(layer):
                pe.wait_ge(kv_ready, 2 * B * (layer + 1))

                def scores(u):
                    i, g = u // 2, u % 2
                    for m in range(2):
                        drained(pe, ("q", layer, i // 4, m))
                    claim(("sx", layer, u), [2 * g, 2 * g + 1])
                    for m in range(2):
                        ins = mm(PS[:, 2 * g + m, 0:4 * T], QT[:, g, P * i:P * i + P], KBD[:, i // TPB, g, 4 * m:4 * m + 4, :])
                    filled(ins, ("sx", layer, u))

                def context_values():
                    wv = W3[:, 1, :, :] if layer else w6(5)
                    loaded(pe, "wv3" if layer else "wv2")
                    for b in range(B):
                        pe.wait_ge(crep_ready, B * layer + b + 1)
                        crep = CREP[layer][b].rearrange("p k h t -> p k (h t)")
                        for j, (lo, rows) in enumerate(PIECES):
                            h0, h1 = PIECE_HEADS[j]
                            key = ("vx", layer, b, j)
                            bank = 6 + (len(PIECES) * b + j) % 2
                            claim(key, [bank])
                            for k in range(KC):
                                ins = mm(PS[0:rows, bank, 0:2 * HD * (h1 - h0)].rearrange("p (g f) -> p g f", g=2), crep[:, k, lo:lo + rows],
                                         wv[:, k, :].rearrange("p (g f) -> p g f", g=2)[:, :, HD * h0:HD * h1],
                                         start=k == 0, stop=k == KC - 1)
                            filled(ins, key)

                def next_queries(u):
                    c, step = (u + 2) // 8 + 1, (u + 2) % 8
                    if c in (2, 3) and 2 <= step < 6:
                        i = 4 * c + step - 2
                        claim(("t_g1", i), [4 + i % 2])
                        pe.wait_ge(ln_ready, ln_count("g1", i))
                        for k in range(KC):
                            ins = nc.tensor.transpose(PS[:, 4 + i % 2, P * k:P * k + P], H[:, i, P * k:P * k + P], ident[:, :])
                        filled(ins, ("t_g1", i))
                    if c < 4 and step == 6:
                        if c == 1:
                            drained(pe, ("turn", 1))
                        else:
                            turned("t_g1", c)
                        queries(0, (w6(3), "wq2"), c)

                def turn_probs(u):
                    pe.wait_ge(ex_ready, UNITS * layer + u + 1)
                    ex = EX[u % 4].rearrange("p h t -> p (h t)")
                    for m in range(2):
                        claim(("px", layer, u, m), [4 + m])
                        for j, (lo, rows) in list(enumerate(PIECES))[4 * m:4 * m + 4]:
                            col = P * (j % 4)
                            ins = nc.tensor.transpose(PS[0:rows, 4 + m, col:col + P], ex[:, lo:lo + rows], ident[:, :])
                        filled(ins, ("px", layer, u, m))

                def values(u):
                    t, g = u // 2, u % 2
                    if g == 0:
                        claim(("ox", layer, t), [6 + t % 2])
                    if u == 0:
                        pe.wait_ge(vx_ready, B * len(PIECES) * (layer + 1))
                    drained(pe, ("px", layer, u, 0))
                    drained(pe, ("px", layer, u, 1))
                    for j, (lo, rows) in enumerate(PIECES):
                        ins = mm(PS[:, 6 + t % 2, VW * HH * g:VW * HH * (g + 1)], PTS[u % 4][0:rows, j, :],
                                 VBD[0:rows, t // TPB, g, j, :, :], start=j == 0, stop=j == len(PIECES) - 1)
                    if g == 1:
                        filled(ins, ("ox", layer, t))

                for u in range(-2, UNITS + 1):
                    if u + 2 < UNITS:
                        scores(u + 2)
                    if u == -1:
                        context_values()
                    if layer == 0:
                        next_queries(u)
                    else:
                        gate_input(0, u - 1, 15, 8)
                    if u >= 1:
                        values(u - 1)
                    if 0 <= u < UNITS:
                        turn_probs(u)
                    if layer == 0:
                        low_rank(u)

            cross(0)

            pe.wait_ge(wf1_split, 4)
            turn("t_g2", "g2", H, 0)
            for s in range(6):
                if s < 4:
                    pe.wait_ge(trg_ready, 4 * s + 4)
                    for f in range(FCH):
                        key = ("f1", s, f)
                        claim(key, [2 + f % 4])
                        trg = (TRR[:, :, 512 * s:512 * s + 512], TRG[s % 2])
                        filled(mm3(PS[:, 2 + f % 4, :], lambda w, k: WF1P[w][:, k, P * f:P * f + P], lambda w, k: trg[w][:, k, :]), key)
                if s > 1:
                    turned("t_xat", s - 2)
                    queries(1, (w6(5), "wq3"), s - 2)
                if 0 < s < 5:
                    turn("t_lin", "lin", H, s - 1)
                if s < 3:
                    turn("t_g2", "g2", H, s + 1)
                if 0 < s < 5:
                    turned("t_lin", s - 1)
                    drained(pe, "l3")
                    for i in range(4 * s - 4, 4 * s):
                        claim(("lin", i), [2 + i % 4])
                        for k in range(KC):
                            ins = mm(PS[:, 2 + i % 4, 0:D], TR[:, k, P * i:P * i + P], WEFF[:, k, :], start=k == 0, stop=k == KC - 1)
                        filled(ins, ("lin", i))
                if s < 4:
                    pe.wait_ge(ht_ready, FCH * (s + 1))
                    pe.wait_ge(wf2_split, 4)
                    for i in range(4 * s, 4 * s + 4):
                        claim(("f2", i), [6 + i % 2])
                        filled(mm3(PS[:, 6 + i % 2, 0:D], lambda w, f: HT[w][:, f, P * (i % 4):P * (i % 4) + P],
                                   lambda w, f: WF2P[w][:, f, :], FCH), ("f2", i))
                if s == 4:
                    context(1, (W3[:, 0, :, :], "wk3"))
                if 0 < s < 5:
                    turn("t_xat", "xat", H, s - 1)
            cross(1)
            for u in range(UNITS, UNITS + 3):
                gate_input(0, u, 15, 8)

            for i in range(TILES):
                for e in range(EXPERTS):
                    bank = 4 + (EXPERTS * i + e) % 4
                    key = ("qkv", i, e)
                    claim(key, [bank])
                    if i == 0:
                        pe.wait_ge(wqkv_split, e + 1)
                    filled(mm3(PS[:, bank, 0:3 * HA], lambda w, k: TRP[0][w][:, k, P * i:P * i + P],
                               lambda w, k: WQKVP[w][:, k, e, :]), key)
                gate_input(0, UNITS + 3 + i, 15, 8)
                if i > 0:
                    qk_transposes(i - 1)
            qk_transposes(TILES - 1)
            loaded(pe, "wo")
            def row_scores(i):
                b, st = i // TPB, i % TPB
                drained(pe, ("qk1", i))
                claim(("s1", i), [0, 1])
                for c in range(st // 4 + 1):
                    cols = min(512, P * (st + 1) - 512 * c)
                    diag = c == st // 4
                    ins = mm(PS[:, c, 0:cols], QK1[:, 0, P * i:P * i + P],
                             QK1[:, 1, S * b + 512 * c:S * b + 512 * c + cols], stop=not diag)
                    if diag:
                        ins = mm(PS[:, c, cols - P:cols], identb[:, :], maskq[:, :], start=False)
                filled(ins, ("s1", i))

            row_scores(0)
            for i in range(TILES + 2):
                if i + 1 < TILES:
                    row_scores(i + 1)
                if 0 < i <= TILES:
                    t = i - 1
                    drained(pe, ("a1", t))
                    claim(("at", t), [5, 6])
                    for e in range(EXPERTS):
                        ins = nc.tensor.transpose(PS[:, 5 + e // 4, P * (e % 4):P * (e % 4) + P], ATT[:, e, :], ident[:, :])
                    filled(ins, ("at", t))
                if i < TILES:
                    drained(pe, ("s1", i))
                    claim(("p1", i), [2, 3])
                    for tt in range(i % TPB + 1):
                        ins = nc.tensor.transpose(PS[:, 2 + tt // 4, P * (tt % 4):P * (tt % 4) + P],
                                                  P1[i % 2][:, P * tt:P * tt + P], ident[:, :])
                    filled(ins, ("p1", i))
                if i > 1:
                    t = i - 2
                    drained(pe, ("at", t))
                    claim(("o1", t), [7])
                    for e in range(EXPERTS):
                        ins = mm(PS[:, 7, 0:D], ATTT[:, e // 4, P * (e % 4):P * (e % 4) + P], WO[:, e, :], start=e == 0, stop=e == EXPERTS - 1)
                    filled(ins, ("o1", t))
                if i < TILES:
                    claim(("a1", i), [4])
                    drained(pe, ("p1", i))
                    for tt in range(i % TPB + 1):
                        ins = mm(PS[:, 4, 0:HA], PT1[:, tt, :], QKV[:, TPB * (i // TPB) + tt, 2 * HA:3 * HA],
                                 start=tt == 0, stop=tt == i % TPB)
                    filled(ins, ("a1", i))
                gate_input(1, i, 8, 4)
            for n in range(4 * EXPERTS + 2):
                if n < 4 * EXPERTS:
                    c, e = n // EXPERTS, n % EXPERTS
                    if c == 0:
                        pe.wait_ge(w1_split, e + 1)
                    for ic in range(2):
                        key = ("m1", n, ic)
                        bank = 2 + (2 * n + ic) % 4
                        claim(key, [bank])
                        filled(mm3(PS[:, bank, :], lambda w, k: W1P[w][:, k, e, P * ic:P * ic + P],
                                   lambda w, k: TRP[1][w][:, k, 512 * c:512 * c + 512]), key)
                if n >= 2:
                    c, e = (n - 2) // EXPERTS, (n - 2) % EXPERTS
                    if c == 0:
                        pe.wait_ge(w2_split, e + 1)
                    pe.wait_ge(int_ready, 2 * (n - 1))
                    for m in range(4):
                        key = ("m2", n - 2, m)
                        bank = (0, 1, 6, 7)[m]
                        claim(key, [bank])
                        filled(mm3(PS[:, bank, 0:D], lambda w, k: INT[(n - 2) % 4][:, w, k, P * m:P * m + P],
                                   lambda w, k: W2P[w][:, e, k, :]), key)
                gate_input(1, TILES + 2 + n, 8, 4)

        @block.sync
        def _(sp):
            def wload(name, dst, key, pattern="(k p) f -> p k f", **kw):
                load(sp, name, dst, a[key].rearrange(pattern, **kw))

            xd = a["x"].rearrange("(i p) d -> p i d", p=P)
            for k in range(4):
                sp.dma_start(X[:, 4 * k:4 * k + 4, :], xd[:, 4 * k:4 * k + 4, :]).then_inc(x_in[k], 16)
                if k == 0:
                    wload("wq1", w6(0), "wq1", p=P)
                    wload("wk1", w6(1), "wk1", p=P)
            load(sp, "ctx", ctxT[:, :, :], a["ctxT"].rearrange("(k p) t -> p k t", p=P))
            wload("wv1", w6(2), "wv1", p=P)
            load(sp, "bc", BC[:, :, :], a["bcast"].rearrange("(o n) d -> o n d", o=1).broadcast_to([P, len(BCAST), D]))
            for n, name in enumerate(("wq2", "wk2", "wv2")):
                wload(name, w6(3 + n), name, p=P)
            load(sp, "bf1", bf1c[:, :], a["bf1"])
            load(sp, "bq3", bq3c[:, :], a["bq3"])
            load(sp, "bk3", bk3c[:, :], a["bk3"])
            for n, name in enumerate(("sim1", "sim2")):
                load(sp, "sims", sims[:, n, :, :], a[name].rearrange("(k p) e -> p k e", p=P))
            for n, name in enumerate(("gates1", "gates2")):
                load(sp, "gates", gates[:, n, :],
                     a[name].rearrange("(o e) -> o e", o=1).broadcast_to([P, EXPERTS]))

            def load_pack(n):
                b, h0 = n // 4, GRP * (n % 4)
                for w, packs, order in ((0, PACKQ, QPART), (1, PACKK, KPART)):
                    src = scratch[b, w].rearrange("(h e) c s -> c e h s", h=HEADS)
                    for r, part in enumerate(order):
                        sp.dma_start(packs[n % SLOTS][HD * r:HD * r + HD, :, :],
                                     src[part, :, h0:h0 + GRP, :]).then_inc(pack_in[n % SLOTS], 16)

            for u in range(8):
                b, g, w = u // 4, u // 2 % 2, u % 2
                sp.wait_ge(parts_ready, 2 * (u + 1))
                sp.dma_start(scratch[b, w, P * g:P * g + P, :, :], PARTS[u % 4]).then_inc(parts_out[u], 16)
                if u == 1:
                    for v in (0, 1):
                        sp.wait_ge(parts_out[v], 16)
                    load_pack(0)
                    load_pack(1)
            for v in range(2, 8):
                sp.wait_ge(parts_out[v], 16)
            load_pack(2)

            for n in range(GROUPS):
                sp.wait_ge(mparts_ready, n + 1)
                for r in range(3):
                    sp.dma_start(PACKQ[n % SLOTS][ROWS + r:ROWS + r + 1, :, :].rearrange("o j (t s) -> o (j t) s", s=P),
                                 mparts[:, n % 2, r, :]).then_inc(mrows_in[n % SLOTS], 16)
                if 1 <= n < GROUPS - 2:
                    arrived(sp, ("score", n - 1, TPB - 1, 1, GRP - 1))
                    load_pack(n + 2)

            sp.wait_ge(sa_used, 4)
            load(sp, "lora", DAUX, a["daux"])
            load(sp, "lora", UPT, a["upT"])
            load(sp, "lora", LDT, a["ldT"])
            load(sp, "lora", LUT, a["luT"])
            wload("wt", WEFF, "wt", p=P)
            wload("wf1", WF1, "wf1", p=P)
            for n, name in enumerate(("wk3", "wv3")):
                wload(name, W3[:, n, :, :], name, p=P)
            arrived(sp, ("vx", 0, B - 1, len(PIECES) - 1))
            wload("wq3", w6(5), "wq3", p=P)
            arrived(sp, ("ox", 0, TILES - 1))
            wload("wf2", WF2, "wf2", "(f p) d -> p f d", p=P)
            load(sp, "masks", MASKS, a["mask_st"].rearrange("(i p) t -> p i t", p=P))
            load(sp, "masks", MASKB,
                 a["mask_bt"].rearrange("(o b) t -> o b t", o=1).broadcast_to([P, B, T]))
            drained(sp, ("lin", TILES - 1))
            arrived(sp, ("vx", 1, B - 1, len(PIECES) - 1))
            sp.wait_ge(kv_ready, 2 * B * 2)
            load(sp, "wqkv", WQKV, a["wqkv"].rearrange("(k p) e f -> p k e f", p=P))
            wload("wo", WO, "wo", "e p f -> p e f")
            arrived(sp, ("qkv", TILES - 1, EXPERTS - 1))
            load(sp, "w1", W1, a["w1"].rearrange("(k p) e f -> p k e f", p=P))
            load(sp, "w2", W2, a["w2"].rearrange("(m p) f -> p m f", p=P).rearrange("p (e k) f -> p e k f", k=KC))

            od = out.rearrange("(i p) d -> p i d", p=P)
            for c in range(8):
                for m in (2 * c % 4, 2 * c % 4 + 1):
                    drained(sp, ("m2", EXPERTS * (c // 2) + EXPERTS - 1, m))
                sp.dma_start(od[:, 2 * c:2 * c + 2, :], X[:, 2 * c:2 * c + 2, :]).then_inc(stored, 16)
            sp.wait_ge(stored, 16 * 8)

        @block.scalar
        def _(act):
            def evacuate(name, c):
                for i in range(4 * c, 4 * c + 4):
                    evacuate_tile(name, i)

            def evacuate_tile(name, i):
                arrived(act, (name, i))
                released(nc.scalar.copy(TR[:, :, P * i:P * i + P],
                                        PS[:, uses[(name, i)][0], 0:D].rearrange("p (k s) -> p k s", k=KC)), (name, i))

            def gate_input(n, u, first, every):
                for m in range(4):
                    c = chunk_at(u, first + m, every)
                    if c is not None:
                        i = 4 * c + m
                        key = (("t_n1", "t_n2")[n], i)
                        arrived(act, key)
                        if TILES * n + i >= 4:
                            act.wait_ge(lower_ready, TILES * n + 4 * c)
                        src = PS[:, uses[key][0], 0:D].rearrange("p (k s) -> p k s", k=KC)
                        nc.scalar.copy(TRP[n][0][:, :, P * i:P * i + P], src)
                        released(nc.scalar.copy(TRF[:, m], src), key)
                c = chunk_at(u, first, every)
                if c is not None:
                    for i in range(4 * c, 4 * c + 4):
                        act.wait_ge(ln_ready, ln_count(("n1", "n2")[n], i))
                        if TILES * n + i >= 2:
                            act.wait_ge(ss_ready, TILES * n + i - 1)
                        nc.scalar.activation(SQ[:, i % 2, :], NBX[:, c % 2, i % 4, :], ACT.Square, accum_out=ss[:, i:i + 1]).then_inc(ss_ready, 1)

            def gate_exponentials(n, u, first, every):
                c = chunk_at(u, first + 5, every)
                if c is not None:
                    act.wait_ge(gate_in, 4 * n + c + 1)
                    nc.scalar.activation(LG[:, 5, :], LG[:, 4, :], ACT.Exp).then_inc(gate_exp, 1)

            def project(b, step):
                if step == 0:
                    for c in (2 * b, 2 * b + 1):
                        evacuate("t_in", c)
                if step < 8:
                    u = 8 * b + step
                    key = ("qk", b, step // 4, step // 2 % 2, step % 2)
                    arrived(act, key)
                    if u >= 8:
                        act.wait_ge(parts_out[u // 2 - 4], 16)
                    nc.scalar.copy(PARTS[u // 2 % 4][:, 0, 512 * (u % 2):512 * (u % 2) + 512],
                                   PS[:, uses[key][0], :]).then_inc(hi_ready, 1)
                if 0 < step < 9:
                    v = 8 * b + step - 1
                    drained(act, ("qk", b, (step - 1) // 4, (step - 1) // 2 % 2, (step - 1) % 2))
                    nc.scalar.copy(PARTS[v // 2 % 4][:, 1, 512 * (v % 2):512 * (v % 2) + 512],
                                   REST[v % 3]).then_inc(mid_ready, 1)

            for step in range(PROJ_STEPS):
                project(0, step)

            loaded(act, "gates")
            nc.scalar.activation(gates[:, :, :], gates[:, :, :], ACT.Exp, scale=-1.0).then_inc(sig_ready, 1)

            step_exp = 0
            for op, n, *at in attention_plan():
                if op == "project":
                    project(1, *at)
                elif op == "score":
                    tt, c, j = at
                    key = ("score", n, tt, c, j)
                    w = 512 * c + 512 - max(P * tt, 512 * c)
                    step = step_exp // GRP
                    arrived(act, key)
                    if step >= 2:
                        act.wait_ge(pv_done, step - 1)
                    ins = nc.scalar.activation(PROB[GRP * (step % 2) + j][:, 0:w], PS[:, uses[key][0], 0:w], ACT.Exp,
                                               scale=HD ** -0.5)
                    released(ins, key)
                    step_exp += 1
                elif op == "turn":
                    arrived(act, ("turn", n))
                    bank = uses[("turn", n)][0]
                    ins = nc.scalar.copy(TR[:, :, 512 * n:512 * n + 512].rearrange("p k (i s) -> p i k s", i=4),
                                         PS[:, bank:bank + 2, :].rearrange("p b (i k s) -> p (b i) k s", i=2, k=KC))
                    released(ins, ("turn", n))
                elif op == "evac":
                    act.wait_ge(pv_done, len(STEPS) * (n + 1))
                    if n > 0:
                        arrived(act, ("out", n - 1))
                    ins = nc.scalar.copy(OTS, PS[:, 6:8, :].rearrange("p b s -> p (b s)"))
                    released(ins, ("values", n))

            def context(layer):
                for g in range(2):
                    arrived(act, ("kx", layer, g))
                    if layer == 0:
                        ins = nc.scalar.copy(KTX[:, g, :], PS[:, 4 + g, 0:B * T])
                    else:
                        ins = nc.scalar.activation(KTX[:, g, :], PS[:, 4 + g, 0:B * T], ACT.Identity, bias=bk3c[:, g:g + 1])
                    released(ins, ("kx", layer, g))

            def queries(layer, c):
                for g in range(2):
                    key = ("q", layer, c, g)
                    arrived(act, key)
                    src, dst = PS[:, 4 + g, :], QT[:, g, 512 * c:512 * c + 512]
                    if layer == 0:
                        ins = nc.scalar.copy(dst, src)
                    else:
                        ins = nc.scalar.activation(dst, src, ACT.Identity, bias=bq3c[:, g:g + 1])
                    released(ins, key)

            def cross(layer):
                for u in range(-2, UNITS + 1):
                    if layer:
                        gate_exponentials(0, u - 1, 15, 8)
                    if 0 <= u < UNITS:
                        if layer:
                            act.wait_ge(shift_ready, u + 1)
                        else:
                            drained(act, ("sx", 0, u))
                        nc.scalar.activation(EX[u % 4], EX[u % 4], ACT.Exp, scale=HD ** -0.5).then_inc(ex_ready, 1)
                    if layer and 4 <= u < 4 + 3 * EXPERTS and (u - 4) % 3 == 0:
                        e = (u - 4) // 3
                        loaded(act, "wqkv")
                        nc.scalar.copy(WQKVP[0][:, :, e, :], WQKV[:, :, e, :]).then_inc(wqkv_upper, 1)
                    if u >= 1:
                        if u >= 5:
                            arrived(act, ("ox", layer, (u - 5) // 2))
                        for m in range(2):
                            key = ("px", layer, u - 1, m)
                            arrived(act, key)
                            rows, cols = ((P, 4), (PIECES[4][1], 1))[m]
                            released(nc.scalar.copy(PTS[(u - 1) % 4][0:rows, 4 * m:4 * m + cols, :],
                                                    PS[0:rows, 4 + m, 0:P * cols].rearrange("p (j s) -> p j s", s=P)), key)
                    c, step = (u + 2) // 8 + 1, (u + 2) % 8
                    if layer == 0 and c in (2, 3) and 2 <= step < 6:
                        evacuate_tile("t_g1", 4 * c + step - 2)
                    if layer == 0 and c < 4 and step == 6:
                        queries(0, c)
                    if layer:
                        gate_input(0, u - 1, 15, 8)

            context(0)
            queries(0, 0)
            cross(0)
            loaded(act, "bf1")
            loaded(act, "bq3")
            loaded(act, "bk3")
            def evacuate_parts(c):
                for i in range(4 * c, 4 * c + 4):
                    key = ("t_g2", i)
                    arrived(act, key)
                    if c > 0:
                        act.wait_ge(trg_ready, 4 * c)
                    src = PS[:, uses[key][0], 0:D].rearrange("p (k s) -> p k s", k=KC)
                    nc.scalar.copy(TRR[:, :, P * i:P * i + P], src)
                    released(nc.scalar.copy(TRGF[:, i % 4], src), key)

            evacuate_parts(0)
            for s in range(6):
                if s < 4:
                    if s > 0:
                        arrived(act, ("f2", 4 * s - 1))
                    for f in range(FCH):
                        key = ("f1", s, f)
                        arrived(act, key)
                        if FCH * s + f >= 4:
                            act.wait_ge(ht_ready, FCH * s + f - 3)
                        src, bias = PS[:, 2 + f % 4, :], bf1c[:, f:f + 1]
                        nc.scalar.activation(HTF[f % 4], src, ACT.Relu, bias=bias)
                        released(nc.scalar.activation(HT[0][:, f, :], src, ACT.Relu, bias=bias), key)
                if s > 1:
                    queries(1, s - 2)
                if 0 < s < 5:
                    evacuate("t_lin", s - 1)
                if s < 3:
                    evacuate_parts(s + 1)
                if s == 4:
                    context(1)
                if 0 < s < 5:
                    evacuate("t_xat", s - 1)
            cross(1)

            for u in range(UNITS, UNITS + 3):
                gate_exponentials(0, u, 15, 8)
                gate_input(0, u, 15, 8)
            for i in range(TILES + 1):
                gate_exponentials(0, UNITS + 3 + i, 15, 8)
                gate_input(0, UNITS + 3 + i, 15, 8)
                if i > 0:
                    t = i - 1
                    arrived(act, ("qk1", t))
                    released(nc.scalar.copy(QK1[:, :, P * t:P * t + P], PS[:, 2 + t % 2, 0:2 * P].rearrange("p (w s) -> p w s", w=2)), ("qk1", t))

            def row_probs(i):
                cols = P * (i % TPB + 1)
                act.wait_ge(bias_ready, i + 1)
                if i >= 2:
                    arrived(act, ("p1", i - 2))
                ins = nc.scalar.activation(P1[i % 2][:, 0:cols], PS[:, 0:2, :].rearrange("p b s -> p (b s)")[:, 0:cols], ACT.Exp,
                                           bias=l1s[:, i % 2, 0:1], scale=HA ** -0.5, accum_out=l1s[:, i % 2, 1:2])
                released(ins, ("s1", i))

            row_probs(0)
            for i in range(TILES + 2):
                gate_input(1, i - 1, 8, 4)
                gate_exponentials(1, i, 8, 4)
                if i < TILES:
                    arrived(act, ("p1", i))
                    if i > 0:
                        arrived(act, ("a1", i - 1))
                    cols = P * (i % TPB + 1)
                    released(nc.scalar.copy(PT1.rearrange("p t s -> p (t s)")[:, 0:cols],
                                            PS[:, 2:4, :].rearrange("p b s -> p (b s)")[:, 0:cols]), ("p1", i))
                if i + 1 < TILES:
                    row_probs(i + 1)
                if 0 < i <= TILES:
                    t = i - 1
                    arrived(act, ("at", t))
                    if t >= 1:
                        arrived(act, ("o1", t - 1))
                    released(nc.scalar.copy(ATTT, PS[:, 5:7, :]), ("at", t))
            gate_input(1, TILES + 1, 8, 4)
            for n in range(4 * EXPERTS):
                gate_exponentials(1, TILES + 2 + n, 8, 4)
                if n >= 4:
                    arrived(act, ("m2", n - 4, 3))
                for ic in range(2):
                    key = ("m1", n, ic)
                    arrived(act, key)
                    if n >= 2:
                        act.wait_ge(int_ready, 2 * (n - 2) + ic + 1)
                    src = PS[:, uses[key][0], :]
                    nc.scalar.activation(INTF[(2 * n + ic) % 4], src, ACT.Gelu)
                    released(nc.scalar.activation(INT[n % 4][:, 0, ic, :], src, ACT.Gelu), key)
                gate_input(1, TILES + 2 + n, 8, 4)

        @block.vector
        def _(dve):
            links = [0]

            def link(ins):
                links[0] += 1
                ins.then_inc(dve_chain, 1)
                dve.wait_ge(dve_chain, links[0])

            v = nc.vector
            norms = [0]

            def tile_of(dst, i):
                return NBX[:, i // 4 % 2, i % 4, :] if dst is NBX else dst[:, i, :]

            def layernorm(src, dst, tiles, scale=None, shift=None):
                statistics(src, tiles)
                if scale:
                    center(src, dst, tiles, scale)
                    divide_by_spread(dst, tiles, shift)
                else:
                    norms[0] += 1
                    dve.wait_ge(rstd_ready, norms[0])
                    for i in tiles:
                        v.tensor_scalar(dst[:, i, :], src[:, i, :], mv[:, i, 0:1], rstd[:, i:i + 1],
                                        ALU.subtract, ALU.mult).then_inc(ln_ready, 1)

            def statistics(src, tiles):
                for i in tiles:
                    ins = v.bn_stats(stats[:, i, :], src[:, i, :])
                link(ins)
                for i in tiles:
                    ins = v.bn_aggr(mv[:, i, :], stats[:, i, :])
                link(ins)
                v.tensor_scalar(var[:, tiles[0]:tiles[-1] + 1], mv[:, tiles[0]:tiles[-1] + 1, 1:2].rearrange("p i o -> p (i o)"),
                                EPS, None, ALU.add).then_inc(var_ready, 1)

            def center(src, dst, tiles, scale):
                for i in tiles:
                    ins = v.scalar_tensor_tensor(out=tile_of(dst, i), in0=src[:, i, :], scalar=mv[:, i, 0:1], in1=bc(scale),
                                                 op0=ALU.subtract, op1=ALU.mult)
                link(ins)

            def divide_by_spread(dst, tiles, shift):
                norms[0] += 1
                dve.wait_ge(rstd_ready, norms[0])
                for i in tiles:
                    v.scalar_tensor_tensor(out=tile_of(dst, i), in0=tile_of(dst, i), scalar=rstd[:, i:i + 1], in1=bc(shift),
                                           op0=ALU.mult, op1=ALU.add).then_inc(ln_ready, 1)

            batches = [list(range(4 * k, 4 * k + 4)) for k in range(4)]
            for k in range(4):
                dve.wait_ge(x_in[k], 16)
                layernorm(X, H, batches[k])

            loaded(dve, "bc")
            def project(b, step):
                if step < 8:
                    u = 8 * b + step
                    key = ("qk", b, step // 4, step // 2 % 2, step % 2)
                    dve.wait_ge(hi_ready, u + 1)
                    if u >= 3:
                        dve.wait_ge(parts_ready, u - 2)
                    released(v.tensor_tensor(REST[u % 3], PS[:, uses[key][0], :], PARTS[u // 2 % 4][:, 0, 512 * (u % 2):512 * (u % 2) + 512],
                                             ALU.subtract), key)
                if 0 < step < 9:
                    t = 8 * b + step - 1
                    part = PARTS[t // 2 % 4]
                    dve.wait_ge(mid_ready, t + 1)
                    drained(dve, ("qk", b, (step - 1) // 4, (step - 1) // 2 % 2, (step - 1) % 2))
                    v.tensor_tensor(part[:, 2, 512 * (t % 2):512 * (t % 2) + 512], REST[t % 3],
                                    part[:, 1, 512 * (t % 2):512 * (t % 2) + 512], ALU.subtract).then_inc(parts_ready, 1)
                if step > 8:
                    for i in (TPB * b + 2 * step - 18, TPB * b + 2 * step - 17):
                        arrived(dve, ("v1", i))
                        released(v.tensor_tensor(VEXT[:, i, :, 0:HD],
                                                 PS[:, uses[("v1", i)][0], 0:D].rearrange("p (h e) -> p h e", h=HEADS),
                                                 bc("bv1").rearrange("p (h e) -> p h e", h=HEADS), ALU.add), ("v1", i))

            for step in range(PROJ_STEPS):
                project(0, step)

            def context(layer):
                if layer == 1:
                    loaded(dve, "masks")
                    maskb = KEEPF[:, 0, :].unsqueeze(1)
                    for b in range(B):
                        link(v.tensor_scalar(KEEPF[:, 0, :], MASKB[:, b, :], 0.0, None, ALU.not_equal))
                        link(v.tensor_scalar(KEEPF[:, TPB:2 * TPB, :], MASKS, 0.0, None, ALU.not_equal))
                        link(v.tensor_tensor(KEEP[:, TPB * b:TPB * b + TPB, :], KEEPF[:, TPB:2 * TPB, :],
                                             maskb.broadcast_to([P, TPB, T]), ALU.mult))
                for g in range(2):
                    drained(dve, ("kx", layer, g))
                for b in range(B):
                    for g in range(2):
                        v.tensor_tensor(KBD[:, b, g, :, :],
                                        KTX[:, g, T * b:T * b + T].unsqueeze(1).broadcast_to([P, 8, T]),
                                        blockm[:, :].unsqueeze(2).broadcast_to([P, 8, T]), ALU.mult).then_inc(kv_ready, 1)

            def context_values(layer):
                bias = bc(("bv2", "bv3")[layer]).rearrange("p (g h e) -> p g h e", g=2, h=HH)
                if layer == 0:
                    dve.wait_ge(vbd_clear, 1)
                for b in range(B):
                    for j, (lo, rows) in enumerate(PIECES):
                        h0, h1 = PIECE_HEADS[j]
                        key = ("vx", layer, b, j)
                        arrived(dve, key)
                        src = PS[0:rows, uses[key][0], 0:2 * HD * (h1 - h0)].rearrange("p (g h e) -> p g h e", g=2, e=HD)
                        released(v.tensor_tensor(VBD[0:rows, b, :, j, h0:h1, 0:HD], src, bias[0:rows, :, h0:h1, :], ALU.add), key)
                for j in (len(PIECES) - 2, len(PIECES) - 1):
                    drained(dve, ("vx", layer, B - 1, j))
                for b in range(B):
                    for j, (lo, rows) in enumerate(PIECES):
                        h0, h1 = PIECE_HEADS[j]
                        part = VBD[0:rows, b, :, j, h0:h1, :]
                        v.tensor_tensor(part[:, :, :, 0:HD], part[:, :, :, 0:HD],
                                        part[:, :, :, HD:VW].broadcast_to([rows, 2, h1 - h0, HD]), ALU.mult).then_inc(vx_ready, 1)

            loaded(dve, "sims")
            v.tensor_tensor(simsq[:, :, :, :], sims[:, :, :, :], sims[:, :, :, :], ALU.mult).then_inc(sim_ready, 1)

            def unit_columns():
                dve.wait_ge(sim_sum, 1)
                link(v.tensor_scalar(siminv[:, :, :], siminv[:, :, :], 1e-12, None, ALU.max))
                link(v.reciprocal(siminv[:, :, :], siminv[:, :, :]))
                link(v.tensor_tensor(sims[:, :, :, :], sims[:, :, :, :],
                                     siminv[:, :, :].unsqueeze(2).broadcast_to([P, 2, KC, EXPERTS]), ALU.mult))
                v.tensor_copy(simparts[:, 0], sims[:, :, :, :]).then_inc(sims_split, 1)
                dve.wait_ge(sims_split, 1)
                v.tensor_tensor(simparts[:, 1], sims[:, :, :, :], simparts[:, 0].bitcast(F32), ALU.subtract).then_inc(sims_split, 1)
                dve.wait_ge(sig_ready, 1)
                link(v.tensor_scalar(gates[:, :, :], gates[:, :, :], 1.0, None, ALU.add))
                link(v.reciprocal(gates[:, :, :], gates[:, :, :]))

            def add_norm(k):
                for i in batches[k]:
                    ins = v.tensor_tensor(H[:, i, :], H[:, i, :], SA[:, i, :], ALU.add)
                ins.then_inc(sa_used, 1)
                dve.wait_ge(sa_used, k + 1)
                layernorm(H, H, batches[k], "g1", "be1")

            for op, n, *at in attention_plan():
                if op == "project":
                    project(1, *at)
                elif op == "max":
                    j, st = at
                    key = ("max", n, j, st)
                    bank = uses[key][0]
                    arrived(dve, key)
                    ins = v.tensor_reduce(negm[:, n % 2, TPB * j + st:TPB * j + st + 1],
                                          PS[:, bank:bank + 2, :].rearrange("p b s -> p (b s)")[:, 0:P * (st + 1)],
                                          AX.X, ALU.max, negate=True)
                    released(ins, key)
                elif op == "neg":
                    key = ("neg", n)
                    arrived(dve, key)
                    src = PS[0:GRP * TPB, uses[key][0], 0:P]
                    if n >= 2:
                        dve.wait_ge(mrows_in[(n - 2) % SLOTS], 3 * 16 * ((n - 2) // SLOTS + 1))
                    link(v.tensor_copy(mparts[:, n % 2, 0, :], src))
                    ins = v.tensor_tensor(mrest, src, mparts[:, n % 2, 0, :], ALU.subtract)
                    released(ins, key)
                    drained(dve, key)
                    link(v.tensor_copy(mparts[:, n % 2, 1, :], mrest))
                    v.tensor_tensor(mparts[:, n % 2, 2, :], mrest, mparts[:, n % 2, 1, :],
                                    ALU.subtract).then_inc(mparts_ready, 1)
                    if n == 0:
                        arrived(dve, "simsum")
                        ins = v.tensor_copy(siminv[:, :, :], PS[:, 7, 0:2 * EXPERTS].rearrange("p (n e) -> p n e", n=2))
                        released(ins, "simsum")
                    elif n == 1:
                        unit_columns()
                elif op == "norm":
                    if n == 0:
                        drained(dve, ("out", GROUPS // 2 - 1))
                    add_norm(n)
                elif op == "out":
                    if n == GROUPS - 1:
                        context(0)
                    key = ("out", n)
                    arrived(dve, key)
                    if n == 0:
                        for k in range(8):
                            dve.wait_ge(parts_out[k], 16)
                    else:
                        drained(dve, ("out", n - 1))
                    src = PS[:, uses[key][0]:uses[key][0] + 2, :].rearrange("p b (m e) -> p (b m) e", e=32)
                    link(v.reciprocal(rsum, src[:, :, HD:HD + 1].rearrange("p m o -> p (m o)")))
                    c0 = GRP * HD * (n % 4)
                    ins = v.tensor_tensor(SA[:, TPB * (n // 4):TPB * (n // 4) + TPB, c0:c0 + GRP * HD].rearrange("p i (j e) -> p i j e", j=GRP),
                                          src[:, :, 0:HD].rearrange("p (i j) e -> p i j e", i=TPB),
                                          rsum.rearrange("p (i j) -> p i j", i=TPB).unsqueeze(3).broadcast_to([P, TPB, GRP, HD]),
                                          ALU.mult)
                    released(ins, key)
            def low_rank(u):
                for n, (key, dst) in enumerate((("l1", LD1), ("l2", LD2))):
                    if u == (13, 17)[n]:
                        arrived(dve, key)
                        released(v.tensor_copy(dst, PS[0:(4, 50)[n], uses[key][0], 0:D]), key)
                if u == 21:
                    arrived(dve, "l3")
                    loaded(dve, "wt")
                    released(v.tensor_tensor(WEFF, WEFF, PS[:, uses["l3"][0], :].rearrange("p (k f) -> p k f", k=KC), ALU.add), "l3")

            def gate_input(n, u, first, every):
                c = chunk_at(u, first + 4, every)
                if c is not None:
                    for m in range(4):
                        i = 4 * c + m
                        drained(dve, (("t_n1", "t_n2")[n], i))
                        v.tensor_tensor(TRP[n][1][:, :, P * i:P * i + P], TRF[:, m],
                                        TRP[n][0][:, :, P * i:P * i + P].bitcast(F32), ALU.subtract).then_inc(lower_ready, 1)
                c = chunk_at(u, first + 5, every)
                if c is not None:
                    gate(n, c)
                c = chunk_at(u, first + 6, every)
                if c is not None:
                    gate_softmax(n, c)

            def norm_input(u):
                c = chunk_at(u, 11, 8)
                if c is not None:
                    norms[0] += 1
                    dve.wait_ge(rstd_ready, norms[0])
                    for i in batches[c]:
                        v.tensor_scalar(H[:, i, :], X[:, i, :], mv[:, i, 0:1], rstd[:, i:i + 1],
                                        ALU.subtract, ALU.mult).then_inc(ln_ready, 1)
                    dve.wait_ge(ln_ready, ln_count("ffn", 4 * c + 3))
                c = chunk_at(u, 12, 8)
                if c is not None:
                    statistics(H, batches[c])
                c = chunk_at(u, 13, 8)
                if c is not None:
                    if c >= 2:
                        dve.wait_ge(ss_ready, 4 * (c - 1))
                    center(H, NBX, batches[c], "n1w")
                c = chunk_at(u, 14, 8)
                if c is not None:
                    divide_by_spread(NBX, batches[c], "n1b")

            def gate(n, c):
                dve.wait_ge(ssr_ready, 4 * n + c + 1)
                length = ssr[:, 4 * c:4 * c + 4]
                link(v.tensor_scalar(length, length, 1e-12, None, ALU.max))
                link(v.reciprocal(length, length))
                l = [LG[:, k, :].rearrange("p (i e) -> p i e", i=4) for k in range(8)]
                s = [gsm[:, k, 0:4] for k in range(4)]
                per = [P, 4, EXPERTS]
                full = [P, 4, EXPERTS, EXPERTS]
                key = ("lg", n, c)
                arrived(dve, key)
                link(v.tensor_tensor(l[0], PS[:, uses[key][0], 0:4 * EXPERTS].rearrange("p (i e) -> p i e", i=4),
                                     length.unsqueeze(2).broadcast_to(per), ALU.mult))
                ins = v.tensor_tensor(l[0], l[0], gates[:, n, :].unsqueeze(1).broadcast_to(per), ALU.subtract)
                released(ins, key)
                drained(dve, key)
                other = l[0].unsqueeze(2).broadcast_to(full)
                own = l[0].unsqueeze(3).broadcast_to(full)
                v.tensor_tensor(RANK[:, 0], other, own, ALU.is_gt)
                v.tensor_scalar(l[1], l[0], 0.0, None, ALU.max)
                link(v.tensor_tensor(RANK[:, 1], other, own, ALU.is_equal))
                v.tensor_reduce(s[0], l[1], AX.X, ALU.max)
                link(v.tensor_tensor(RANK[:, 1], RANK[:, 1], lower[:, :, :].unsqueeze(1).broadcast_to(full), ALU.mult))
                v.tensor_tensor(l[4], l[1], s[0].unsqueeze(2).broadcast_to(per), ALU.subtract).then_inc(gate_in, 1)
                link(v.tensor_tensor(RANK[:, 0], RANK[:, 0], RANK[:, 1], ALU.add))
                v.tensor_reduce(l[3], RANK[:, 0], AX.X, ALU.add)
                v.tensor_scalar(l[2], l[0], 0.0, None, ALU.is_gt)
                link(v.tensor_scalar(s[1], s[0], 0.0, None, ALU.is_equal))
                link(v.scalar_tensor_tensor(out=l[6], in0=l[3], scalar=2.0, in1=s[1].unsqueeze(2).broadcast_to(per),
                                            op0=ALU.is_lt, op1=ALU.mult))
                link(v.tensor_tensor(l[2], l[2], l[6], ALU.max))

            def gate_softmax(n, c):
                l = [LG[:, k, :].rearrange("p (i e) -> p i e", i=4) for k in range(8)]
                s = [gsm[:, k, 0:4] for k in range(4)]
                per = [P, 4, EXPERTS]
                dve.wait_ge(gate_exp, 4 * n + c + 1)
                link(v.tensor_tensor(l[7], l[5], l[2], ALU.mult))
                link(v.tensor_reduce(s[2], l[7], AX.X, ALU.add))
                link(v.reciprocal(s[3], s[2]))
                link(v.tensor_tensor(rw[:, n, 4 * c:4 * c + 4, :], l[7], s[3].unsqueeze(2).broadcast_to(per), ALU.mult))

            def cross(layer):
                x = X if layer else H

                def shift(u):
                    i, g = u // 2, u % 2
                    key = ("sx", layer, u)
                    full = [P, 2, 4, T]
                    ex = EX[u % 4].rearrange("p (m h) t -> p m h t", m=2)
                    src = PS[:, 2 * g:2 * g + 2, 0:4 * T].rearrange("p m (h t) -> p m h t", h=4)
                    most = mx[:, 0, HH * g:HH * g + HH].rearrange("p (m h) -> p m h", m=2)
                    if u >= 4:
                        arrived(dve, ("px", layer, u - 4, 1))
                    if layer:
                        dve.wait_ge(fill_ready, u + 1)
                        arrived(dve, key)
                        ins = v.copy_predicated(ex, KEEP[:, i, :].unsqueeze(1).unsqueeze(1).broadcast_to(full), src)
                        released(ins, key)
                        drained(dve, key)
                        if u >= 2:
                            dve.wait_ge(shift_ready, u - 1)
                        v.tensor_reduce(most, ex, AX.X, ALU.max).then_inc(most_ready, 1)
                        return
                    arrived(dve, key)
                    link(v.tensor_reduce(most, src, AX.X, ALU.max))
                    released(v.tensor_tensor(ex, src, most.unsqueeze(3).broadcast_to(full), ALU.subtract), key)

                def divide(t):
                    key = ("ox", layer, t)
                    arrived(dve, key)
                    src = PS[:, 6 + t % 2, 0:HEADS * VW].rearrange("p (h e) -> p h e", h=HEADS)
                    link(v.reciprocal(mx[:, 1, :], src[:, :, HD:HD + 1].rearrange("p h o -> p (h o)")))
                    ins = v.tensor_tensor(tmp[:, t % 2, :].rearrange("p (h e) -> p h e", h=HEADS), src[:, :, 0:HD],
                                          mx[:, 1, :].unsqueeze(2).broadcast_to([P, HEADS, HD]), ALU.mult)
                    released(ins, key)
                    drained(dve, key)
                    link(v.tensor_tensor(x[:, t, :], x[:, t, :], tmp[:, t % 2, :], ALU.add))
                    if t % 4 == 3:
                        statistics(x, batches[t // 4])

                for u in range(UNITS + 5 if layer == 0 else UNITS + 3):
                    if u < UNITS:
                        shift(u)
                    if u == 1:
                        context_values(layer)
                    if layer == 0 and u in (3, 7):
                        if u == 3:
                            drained(dve, ("out", GROUPS - 1))
                        add_norm(u // 4 + 2)
                    if u >= 4 and u % 2 == 0 and u < UNITS + 3:
                        divide((u - 4) // 2)
                    if layer == 0:
                        low_rank(u)
                        c = chunk_at(u, 11, 8)
                        if c is not None:
                            center(H, H, batches[c], "g2")
                        c = chunk_at(u, 12, 8)
                        if c is not None:
                            divide_by_spread(H, batches[c], "be2")
                    else:
                        norm_input(u)
                        gate_input(0, u, 15, 8)

            cross(0)

            loaded(dve, "wf2")
            for n in range(4):
                v.tensor_copy(WF2P[0][:, 2 * n:2 * n + 2, :], WF2[:, 2 * n:2 * n + 2, :]).then_inc(wf2_upper, 1)
            for n in range(4):
                dve.wait_ge(wf2_upper, n + 1)
                v.tensor_tensor(WF2P[1][:, 2 * n:2 * n + 2, :], WF2[:, 2 * n:2 * n + 2, :],
                                WF2P[0][:, 2 * n:2 * n + 2, :].bitcast(F32), ALU.subtract).then_inc(wf2_split, 1)
            for s in range(5):
                if s > 0:
                    for i in batches[s - 1]:
                        arrived(dve, ("lin", i))
                        released(v.tensor_tensor(tmp[:, i % 2, :], PS[:, 2 + i % 4, 0:D], bc("lb"), ALU.add), ("lin", i))
                        drained(dve, ("lin", i))
                        link(v.tensor_tensor(X[:, i, :], X[:, i, :], tmp[:, i % 2, :], ALU.add))
                    layernorm(X, H, batches[s - 1])
                if s < 4:
                    for i in batches[s]:
                        arrived(dve, ("f2", i))
                        released(v.tensor_tensor(tmp[:, i % 2, :], PS[:, 6 + i % 2, 0:D], bc("bf2"), ALU.add), ("f2", i))
                        drained(dve, ("f2", i))
                        link(v.tensor_tensor(H[:, i, :], H[:, i, :], tmp[:, i % 2, :], ALU.add))
                    layernorm(H, H, batches[s], "g3", "be3")
                    dve.wait_ge(ln_ready, ln_count("g3", 4 * s + 3))
                    for i in batches[s]:
                        ins = v.tensor_tensor(X[:, i, :], X[:, i, :], H[:, i, :], ALU.add)
                    link(ins)
                    layernorm(X, H, batches[s])
            context(1)
            cross(1)

            for i in range(TILES):
                gate_input(0, UNITS + 3 + i, 15, 8)
                norm_input(UNITS + 3 + i)
                for e in range(EXPERTS):
                    key = ("qkv", i, e)
                    arrived(dve, key)
                    src, w = PS[:, uses[key][0], 0:3 * HA], rw[:, 0, i, e:e + 1]
                    if e == 0:
                        ins = v.tensor_scalar(QKV[:, i, :], src, w, None, ALU.mult)
                    else:
                        ins = v.scalar_tensor_tensor(out=QKV[:, i, :], in0=src, scalar=w, in1=QKV[:, i, :], op0=ALU.mult, op1=ALU.add)
                    released(ins, key)
                    drained(dve, key)
            def row_max(i):
                arrived(dve, ("s1", i))
                s = l1s[:, i % 2, :]
                link(v.tensor_reduce(s[:, 3:4], PS[:, 0:2, :].rearrange("p b s -> p (b s)")[:, 0:P * (i % TPB + 1)],
                                     AX.X, ALU.max, negate=True))
                v.tensor_scalar(s[:, 0:1], s[:, 3:4], HA ** -0.5, None, ALU.mult).then_inc(bias_ready, 1)

            def second_norm(i):
                c = chunk_at(i, 5, 4)
                if c is not None:
                    drained(dve, ("o1", 4 * c + 3))
                    statistics(H, batches[c])
                c = chunk_at(i, 6, 4)
                if c is not None:
                    dve.wait_ge(ss_ready, TILES + 4 * (c - 1))
                    center(H, NBX, batches[c], "n2w")
                c = chunk_at(i, 7, 4)
                if c is not None:
                    divide_by_spread(NBX, batches[c], "n2b")
                c = chunk_at(i, 8, 4)
                if c is not None:
                    link(v.tensor_tensor(X[:, 4 * c:4 * c + 4, :], X[:, 4 * c:4 * c + 4, :], H[:, 4 * c:4 * c + 4, :], ALU.add))

            row_max(0)
            for i in range(TILES + 2):
                if 0 < i <= TILES:
                    t = i - 1
                    s = l1s[:, t % 2, :]
                    arrived(dve, ("a1", t))
                    if t >= 1:
                        arrived(dve, ("at", t - 1))
                    drained(dve, ("s1", t))
                    link(v.reciprocal(s[:, 2:3], s[:, 1:2]))
                    full = [P, EXPERTS, HA]
                    released(v.scalar_tensor_tensor(out=ATT, in0=PS[:, 4, 0:HA].unsqueeze(1).broadcast_to(full), scalar=s[:, 2:3],
                                                    in1=rw[:, 0, t, :].unsqueeze(2).broadcast_to(full), op0=ALU.mult, op1=ALU.mult), ("a1", t))
                if i + 1 < TILES:
                    row_max(i + 1)
                gate_input(1, i, 8, 4)
                if 1 < i <= TILES + 1:
                    t = i - 2
                    key = ("o1", t)
                    arrived(dve, key)
                    released(v.tensor_tensor(H[:, t, :], H[:, t, :], PS[:, 7, 0:D], ALU.add), key)
                second_norm(i)
            for n in range(4 * EXPERTS + 2):
                gate_input(1, TILES + 2 + n, 8, 4)
                second_norm(TILES + 2 + n)
                if n < 4 * EXPERTS:
                    for ic in range(2):
                        drained(dve, ("m1", n, ic))
                        v.tensor_tensor(INT[n % 4][:, 1, ic, :], INTF[(2 * n + ic) % 4], INT[n % 4][:, 0, ic, :].bitcast(F32),
                                        ALU.subtract).then_inc(int_ready, 1)
                if n >= 2:
                    c, e = (n - 2) // EXPERTS, (n - 2) % EXPERTS
                    for m in range(4):
                        key = ("m2", n - 2, m)
                        i = 4 * c + m
                        arrived(dve, key)
                        if n >= 3:
                            drained(dve, ("m2", n - 3, m))
                        ins = v.scalar_tensor_tensor(out=X[:, i, :], in0=PS[:, uses[key][0], 0:D], scalar=rw[:, 1, i, e:e + 1],
                                                     in1=X[:, i, :], op0=ALU.mult, op1=ALU.add)
                        released(ins, key)

        @block.gpsimd
        def _(pool):
            g = nc.gpsimd
            links = [0]

            def link(ins):
                links[0] += 1
                ins.then_inc(pool_chain, 1)
                pool.wait_ge(pool_chain, links[0])

            g.memset(ident[:, :], 0.0)
            g.memset(halves[:, :], -0.5)
            g.memset(halfp[:, :], 0.5)
            g.memset(maskq[:, :], 0.0)
            g.memset(blockm[:, :], 1.0)
            link(g.memset(lower[:, :, :], 1.0))
            ins = g.memset(ones, 1.0)
            link(g.affine_select(out=ident[:, :], in_=ident[:, :], compare_op=ALU.not_equal, fill=1.0, base=0,
                                 pattern=[[-1, P]], channel_multiplier=1))
            g.affine_select(out=maskq[:, :], in_=maskq[:, :], compare_op=ALU.is_ge, fill=BIG, base=0,
                            pattern=[[-1, P]], channel_multiplier=1)
            link(g.affine_select(out=blockm[:, :], in_=blockm[:, :], compare_op=ALU.is_ge, fill=0.0, base=0,
                                 pattern=[[-HD, 8]], channel_multiplier=1))
            g.affine_select(out=blockm[:, :], in_=blockm[:, :], compare_op=ALU.is_ge, fill=0.0, base=HD - 1,
                            pattern=[[HD, 8]], channel_multiplier=-1)
            g.affine_select(out=lower[:, :, :], in_=lower[:, :, :], compare_op=ALU.is_gt, fill=0.0, base=0,
                            pattern=[[1, EXPERTS], [-1, EXPERTS]], channel_multiplier=0)
            g.tensor_copy(identb[:, :], ident[:, :]).then_inc(consts, 1)
            def repeat_context(layer, b):
                ins = g.tensor_copy(CREP[layer][b], ctxT[:, :, T * b:T * b + T].unsqueeze(2).broadcast_to([P, KC, HH, T]))
                ins.then_inc(crep_ready, 1)

            def split(raw, upper, lower, done):
                link(g.tensor_copy(upper, raw))
                g.tensor_tensor(lower, raw, upper.bitcast(F32), ALU.subtract).then_inc(done, 1)

            def lengths(n, c):
                pool.wait_ge(ss_ready, TILES * n + 4 * c + 4)
                g.tensor_tensor(ssr[:, 4 * c:4 * c + 4], ss[:, 4 * c:4 * c + 4], halfp[:, 0:4], ALU.pow).then_inc(ssr_ready, 1)

            def fill(u):
                if u >= 4:
                    arrived(pool, ("px", 1, u - 4, 1))
                elif u == 0:
                    arrived(pool, ("ox", 0, TILES - 1))
                g.memset(EX[u % 4], MASKED / HD ** -0.5).then_inc(fill_ready, 1)

            def power(name, k):
                pool.wait_ge(var_ready, NORMS.index((name, k)) + 1)
                g.tensor_tensor(rstd[:, 4 * k:4 * k + 4], var[:, 4 * k:4 * k + 4], halves[:, 0:4], ALU.pow).then_inc(rstd_ready, 1)

            def lower_parts(c):
                for i in range(4 * c, 4 * c + 4):
                    drained(pool, ("t_g2", i))
                    if c >= 2:
                        arrived(pool, ("f1", c - 2, FCH - 1))
                    g.tensor_tensor(TRG[c % 2][:, :, P * (i % 4):P * (i % 4) + P], TRGF[:, i % 4],
                                    TRR[:, :, P * i:P * i + P].bitcast(F32), ALU.subtract).then_inc(trg_ready, 1)

            def lower_units(c, pieces):
                for f in pieces:
                    drained(pool, ("f1", c, f))
                    if c > 0 and f == 0:
                        arrived(pool, ("f2", 4 * c - 1))
                    g.tensor_tensor(HT[1][:, f, :], HTF[f % 4], HT[0][:, f, :].bitcast(F32), ALU.subtract).then_inc(ht_ready, 1)

            def self_attention():
                step = 0
                for op, n, *at in attention_plan():
                    if op == "score":
                        tt, c, j = at
                        if c == tt // 4:
                            prob = PROB[GRP * (step // GRP % 2) + j][:, 0:P]
                            drained(pool, ("score", n, tt, c, j))
                            g.affine_select(out=prob, in_=prob, compare_op=ALU.is_ge, fill=0.0, base=0,
                                            pattern=[[1, P]], channel_multiplier=-1).then_inc(cleared, 1)
                        step += 1
                    elif op == "norm":
                        power("g1", n)
                    elif op == "neg" and n == 0:
                        loaded(pool, "ctx")
                        arrived(pool, ("v1", TILES - 1))
                        pool.wait_ge(parts_ready, 16)
                        for b in range(B):
                            repeat_context(0, b)
                        drained(pool, "simsum")
                        g.tensor_tensor(siminv[:, :, :].rearrange("p n e -> p (n e)"), siminv[:, :, :].rearrange("p n e -> p (n e)"),
                                        halfp[:, :], ALU.pow).then_inc(sim_sum, 1)
                arrived(pool, ("score", GROUPS - 1, TPB - 1, 1, GRP - 1))
                arrived(pool, ("kx", 0, 0))
                link(g.memset(VBD, 0.0))
                flag = VBD.rearrange("p b g j h e -> p (b g) j h e")[:, :, :, :, HD]
                link(g.memset(flag, 1.0))
                link(g.affine_select(out=flag, in_=flag, compare_op=ALU.is_ge, fill=0.0, base=0,
                                     pattern=[[0, 2 * B], [P, len(PIECES)], [-T, HH]], channel_multiplier=1))
                g.affine_select(out=flag, in_=flag, compare_op=ALU.is_ge, fill=0.0, base=T - 1,
                                pattern=[[0, 2 * B], [-P, len(PIECES)], [T, HH]], channel_multiplier=-1).then_inc(vbd_clear, 1)

            for name, k in NORMS[:NORMS.index(("ffn", 0))]:
                if (name, k) in (("g1", 0), ("g1", 1)):
                    continue
                if name == "lin" and k < 3:
                    lower_units(k + 1, range(EARLY_PIECES))
                if (name, k) == ("g3", 0):
                    lower_units(0, range(FCH))
                    lower_parts(1)
                if name == "xat" and k < 3:
                    lower_units(k + 1, range(EARLY_PIECES, FCH))
                    if k < 2:
                        lower_parts(k + 2)
                power(name, k)
                if (name, k) == ("in", 3):
                    link(g.memset(VEXT[:, :, :, HD:HD + 1], 1.0))
                    for s in range(SLOTS):
                        link(g.memset(PACKK[s][ROWS:ROWS + 3, :, :], 1.0))
                    g.memset(mparts[:, :, :, :], 0.0).then_inc(consts, 1)
                    self_attention()
                if (name, k) == ("g2", 1):
                    loaded(pool, "wf1")
                    for n in range(4):
                        cols = slice(n * FF // 4, (n + 1) * FF // 4)
                        split(WF1[:, :, cols], WF1P[0][:, :, cols], WF1P[1][:, :, cols], wf1_split)
                if (name, k) == ("g2", 3):
                    lower_parts(0)
                if (name, k) == ("lin", 3):
                    arrived(pool, ("f2", 15))
                    for b in range(B):
                        repeat_context(1, b)

            for u in range(3):
                fill(u)
            for u in range(42):
                if u < UNITS:
                    h0 = HH * (u % 2)
                    pool.wait_ge(most_ready, u + 1)
                    g.tensor_tensor(EX[u % 4], EX[u % 4], mx[:, 0, h0:h0 + HH].unsqueeze(2).broadcast_to([P, HH, T]),
                                    ALU.subtract).then_inc(shift_ready, 1)
                for name, first in (("ffn", 10), ("n1", 12)):
                    c = chunk_at(u, first, 8)
                    if c is not None:
                        power(name, c)
                if u + 3 < UNITS:
                    fill(u + 3)
                c = chunk_at(u, 17, 8)
                if c is not None:
                    lengths(0, c)
                if 4 <= u < 4 + 3 * EXPERTS and (u - 4) % 3 == 0:
                    e = (u - 4) // 3
                    pool.wait_ge(wqkv_upper, e + 1)
                    g.tensor_tensor(WQKVP[1][:, :, e, :], WQKV[:, :, e, :], WQKVP[0][:, :, e, :].bitcast(F32),
                                    ALU.subtract).then_inc(wqkv_split, 1)

            def split_w2(e):
                split(W2[:, e], W2P[0][:, e], W2P[1][:, e], w2_split)

            loaded(pool, "w1")
            for k in range(4):
                for e in (2 * k, 2 * k + 1):
                    split(W1[:, :, e, :], W1P[0][:, :, e, :], W1P[1][:, :, e, :], w1_split)
                if k == 3:
                    loaded(pool, "w2")
                    arrived(pool, ("s1", TILES - 1))
                    split_w2(0)
                    split_w2(1)
                power("n2", k)
                if k == 3:
                    split_w2(2)
                    split_w2(3)
                lengths(1, k)
            for e in range(4, EXPERTS):
                split_w2(e)


def _layout(inputs):
    import numpy as np

    f = {k: np.asarray(v) for k, v in inputs.items()}
    r = {"x": f["x"].reshape(N, D), "ctxT": f["ctx_1024"].reshape(B * T, D).T}
    for n in (1, 2):
        for w in "qkv":
            r[f"w{w}{n}"] = f[f"L0_xattn_W{w}{n}"].transpose(1, 0, 2).reshape(D, D)
    for w in "qkv":
        r[f"w{w}3"] = f[f"L1_xattn_W{w}"].T
    r |= {"bq3": f["L1_xattn_bq"], "bk3": f["L1_xattn_bk"], "bf1": f["L0_xattn_bf1"], "wf1": f["L0_xattn_Wf1"],
          "wf2": f["L0_xattn_Wf2"], "wt": f["L0_ffn_W"].T, "daux": f["L0_ffn_down_aux"], "upT": f["L0_ffn_up_aux"].T,
          "ldT": f["L0_ffn_lora_down"].T, "luT": f["L0_ffn_lora_up"].T}
    r["wqkv"] = np.concatenate([f[f"L1_ffn_{w}_proj"].transpose(1, 0, 2) for w in "qkv"], axis=2)
    r |= {"wo": f["L1_ffn_o_proj"], "w1": f["L1_ffn_w1"].transpose(1, 0, 2), "w2": f["L1_ffn_w2"].reshape(EXPERTS * D, D), "sim1": f["L1_ffn_smha_sim"],
          "sim2": f["L1_ffn_moe_sim"], "gates1": f["L1_ffn_smha_gates"], "gates2": f["L1_ffn_moe_gates"],
          "mask_st": f["mask_1x1xSxS2_ik0"].reshape(S, T), "mask_bt": f["mask_Bx1x1xS2_ik0"].reshape(B, T)}
    for name in ("bq3", "bk3", "bf1"):
        r[name] = r[name].reshape(-1, P).T
    rows = {"bv1": f["L0_xattn_bv1"], "bv2": f["L0_xattn_bv2"], "g1": f["L0_xattn_g1"], "be1": f["L0_xattn_be1"],
            "g2": f["L0_xattn_g2"], "be2": f["L0_xattn_be2"], "g3": f["L0_xattn_g3"], "be3": f["L0_xattn_be3"],
            "bf2": f["L0_xattn_bf2"], "lb": f["L0_ffn_b"], "bv3": f["L1_xattn_bv"], "n1w": f["L1_ffn_ln1_w"],
            "n1b": f["L1_ffn_ln1_b"], "n2w": f["L1_ffn_ln2_w"], "n2b": f["L1_ffn_ln2_b"]}
    r["bcast"] = np.stack([rows[name].reshape(D) for name in BCAST])
    return {k: np.ascontiguousarray(v) for k, v in r.items()}


def kernel(**inputs):
    import concourse.bacc as bacc
    from concourse.bass_utils import run_bass_kernel_spmd

    arrays = _layout(inputs)
    nc = bacc.Bacc("TRN2", target_bir_lowering=False, num_devices=1)
    args = {k: nc.dram_tensor(f"in_{k}", v.shape, mybir.dt.from_np(v.dtype), kind="ExternalInput").ap()
            for k, v in arrays.items()}
    out = nc.dram_tensor("out_x", (N, D), F32, kind="ExternalOutput").ap()
    build(nc, args, out)
    r = run_bass_kernel_spmd(nc, [{f"in_{k}": v for k, v in arrays.items()}], core_ids=[0])
    return r.results[0]["out_x"].reshape(B, S, D)
```
